# Optimizing a Trainium2 kernel written in Bass

```python
import numpy as np
import jax
import jax.numpy as jnp

def _softmax(x, axis=-1):
    return jax.nn.softmax(x, axis=axis)

def _gelu(x):
    return jax.nn.gelu(x, approximate=True)

def _silu(x):
    return jax.nn.silu(x)

def _sigmoid(x):
    return jax.nn.sigmoid(x)

def _layernorm(x, axis=-1, eps=1e-05):
    m = jnp.mean(x, axis=axis, keepdims=True)
    v = jnp.var(x, axis=axis, keepdims=True)
    return (x - m) / jnp.sqrt(v + eps)

def _scatter_add(tgt, idx, src, axis=0):
    return tgt.at[idx].add(src)

def _segment_sum(src, seg, n):
    return jax.ops.segment_sum(src, seg, n)
kernel_name = 'mk_seq_postln_d2_jaxref_r8_a78cc7'

def setup_inputs(seed: int=0):
    np.random.seed(seed)
    _w = jnp.asarray

    def _L0_attn_setup():
        import jax, jax.numpy as jnp
        import numpy as np
        B, N, D, H = (2, 128, 128, 16)
        DH = D // H
        SCALE = 1.0 / DH ** 0.5
        STJ_Q = 1.0
        NUM_ITER = 4
        CAUSAL = True
        EPS = 1e-06

        def stieltjes_attention(Q, K, V, scale, causal, q, num_iter):
            n = Q.shape[2]
            s = jnp.einsum('bhnd,bhmd->bhnm', Q, K) * scale
            if causal:
                mask = jnp.tril(jnp.ones((n, n), bool))
            else:
                mask = jnp.ones((n, n), bool)
            s_masked = jnp.where(mask, s, -1e+30)
            lam = s_masked.max(-1) + 1.0
            for _ in range(num_iter):
                d = jnp.maximum(lam[..., None] - s, EPS)
                w = jnp.where(mask, d ** (-q), 0.0)
                f = w.sum(-1) - 1.0
                fp = -q * jnp.where(mask, d ** (-q - 1.0), 0.0).sum(-1)
                lam = lam - f / fp
            d = jnp.maximum(lam[..., None] - s, EPS)
            p = jnp.where(mask, d ** (-q), 0.0)
            p = p / p.sum(-1, keepdims=True)
            return jnp.einsum('bhnm,bhmd->bhnd', p, V)
        key = jax.random.key(seed)
        k1, k2, k3 = jax.random.split(key, 3)
        x = jax.random.normal(k1, (B, N, D), jnp.float32)
        Wqkv = jax.random.normal(k2, (3 * D, D), jnp.float32) / np.float32(np.sqrt(D))
        Wo = jax.random.normal(k3, (D, D), jnp.float32) / np.float32(np.sqrt(D))
        return {'x': x, 'Wqkv': Wqkv, 'Wo': Wo}
    _L0_attn_in = _L0_attn_setup()

    def _L0_ffn_setup():
        import jax, jax.numpy as jnp
        import numpy as np
        N_EXPERTS = 8
        CAP_FACTOR = 1.25
        BATCH, SEQ, DMODEL, DFF = (4, 256, 128, 512)
        key = jax.random.key(seed)
        k0, k1, k2, k3 = jax.random.split(key, 4)
        x = jax.random.normal(k0, (BATCH, SEQ, DMODEL), dtype=jnp.float32)
        Wr = jax.random.normal(k1, (DMODEL, N_EXPERTS), dtype=jnp.float32) * 0.02
        W1 = jax.random.normal(k2, (N_EXPERTS, DMODEL, DFF), dtype=jnp.float32) * 0.02
        W2 = jax.random.normal(k3, (N_EXPERTS, DFF, DMODEL), dtype=jnp.float32) * 0.02
        return {'x': x, 'Wr': Wr, 'W1': W1, 'W2': W2}
    _L0_ffn_in = _L0_ffn_setup()

    def _L1_attn_setup():
        import jax, jax.numpy as jnp
        import numpy as np
        B, T, D = (1, 512, 128)
        HQ, HKV, HD = (16, 4, 64)
        G = HQ // HKV
        NEG = jnp.float32(-1e+30)
        key = jax.random.key(seed)
        ks = jax.random.split(key, 5)
        s = D ** (-0.5)
        return {'x': jax.random.normal(ks[0], (B, T, D), jnp.float32), 'Wq': jax.random.normal(ks[1], (D, HQ * HD), jnp.float32) * s, 'Wk': jax.random.normal(ks[2], (D, HKV * HD), jnp.float32) * s, 'Wv': jax.random.normal(ks[3], (D, HKV * HD), jnp.float32) * s, 'Wo': jax.random.normal(ks[4], (HQ * HD, D), jnp.float32) * s}
    _L1_attn_in = _L1_attn_setup()

    def _L1_ffn_setup():
        import jax, jax.numpy as jnp
        import numpy as np
        EMB = 128
        HEADS = 16
        SEQ = 256
        LATENT = 64
        N_EXP = 8
        TOP_K = 2
        EXP_DIM = 256
        BATCH = 2
        EPS = 1e-06

        def _rmsnorm(x, g):
            return x * jax.lax.rsqrt(jnp.mean(x * x, axis=-1, keepdims=True) + EPS) * g

        def _mla(h, Wq, Wdkv, Wuk, Wuv, Wo):
            B, S, D = h.shape
            hd = D // HEADS
            q = (h @ Wq).reshape(B, S, HEADS, hd)
            c = h @ Wdkv
            k = (c @ Wuk).reshape(B, S, HEADS, hd)
            v = (c @ Wuv).reshape(B, S, HEADS, hd)
            scores = jnp.einsum('bqhd,bkhd->bhqk', q, k) / jnp.sqrt(jnp.asarray(hd, h.dtype))
            causal = jnp.tril(jnp.ones((S, S), bool))
            scores = jnp.where(causal, scores, jnp.asarray(-1000000000.0, h.dtype))
            a = jax.nn.softmax(scores, axis=-1)
            out = jnp.einsum('bhqk,bkhd->bqhd', a, v).reshape(B, S, D)
            return out @ Wo

        def _moe(h, gate_w, w1, w2):
            B, S, D = h.shape
            t = h.reshape(B * S, D)
            logits = t @ gate_w
            top_v, top_i = jax.lax.top_k(logits, TOP_K)
            gates = jax.nn.softmax(top_v, axis=-1)
            T = t.shape[0]
            combine = jnp.zeros((T, N_EXP), t.dtype).at[jnp.arange(T)[:, None], top_i].add(gates)
            hid = jax.nn.silu(jnp.einsum('td,edh->teh', t, w1))
            ye = jnp.einsum('teh,ehd->ted', hid, w2)
            out = jnp.einsum('te,ted->td', combine, ye)
            return out.reshape(B, S, D)
        key = jax.random.key(seed)
        ks = jax.random.split(key, 12)
        s = 0.02
        return {'x': jax.random.normal(ks[0], (BATCH, SEQ, EMB), jnp.float32), 'g1': jnp.ones((EMB,), jnp.float32), 'Wq': jax.random.normal(ks[1], (EMB, EMB), jnp.float32) * s, 'Wdkv': jax.random.normal(ks[2], (EMB, LATENT), jnp.float32) * s, 'Wuk': jax.random.normal(ks[3], (LATENT, EMB), jnp.float32) * s, 'Wuv': jax.random.normal(ks[4], (LATENT, EMB), jnp.float32) * s, 'Wo': jax.random.normal(ks[5], (EMB, EMB), jnp.float32) * s, 'g2': jnp.ones((EMB,), jnp.float32), 'gate_w': jax.random.normal(ks[6], (EMB, N_EXP), jnp.float32) * s, 'w1': jax.random.normal(ks[7], (N_EXP, EMB, EXP_DIM), jnp.float32) * s, 'w2': jax.random.normal(ks[8], (N_EXP, EXP_DIM, EMB), jnp.float32) * s}
    _L1_ffn_in = _L1_ffn_setup()
    _d = {'L0_attn_x': _L0_attn_in['x'], 'L0_attn_Wqkv': _L0_attn_in['Wqkv'], 'L0_attn_Wo': _L0_attn_in['Wo'], 'L0_ffn_Wr': _L0_ffn_in['Wr'], 'L0_ffn_W1': _L0_ffn_in['W1'], 'L0_ffn_W2': _L0_ffn_in['W2'], 'L1_attn_Wq': _L1_attn_in['Wq'], 'L1_attn_Wk': _L1_attn_in['Wk'], 'L1_attn_Wv': _L1_attn_in['Wv'], 'L1_attn_Wo': _L1_attn_in['Wo'], 'L1_ffn_g1': _L1_ffn_in['g1'], 'L1_ffn_Wq': _L1_ffn_in['Wq'], 'L1_ffn_Wdkv': _L1_ffn_in['Wdkv'], 'L1_ffn_Wuk': _L1_ffn_in['Wuk'], 'L1_ffn_Wuv': _L1_ffn_in['Wuv'], 'L1_ffn_Wo': _L1_ffn_in['Wo'], 'L1_ffn_g2': _L1_ffn_in['g2'], 'L1_ffn_gate_w': _L1_ffn_in['gate_w'], 'L1_ffn_w1': _L1_ffn_in['w1'], 'L1_ffn_w2': _L1_ffn_in['w2']}
    _x0 = _d['L0_attn_x']
    _d['L0_attn_x'] = jax.random.normal(jax.random.fold_in(jax.random.key(seed), 1), (32, 256, 128), dtype=_x0.dtype)
    del _x0
    return _d

def reference(L0_attn_x, L0_attn_Wqkv, L0_attn_Wo, L0_ffn_Wr, L0_ffn_W1, L0_ffn_W2, L1_attn_Wq, L1_attn_Wk, L1_attn_Wv, L1_attn_Wo, L1_ffn_g1, L1_ffn_Wq, L1_ffn_Wdkv, L1_ffn_Wuk, L1_ffn_Wuv, L1_ffn_Wo, L1_ffn_g2, L1_ffn_gate_w, L1_ffn_w1, L1_ffn_w2):

    def _L0_attn_ref(x, Wqkv, Wo):
        import jax, jax.numpy as jnp
        import numpy as np
        B, N, D, H = (2, 128, 128, 16)
        DH = D // H
        SCALE = 1.0 / DH ** 0.5
        STJ_Q = 1.0
        NUM_ITER = 4
        CAUSAL = True
        EPS = 1e-06

        def stieltjes_attention(Q, K, V, scale, causal, q, num_iter):
            n = Q.shape[2]
            s = jnp.einsum('bhnd,bhmd->bhnm', Q, K) * scale
            if causal:
                mask = jnp.tril(jnp.ones((n, n), bool))
            else:
                mask = jnp.ones((n, n), bool)
            s_masked = jnp.where(mask, s, -1e+30)
            lam = s_masked.max(-1) + 1.0
            for _ in range(num_iter):
                d = jnp.maximum(lam[..., None] - s, EPS)
                w = jnp.where(mask, d ** (-q), 0.0)
                f = w.sum(-1) - 1.0
                fp = -q * jnp.where(mask, d ** (-q - 1.0), 0.0).sum(-1)
                lam = lam - f / fp
            d = jnp.maximum(lam[..., None] - s, EPS)
            p = jnp.where(mask, d ** (-q), 0.0)
            p = p / p.sum(-1, keepdims=True)
            return jnp.einsum('bhnm,bhmd->bhnd', p, V)
        b, n, dmodel = x.shape
        qkv = (x @ Wqkv.T).reshape(b, n, 3, H, DH).transpose(2, 0, 3, 1, 4)
        Q, K, V = (qkv[0], qkv[1], qkv[2])
        o = stieltjes_attention(Q, K, V, SCALE, CAUSAL, STJ_Q, NUM_ITER)
        o = o.transpose(0, 2, 1, 3).reshape(b, n, dmodel)
        return o @ Wo.T

    def _L0_ffn_ref(x, Wr, W1, W2):
        import jax, jax.numpy as jnp
        import numpy as np
        N_EXPERTS = 8
        CAP_FACTOR = 1.25
        BATCH, SEQ, DMODEL, DFF = (4, 256, 128, 512)
        B, S, D = x.shape
        E = W1.shape[0]
        cap = int(CAP_FACTOR * B * S / E)
        t = x.reshape(-1, D)
        probs = jax.nn.softmax(t @ Wr, axis=-1)
        idx = jnp.argmax(probs, axis=-1)
        pmax = jnp.max(probs, axis=-1)
        onehot = jax.nn.one_hot(idx, E, dtype=jnp.int32)
        pos = jnp.sum(jnp.cumsum(onehot, axis=0) * onehot, axis=-1) - 1
        kept = pos < cap
        flat = idx * cap + jnp.minimum(pos, cap - 1)
        disp = jnp.zeros((E * cap, D), t.dtype).at[flat].add(t * kept[:, None].astype(t.dtype))
        ein = disp.reshape(E, cap, D)
        h = jax.nn.relu(jnp.einsum('ecd,edf->ecf', ein, W1))
        eout = jnp.einsum('ecf,efd->ecd', h, W2).reshape(E * cap, D)
        comb = jnp.where(kept[:, None], eout[flat], t)
        factor = jnp.where(kept, pmax, jnp.ones_like(pmax))
        out = (comb * factor[:, None]).reshape(B, S, D)
        return out

    def _L1_attn_ref(x, Wq, Wk, Wv, Wo):
        import jax, jax.numpy as jnp
        import numpy as np
        B, T, D = (1, 512, 128)
        HQ, HKV, HD = (16, 4, 64)
        G = HQ // HKV
        NEG = jnp.float32(-1e+30)
        b, t, _ = x.shape
        q = (x @ Wq).reshape(b, t, HKV, G, HD)
        k = (x @ Wk).reshape(b, t, HKV, HD)
        v = (x @ Wv).reshape(b, t, HKV, HD)
        scores = jnp.einsum('bqhgd,bkhd->bhgqk', q, k) / jnp.sqrt(jnp.float32(HD))
        causal = jnp.tril(jnp.ones((t, t), bool))
        scores = jnp.where(causal, scores, NEG)
        attn = jax.nn.softmax(scores, axis=-1)
        ctx = jnp.einsum('bhgqk,bkhd->bqhgd', attn, v).reshape(b, t, HQ * HD)
        return ctx @ Wo

    def _L1_ffn_ref(x, g1, Wq, Wdkv, Wuk, Wuv, Wo, g2, gate_w, w1, w2):
        import jax, jax.numpy as jnp
        import numpy as np
        EMB = 128
        HEADS = 16
        SEQ = 256
        LATENT = 64
        N_EXP = 8
        TOP_K = 2
        EXP_DIM = 256
        BATCH = 2
        EPS = 1e-06

        def _rmsnorm(x, g):
            return x * jax.lax.rsqrt(jnp.mean(x * x, axis=-1, keepdims=True) + EPS) * g

        def _mla(h, Wq, Wdkv, Wuk, Wuv, Wo):
            B, S, D = h.shape
            hd = D // HEADS
            q = (h @ Wq).reshape(B, S, HEADS, hd)
            c = h @ Wdkv
            k = (c @ Wuk).reshape(B, S, HEADS, hd)
            v = (c @ Wuv).reshape(B, S, HEADS, hd)
            scores = jnp.einsum('bqhd,bkhd->bhqk', q, k) / jnp.sqrt(jnp.asarray(hd, h.dtype))
            causal = jnp.tril(jnp.ones((S, S), bool))
            scores = jnp.where(causal, scores, jnp.asarray(-1000000000.0, h.dtype))
            a = jax.nn.softmax(scores, axis=-1)
            out = jnp.einsum('bhqk,bkhd->bqhd', a, v).reshape(B, S, D)
            return out @ Wo

        def _moe(h, gate_w, w1, w2):
            B, S, D = h.shape
            t = h.reshape(B * S, D)
            logits = t @ gate_w
            top_v, top_i = jax.lax.top_k(logits, TOP_K)
            gates = jax.nn.softmax(top_v, axis=-1)
            T = t.shape[0]
            combine = jnp.zeros((T, N_EXP), t.dtype).at[jnp.arange(T)[:, None], top_i].add(gates)
            hid = jax.nn.silu(jnp.einsum('td,edh->teh', t, w1))
            ye = jnp.einsum('teh,ehd->ted', hid, w2)
            out = jnp.einsum('te,ted->td', combine, ye)
            return out.reshape(B, S, D)
        x = x + _mla(_rmsnorm(x, g1), Wq, Wdkv, Wuk, Wuv, Wo)
        x = x + _moe(_rmsnorm(x, g2), gate_w, w1, w2)
        return x
    x = L0_attn_x
    x = _layernorm(x + _L0_attn_ref(x, L0_attn_Wqkv, L0_attn_Wo), axis=-1)
    x = _layernorm(x + _L0_ffn_ref(x, L0_ffn_Wr, L0_ffn_W1, L0_ffn_W2), axis=-1)
    x = _layernorm(x + _L1_attn_ref(x, L1_attn_Wq, L1_attn_Wk, L1_attn_Wv, L1_attn_Wo), axis=-1)
    x = _layernorm(x + _L1_ffn_ref(x, L1_ffn_g1, L1_ffn_Wq, L1_ffn_Wdkv, L1_ffn_Wuk, L1_ffn_Wuv, L1_ffn_Wo, L1_ffn_g2, L1_ffn_gate_w, L1_ffn_w1, L1_ffn_w2), axis=-1)
    return x

_drawn_inputs = setup_inputs


def setup_inputs(seed=0):
    import zlib

    import numpy as np

    out = dict(_drawn_inputs(seed))
    spreads = {'L1_ffn_g1': (1.0, 0.6), 'L1_ffn_g2': (1.0, 0.6)}
    factors = {'L0_ffn_Wr': 4.383,
     'L0_ffn_W1': 5.031,
     'L0_ffn_W2': 3.95,
     'L1_ffn_Wq': 8.0,
     'L1_ffn_Wdkv': 8.0,
     'L1_ffn_Wuk': 8.0,
     'L1_ffn_Wuv': 8.0,
     'L1_ffn_Wo': 8.0,
     'L1_ffn_gate_w': 4.933,
     'L1_ffn_w1': 4.307,
     'L1_ffn_w2': 4.296}
    for name, (base, spread) in spreads.items():
        noise = np.random.default_rng([zlib.crc32(name.encode()), seed]).standard_normal(out[name].shape)
        drawn = base * np.exp(spread * noise) if base else spread * noise
        out[name] = jnp.asarray(drawn.astype(out[name].dtype))
    for name, factor in factors.items():
        out[name] = (out[name] * factor).astype(out[name].dtype)
    return out
```

```python
from contextlib import ExitStack

import numpy as np
import concourse.bass as bass
from concourse import mybir

F32 = mybir.dt.float32
BF16 = mybir.dt.bfloat16
F16 = mybir.dt.float16
I32 = mybir.dt.int32
U32 = mybir.dt.uint32
ALU = mybir.AluOpType
ACT = mybir.ActivationFunctionType
AX = mybir.AxisListType

P = 128
B, N, D = 32, 256, 128
TILES = B * N // P
H = 16
DH = D // H
LN_EPS = 1e-5
RMS_EPS = 1e-6


def broadcast_last(ap, n):
    return ap.unsqueeze(2).to_broadcast([ap.shape[0], ap.shape[1], n])


def broadcast_middle(ap, n):
    return ap.unsqueeze(1).to_broadcast([ap.shape[0], n, ap.shape[1]])


def constants(nc, ctx, sem):
    c = {}

    def sb(name, shape, dt):
        c[name] = ctx.enter_context(nc.sbuf_tensor(name, shape, dt))
        return c[name]

    sb("ident", [P, P], F32)
    sb("ident_bf", [P, P], BF16)
    sb("ident_h", [P, P], F16)
    sb("far_mask", [P, P], BF16)
    sb("row_mask", [P, 4], F32)
    sb("prefix", [P, P], F32)
    sb("ones", [P, P], F32)
    sb("carrier", [P, 1], F32)
    sb("minus_ident_bf", [P, P], BF16)
    return c


def make_constants(pool, c, const_step):
    n = 0
    for t, v in ((c["ident"], 0.0), (c["ident_bf"], 0.0), (c["ident_h"], 0.0), (c["far_mask"], 0.0),
                 (c["row_mask"], 1.0), (c["prefix"], 1.0), (c["ones"], 1.0), (c["minus_ident_bf"], 0.0)):
        pool.memset(t[:, :], v).then_inc(const_step, 1)
        n += 1
    pool.wait_ge(const_step, n)
    for t in (c["ident"], c["ident_bf"], c["ident_h"]):
        pool.affine_select(out=t[:, :], in_=t[:, :], compare_op=ALU.not_equal, fill=1.0, base=0,
                           pattern=[[-1, P]], channel_multiplier=1).then_inc(const_step, 1)
    pool.affine_select(out=c["minus_ident_bf"][:, :], in_=c["minus_ident_bf"][:, :], compare_op=ALU.not_equal,
                       fill=-1.0, base=0, pattern=[[-1, P]], channel_multiplier=1).then_inc(const_step, 1)
    pool.affine_select(out=c["far_mask"][:, :], in_=c["far_mask"][:, :], compare_op=ALU.is_ge, fill=1e28,
                       base=0, pattern=[[-1, P]], channel_multiplier=1).then_inc(const_step, 1)
    pool.affine_select(out=c["prefix"][:, :], in_=c["prefix"][:, :], compare_op=ALU.is_ge, fill=0.0,
                       base=0, pattern=[[1, P]], channel_multiplier=-1).then_inc(const_step, 1)
    n += 6
    rows = c["row_mask"]
    for g in range(4):
        part = rows[32 * g:32 * g + 32, :]
        pool.affine_select(out=part, in_=part, compare_op=ALU.is_ge, fill=0.0, base=0,
                           pattern=[[-8, 4]], channel_multiplier=1).then_inc(const_step, 1)
        n += 1
        pool.wait_ge(const_step, n)
        pool.affine_select(out=part, in_=part, compare_op=ALU.is_ge, fill=0.0, base=7,
                           pattern=[[8, 4]], channel_multiplier=-1).then_inc(const_step, 1)
        n += 1
    return n


CONSTANTS = 8 + 6 + 8


def tile_statistics(dve, rows, lnst, agg, carrier, stats, n, step):
    tiles = rows.shape[1]
    dve.wait_ge(step, n * 4 + 1)
    for t in range(tiles):
        last = dve.bn_stats(lnst[:, t, :], rows[:, t, :])
    last.then_inc(step, 1)
    dve.wait_ge(step, n * 4 + 2)
    dve.memset(carrier[:, :], 0.0)
    for t in range(tiles):
        last = dve.bn_aggr(agg[:, t, :], lnst[:, t, :])
    last.then_inc(step, 1)
    dve.wait_ge(step, n * 4 + 3)
    dve.tensor_scalar(stats[:, bass.ds(n * tiles, tiles), :], agg[:, :, :], 1.0, None, ALU.mult).then_inc(step, 1)



GROUPS = 2
CHUNKS = [[(0, 0, 8), (1, 0, 4), (1, 4, 4)], [(0, 8, 8), (1, 8, 4), (1, 12, 4)]]
NEWTON = 4
PROJECT_AT = (1, 2, 4)


def stage1(nc, ctx, sems, dram, X, stats, c):
    def sb(name, shape, dt=F32):
        return ctx.enter_context(nc.sbuf_tensor("s1_" + name, shape, dt))

    def sem(name):
        return sems("s1_" + name)

    wqkv = sb("wqkv", [P, 3 * D])
    wo = sb("wo", [P, D])
    xin = [sb(f"xin{u}", [P, 2, D]) for u in range(2)]
    xT = sb("xT", [P, N])
    qT = [sb(f"qT{u}", [P, N]) for u in range(2)]
    kM = [sb(f"kM{u}", [P, 4, N]) for u in range(2)]
    vS = [sb(f"vS{u}", [P, 2, D]) for u in range(2)]
    root = [sb(f"root{s}", [P, 1024]) for s in range(3)]
    w = [sb(f"w{s}", [P, 1024]) for s in range(3)]
    wT = [sb(f"wT{s}", [P, 1024]) for s in range(3)]
    low = [sb(f"low{s}", [P, 8]) for s in range(3)]
    lam = [sb(f"lam{s}", [P, 8]) for s in range(3)]
    st = [sb(f"st{s}", [P, 8, 6]) for s in range(3)]
    sq = [sb(f"sq{s}", [P, 8, 2]) for s in range(3)]
    s2p = [sb(f"s2p{s}", [P, 8, 2]) for s in range(3)]
    s2 = [sb(f"s2{s}", [P, 8]) for s in range(3)]
    s1 = [sb(f"s1{s}", [P, 8]) for s in range(3)]
    rs2 = [sb(f"rs2{s}", [P, 8]) for s in range(3)]
    step = [sb(f"step{s}", [P, 8]) for s in range(3)]
    step_hi = [sb(f"step_hi{s}", [P, 8], F16) for s in range(3)]
    step_lo = [sb(f"step_lo{s}", [P, 8], F16) for s in range(3)]
    rinv = [sb(f"rinv{u}", [P, 2, H]) for u in range(2)]
    o_sb = sb("o_sb", [P, 2, D])
    oT = sb("oT", [P, N])
    total = sb("total", [P, 2, D])
    lnst = sb("lnst", [P, 2, 6])
    agg = sb("agg", [P, 2, 2])
    dist = [ctx.enter_context(nc.psum_tensor(f"s1_dist{s}", [P, 1024], F32)) for s in range(3)]
    work = ctx.enter_context(nc.psum_tensor("s1_work", [P, 512], F32))
    heads_out = ctx.enter_context(nc.psum_tensor("s1_heads_out", [P, 2, H, DH], F32))

    weights_loaded = sem("weights_loaded")
    x_loaded = [sem(f"x_loaded{u}") for u in range(2)]
    x_turned = sem("x_turned")
    xT_ready = sem("xT_ready")
    qk_made = sem("qk_made")
    q_ready = sem("q_ready")
    k_ready = sem("k_ready")
    v_made = sem("v_made")
    v_ready = sem("v_ready")
    scores_ready = [sem(f"scores_ready{s}") for s in range(3)]
    lam_ready = [sem(f"lam_ready{s}") for s in range(3)]
    step_ready = [sem(f"step_ready{s}") for s in range(3)]
    dist_ready = [sem(f"dist_ready{s}") for s in range(3)]
    root_ready = [sem(f"root_ready{s}") for s in range(3)]
    w_ready = [sem(f"w_ready{s}") for s in range(3)]
    w_turned = [sem(f"w_turned{s}") for s in range(3)]
    wT_ready = [sem(f"wT_ready{s}") for s in range(3)]
    heads_made = sem("heads_made")
    rinv_ready = sem("rinv_ready")
    o_ready = sem("o_ready")
    o_turned = sem("o_turned")
    oT_ready = sem("oT_ready")
    out_made = sem("out_made")
    added = sem("added")
    dve_step = sem("dve_step")
    ln_step = sem("ln_step")

    DVE_STEPS = GROUPS * 3 * (1 + 6 * NEWTON + 3)
    def keys_of(g, s):
        return (CHUNKS[g][s][0] + 1) * P

    def per_head(ap, keys):
        return ap.rearrange("p (h k) -> p h k", k=keys)

    def bodies(eng, body):
        body(0, 0, first=True)
        body(1, 1)
        with eng.Fori(1, B // 2 - 1) as i:
            body(i * 2, 0)
            body(i * 2 + 1, 1)
        body(B - 2, 0)
        body(B - 1, 1, last=True)

    with nc.Block() as block:

        @block.gpsimd
        def _(pool):
            def body(n, u, first=False, last=False):
                for g in range(GROUPS):
                    for it in range(NEWTON + 1):
                        pool.wait_ge(root_ready[2], (n * GROUPS + g) * (NEWTON + 1) + it + 1)
                        pool.tensor_tensor(w[2][:, :], root[2][:, :], root[2][:, :], ALU.mult).then_inc(w_ready[2], 1)

            bodies(pool, body)

        @block.sync
        def _(sp):
            sp.dma_start(wqkv[:, :], dram["WqkvT"]).then_inc(weights_loaded, 16)
            sp.dma_start(wo[:, :], dram["WoT"]).then_inc(weights_loaded, 16)
            src = dram["L0_attn_x"].rearrange("b (t p) d -> b p t d", p=P)
            sp.dma_start(xin[0][:, :, :], src[0]).then_inc(x_loaded[0], 16)
            sp.dma_start(xin[1][:, :, :], src[1]).then_inc(x_loaded[1], 16)
            with sp.Fori(1, B // 2) as i:
                for u in range(2):
                    sp.wait_ge(added, i * 2 + u - 1)
                    sp.dma_start(xin[u][:, :, :], src[bass.ds(i * 2 + u, 1)].squeeze(0)).then_inc(x_loaded[u], 16)

        @block.tensor
        def _(pe):
            pe.wait_ge(c["const_step"], CONSTANTS)
            pe.wait_ge(weights_loaded, 32)

            def project(n, u, part, loads):
                if part == 0:
                    pe.wait_ge(x_loaded[u], loads * 16)
                    for t in range(2):
                        last = pe.transpose(work[:, t * P:(t + 1) * P], xin[u][:, t, :], c["ident"][:, :])
                    last.then_inc(x_turned, 1)
                if part == 1:
                    pe.wait_ge(xT_ready, n + 1)
                    for j in range(2):
                        last = pe.matmul(work[:, j * N:(j + 1) * N], wqkv[:, j * D:(j + 1) * D], xT[:, :],
                                         start=True, stop=True)
                    last.then_inc(qk_made, 1)
                if part == 2:
                    pe.wait_ge(q_ready, n + 1)
                    pe.wait_ge(k_ready, n + 1)
                    for t in range(2):
                        last = pe.matmul(work[:, t * D:(t + 1) * D], xT[:, t * P:(t + 1) * P], wqkv[:, 2 * D:],
                                         start=True, stop=True)
                    last.then_inc(v_made, 1)

            def finish(n, part):
                if part == 0:
                    pe.wait_ge(o_ready, n + 1)
                    for t in range(2):
                        last = pe.transpose(work[:, t * P:(t + 1) * P], o_sb[:, t, :], c["ident"][:, :])
                    last.then_inc(o_turned, 1)
                else:
                    pe.wait_ge(oT_ready, n + 1)
                    for t in range(2):
                        last = pe.matmul(work[:, t * D:(t + 1) * D], oT[:, t * P:(t + 1) * P], wo[:, :],
                                         start=True, stop=True)
                    last.then_inc(out_made, 1)

            def weigh_values(n, u, g, s, first=False):
                half, h0, nh = CHUNKS[g][s]
                pe.wait_ge(wT_ready[s], n * GROUPS + g + 1)
                if g == 0 and s == 0 and not first:
                    pe.wait_ge(o_ready, n)
                if g == 0 and s == 0:
                    pe.wait_ge(v_ready, n + 1)
                for h in range(nh):
                    for kb in range(half + 1):
                        col = (h * (half + 1) + kb) * P
                        last = pe.matmul(heads_out[:, half, h0 + h, :], wT[s][:, col:col + P],
                                         vS[u][:, kb, (h0 + h) * DH:(h0 + h + 1) * DH],
                                         start=(kb == 0), stop=(kb == half), skip_group_check=True)
                if g == GROUPS - 1 and s == 2:
                    last.then_inc(heads_made, 1)

            def score(n, u, g, s):
                half, h0, nh = CHUNKS[g][s]
                keys = keys_of(g, s)
                pe.wait_ge(q_ready, n + 1)
                pe.wait_ge(k_ready, n + 1)
                for h in range(nh):
                    r, m = divmod(h0 + h, 4)
                    pe.matmul(dist[s][:, h * keys:(h + 1) * keys], qT[u][32 * r:32 * r + 32, half * P:(half + 1) * P],
                              kM[u][32 * r:32 * r + 32, m, 0:keys], start=(h * keys % 512 == 0), stop=False,
                              skip_group_check=True)
                for bank in range(2):
                    out = per_head(dist[s][:, bank * 512:(bank + 1) * 512], keys)
                    last = pe.matmul(out[:, :, keys - P:keys], c["ident_bf"][:, :],
                                     broadcast_middle(c["far_mask"][:, :], 512 // keys),
                                     start=False, stop=False, skip_group_check=True)
                last.then_inc(scores_ready[s], 1)

            def move(g, s, identity, parts):
                keys = keys_of(g, s)
                per = 512 // keys
                for bank in range(2):
                    out = per_head(dist[s][:, bank * 512:(bank + 1) * 512], keys)
                    for part in parts:
                        last = pe.matmul(out, identity[:, :], broadcast_last(part[:, bank * per:(bank + 1) * per], keys),
                                         start=False, stop=False, skip_group_check=True)
                last.then_inc(dist_ready[s], 1)

            def body(n, u, pair, first=False, last=False):
                for g in range(GROUPS):
                    use = n * GROUPS + g
                    for s in range(3):
                        if g == 1:
                            weigh_values(n, u, 0, s, first)
                        elif not first:
                            weigh_values(n - 1, 1 - u, 1, s)
                        score(n, u, g, s)
                    for s in range(3):
                        pe.wait_ge(lam_ready[s], use + 1)
                        move(g, s, c["ident"], [lam[s]])
                    for it in range(1, NEWTON + 1):
                        if g == 0 and it in (1, 2) and not first:
                            finish(n - 1, it - 1)
                        if g == 1 and it in PROJECT_AT and not last:
                            project(n + 1, 1 - u, PROJECT_AT.index(it), pair + 1 + u)
                        for s in range(3):
                            pe.wait_ge(step_ready[s], use * NEWTON + it)
                            move(g, s, c["ident_h"], [step_hi[s], step_lo[s]])
                    for s in range(3):
                        pe.wait_ge(w_ready[s], (use + 1) * (NEWTON + 1))
                        for k in range(8):
                            t = pe.transpose(dist[s][:, k * P:(k + 1) * P], w[s][:, k * P:(k + 1) * P], c["ident"][:, :])
                        t.then_inc(w_turned[s], 1)
                if last:
                    for s in range(3):
                        weigh_values(n, u, 1, s)
                    pe.wait_ge(added, n)
                    finish(n, 0)
                    finish(n, 1)

            for part in range(3):
                project(0, 0, part, 1)
            body(0, 0, 0, first=True)
            body(1, 1, 0)
            with pe.Fori(1, B // 2 - 1) as i:
                body(i * 2, 0, i)
                body(i * 2 + 1, 1, i)
            body(B - 2, 0, B // 2 - 1)
            body(B - 1, 1, B // 2 - 1, last=True)

        @block.scalar
        def _(act):
            def copy_qv(n, u, part):
                if part == 0:
                    act.wait_ge(x_turned, n + 1)
                    act.activation(xT[:, :], work[:, 0:N], ACT.Copy).then_inc(xT_ready, 1)
                if part == 1:
                    act.wait_ge(qk_made, n + 1)
                    act.activation(qT[u][:, :], work[:, 0:N], ACT.Copy, scale=-float(DH) ** -0.5).then_inc(q_ready, 1)
                if part == 2:
                    act.wait_ge(v_made, n + 1)
                    act.activation(vS[u][:, :, :], work[:, 0:N].rearrange("p (t d) -> p t d", t=2), ACT.Copy)\
                        .then_inc(v_ready, 1)

            def copy_oT(n):
                act.wait_ge(o_turned, n + 1)
                act.activation(oT[:, :], work[:, 0:N], ACT.Copy).then_inc(oT_ready, 1)

            def roots(k, s):
                act.wait_ge(dist_ready[s], k)
                act.activation(root[s][:, :], dist[s][:, :], ACT.Abs_reciprocal_sqrt).then_inc(root_ready[s], 1)

            def square(k, s):
                act.wait_ge(root_ready[s], k)
                act.activation(w[s][:, :], root[s][:, :], ACT.Square).then_inc(w_ready[s], 1)

            def body(n, u, first=False, last=False):
                for g in range(GROUPS):
                    use = n * GROUPS + g
                    for it in range(NEWTON + 1):
                        k = use * (NEWTON + 1) + it + 1
                        roots(k, 0)
                        roots(k, 1)
                        square(k, 0)
                        roots(k, 2)
                        square(k, 1)
                        if g == 0 and it == 1 and not first:
                            copy_oT(n - 1)
                        if g == 1 and it in PROJECT_AT and not last:
                            copy_qv(n + 1, 1 - u, PROJECT_AT.index(it))
                    for s in range(3):
                        act.wait_ge(w_turned[s], use + 1)
                        act.activation(wT[s][:, :], dist[s][:, :], ACT.Copy).then_inc(wT_ready[s], 1)
                if last:
                    copy_oT(n)

            for part in range(3):
                copy_qv(0, 0, part)
            bodies(act, body)

        @block.vector
        def _(dve):
            steps = [0, 0]

            def settle(ins):
                steps[1] += 1
                ins.then_inc(dve_step, 1)
                dve.wait_ge(dve_step, steps[0] * DVE_STEPS + steps[1])

            def mask_k(n, u):
                dve.wait_ge(q_ready, n + 1)
                for m in range(4):
                    last = dve.tensor_scalar(kM[u][:, m, :], work[:, N:2 * N], c["row_mask"][:, m:m + 1], None, ALU.mult)
                last.then_inc(k_ready, 1)

            def first_lambda(use, g, s):
                nh = CHUNKS[g][s][2]
                dve.wait_ge(scores_ready[s], use + 1)
                settle(dve.tensor_reduce(low[s][:, 0:nh], per_head(dist[s][:, :], keys_of(g, s)), AX.X, ALU.min))
                dve.tensor_scalar(lam[s][:, 0:nh], low[s][:, 0:nh], -1.0, 1.0, ALU.mult, ALU.add).then_inc(lam_ready[s], 1)

            def moments(k, g, s):
                keys = keys_of(g, s)
                dve.wait_ge(w_ready[s], k)
                for h in range(CHUNKS[g][s][2]):
                    last = dve.bn_stats(st[s][:, h, :], w[s][:, h * keys:(h + 1) * keys])
                settle(last)

            def newton(k, g, s):
                nh, keys = CHUNKS[g][s][2], keys_of(g, s)
                count = keys / 2
                moments(k, g, s)
                v = st[s][:, 0:nh, :].rearrange("p h (a c) -> p h a c", c=3)
                dve.tensor_tensor(s1[s][:, 0:nh], v[:, :, 0, 1], v[:, :, 1, 1], ALU.add)
                settle(dve.tensor_tensor(sq[s][:, 0:nh, :], v[:, :, :, 1], v[:, :, :, 1], ALU.mult))
                settle(dve.scalar_tensor_tensor(s2p[s][:, 0:nh, :], v[:, :, :, 2], 1.0 / count, sq[s][:, 0:nh, :],
                                                ALU.mult, ALU.add))
                settle(dve.tensor_tensor(s2[s][:, 0:nh], s2p[s][:, 0:nh, 0], s2p[s][:, 0:nh, 1], ALU.add))
                settle(dve.reciprocal(rs2[s][:, 0:nh], s2[s][:, 0:nh]))
                dve.scalar_tensor_tensor(step[s][:, 0:nh], s1[s][:, 0:nh], -1.0 / count, rs2[s][:, 0:nh], ALU.add, ALU.mult)
                settle(dve.scalar_tensor_tensor(step_hi[s][:, 0:nh], s1[s][:, 0:nh], -1.0 / count, rs2[s][:, 0:nh],
                                                ALU.add, ALU.mult))
                dve.tensor_tensor(step_lo[s][:, 0:nh], step[s][:, 0:nh], step_hi[s][:, 0:nh], ALU.subtract)\
                    .then_inc(step_ready[s], 1)

            def row_sums(k, g, s, u):
                half, h0, nh = CHUNKS[g][s]
                moments(k, g, s)
                v = st[s][:, 0:nh, :].rearrange("p h (a c) -> p h a c", c=3)
                settle(dve.tensor_tensor(s1[s][:, 0:nh], v[:, :, 0, 1], v[:, :, 1, 1], ALU.add))
                settle(dve.reciprocal(rs2[s][:, 0:nh], s1[s][:, 0:nh]))
                dve.tensor_scalar(rinv[u][:, half, h0:h0 + nh], rs2[s][:, 0:nh], 2.0 / keys_of(g, s), None, ALU.mult)\
                    .then_inc(rinv_ready, 1)

            def normalise(n, u):
                dve.wait_ge(heads_made, n + 1)
                dve.wait_ge(rinv_ready, (n + 1) * GROUPS * 3)
                for half in range(2):
                    last = dve.tensor_tensor(o_sb[:, half, :].rearrange("p (h d) -> p h d", d=DH), heads_out[:, half, :, :],
                                             broadcast_last(rinv[u][:, half, :], DH), ALU.mult)
                last.then_inc(o_ready, 1)

            def add(n, u):
                dve.wait_ge(out_made, n + 1)
                attended = work[:, 0:2 * D].rearrange("p (t d) -> p t d", t=2)
                dve.tensor_tensor(total[:, :, :], attended, xin[u][:, :, :], ALU.add).then_inc(ln_step, 1)
                dve.tensor_tensor(X[:, bass.ds(n * 2, 2), :], attended, xin[u][:, :, :], ALU.add).then_inc(added, 1)
                tile_statistics(dve, total, lnst, agg, c["carrier"], stats, n, ln_step)

            def body(n, u, first=False, last=False):
                steps[0], steps[1] = n, 0
                for g in range(GROUPS):
                    use = n * GROUPS + g
                    for s in range(3):
                        first_lambda(use, g, s)
                    if g == 0 and not first:
                        normalise(n - 1, 1 - u)
                    for it in range(NEWTON):
                        for s in range(3):
                            newton(use * (NEWTON + 1) + it + 1, g, s)
                        if g == 0 and it == 1 and not first:
                            add(n - 1, 1 - u)
                        if g == 1 and it == 2 and not last:
                            mask_k(n + 1, 1 - u)
                    for s in range(3):
                        row_sums((use + 1) * (NEWTON + 1), g, s, u)
                assert steps[1] == DVE_STEPS
                if last:
                    normalise(n, u)
                    add(n, u)

            dve.wait_ge(c["const_step"], CONSTANTS)
            mask_k(0, 0)
            bodies(dve, body)



def inverse_roots(nc, ctx, sems, name, chains):
    ends = []
    made = sems(name + "_made")
    rooted = sems(name + "_rooted")
    shift = [ctx.enter_context(nc.sbuf_tensor(f"{name}_shift{i}", [P, TILES], F32)) for i in range(len(chains))]
    with nc.Block() as block:

        @block.vector
        def _(dve):
            n = 0
            for i, (source, out, eps) in enumerate(chains):
                if i:
                    dve.wait_ge(rooted, i)
                for ins in source(dve, shift[i]):
                    n += 1
                    ins.then_inc(made, 1)
                    dve.wait_ge(made, n)
                n += 1
                dve.tensor_scalar(shift[i][:, :], shift[i][:, :], eps, None, ALU.add).then_inc(made, 1)
                ends.append(n)

        @block.scalar
        def _(act):
            for i, (source, out, eps) in enumerate(chains):
                act.wait_ge(made, ends[i])
                act.activation(out[:, :], shift[i][:, :], ACT.Abs_reciprocal_sqrt).then_inc(rooted, 1)



def router(nc, ctx, sems, name, X, centre, scale, gain, keep_rows, hT_all, weights, logits, c):
    def sb(n, shape, dt=F32):
        return ctx.enter_context(nc.sbuf_tensor(f"{name}_{n}", shape, dt))

    E = weights.shape[1]
    wr = sb("wr", [P, E])
    rows = [sb(f"rows{u}", [P, 2, D]) for u in range(2)]
    rT = [sb(f"rT{u}", [P, N]) for u in range(2)]
    gcol = sb("gcol", [P, 1]) if gain is not None else None
    turn = [ctx.enter_context(nc.psum_tensor(f"{name}_turn{u}", [P, 512], F32)) for u in range(2)]
    lg = [ctx.enter_context(nc.psum_tensor(f"{name}_lg{u}", [P, 2, E], F32)) for u in range(2)]
    loaded = sems(name + "_loaded")
    rows_ready = sems(name + "_rows_ready")
    rows_kept = sems(name + "_rows_kept")
    turned = sems(name + "_turned")
    rT_ready = sems(name + "_rT_ready")
    lg_made = sems(name + "_lg_made")
    lg_read = sems(name + "_lg_read")
    NB = B

    def pairs(eng, body):
        body(0, 0, True)
        body(1, 1, True)
        with eng.Fori(1, NB // 2) as i:
            body(i * 2, 0, False)
            body(i * 2 + 1, 1, False)

    with nc.Block() as block:

        @block.sync
        def _(sp):
            sp.dma_start(wr[:, :], weights).then_inc(loaded, 16)
            if gain is not None:
                sp.dma_start(gcol[:, :], gain).then_inc(loaded, 16)

        @block.vector
        def _(dve):
            def normalise(n, u, first):
                if not first:
                    dve.wait_ge(turned, n - 1)
                    if keep_rows:
                        dve.wait_ge(rows_kept, n - 1)
                for t in range(2):
                    tile = n * 2 + t
                    x = X[:, bass.ds(tile, 1), :].squeeze(1)
                    s = scale[:, bass.ds(tile, 1)]
                    if centre is None:
                        last = dve.tensor_scalar(rows[u][:, t, :], x, s, None, ALU.mult)
                    else:
                        last = dve.tensor_scalar(rows[u][:, t, :], x, centre[:, bass.ds(tile, 1), 0], s,
                                                 ALU.subtract, ALU.mult)
                last.then_inc(rows_ready, 1)

            def body(n, u, first):
                if first and u == 0:
                    normalise(0, 0, True)
                if first and u == 0:
                    normalise(1, 1, True)
                elif first:
                    normalise(2, 0, False)
                else:
                    normalise_next(n, u)
                dve.wait_ge(lg_made, n + 1)
                dve.tensor_scalar(logits[:, bass.ds(n * 2, 2), :], lg[u][:, :, :], 1.0, None, ALU.mult)\
                    .then_inc(lg_read, 1)

            def normalise_next(n, u):
                normalise(n + 1, 1 - u, False)

            body(0, 0, True)
            body(1, 1, True)
            with dve.Fori(1, NB // 2 - 1) as i:
                body(i * 2, 0, False)
                body(i * 2 + 1, 1, False)
            body(NB - 2, 0, False)
            dve.wait_ge(lg_made, NB)
            dve.tensor_copy(logits[:, 2 * NB - 2:2 * NB, :], lg[1][:, :, :])

        @block.gpsimd
        def _(pool):
            def body(n, u, first):
                if keep_rows:
                    pool.wait_ge(rows_ready, n + 1)
                    pool.tensor_copy(X[:, bass.ds(n * 2, 2), :], rows[u][:, :, :]).then_inc(rows_kept, 1)
            if keep_rows:
                pairs(pool, body)

        @block.tensor
        def _(pe):
            pe.wait_ge(loaded, 32 if gain is not None else 16)

            def body(n, u, first):
                pe.wait_ge(rows_ready, n + 1)
                if not first:
                    pe.wait_ge(rT_ready, n - 1)
                for t in range(2):
                    last = pe.transpose(turn[u][:, t * P:(t + 1) * P], rows[u][:, t, :], c["ident"][:, :])
                last.then_inc(turned, 1)
                if not first:
                    pe.wait_ge(lg_read, n - 1)
                pe.wait_ge(rT_ready, n + 1)
                for t in range(2):
                    last = pe.matmul(lg[u][:, t, :], rT[u][:, t * P:(t + 1) * P], wr[:, :], start=True, stop=True)
                last.then_inc(lg_made, 1)

            pairs(pe, body)

        @block.scalar
        def _(act):
            act.wait_ge(loaded, 32 if gain is not None else 16)

            def body(n, u, first):
                if not first:
                    act.wait_ge(lg_made, n - 1)
                act.wait_ge(turned, n + 1)
                g = gcol[:, 0:1] if gain is not None else 1.0
                act.activation(rT[u][:, :], turn[u][:, 0:N], ACT.Identity, scale=g).then_inc(rT_ready, 1)
                if hT_all is not None:
                    act.wait_ge(rT_ready, n + 1)
                    act.activation(hT_all[:, bass.ds(n * N, N)], rT[u][:, :], ACT.Copy)

            pairs(act, body)



E1 = 8
F1 = 512
CAP = int(1.25 * B * N / E1)
ROWS = 256
FAR = float(1 << 20)


def stage2(nc, ctx, sems, dram, X, stats, logits, c):
    def sb(name, shape, dt=F32):
        return ctx.enter_context(nc.sbuf_tensor("s2_" + name, shape, dt))

    def ps(name, shape):
        return ctx.enter_context(nc.psum_tensor("s2_" + name, shape, F32))

    T = TILES
    best = sb("best", [P, T])
    eq = sb("eq", [P, T, E1])
    hot = sb("hot", [P, T, E1])
    shifted = sb("shifted", [P, T, E1])
    tot = sb("tot", [P, T, E1])
    upto = sb("upto", [P, T, E1])
    place = sb("place", [P, T, E1])
    rank = sb("rank", [P, T])
    pos = sb("pos", [P, T])
    first_slot = sb("first_slot", [P, T])
    kept = sb("kept", [P, T])
    total = sb("total", [P, T])
    factor = sb("factor", [P, T])
    slot = sb("slot", [P, T])
    slot_u = sb("slot_u", [P, T], U32)
    early = sb("early", [P, E1])
    begin = sb("begin", [P, E1])
    unit = sb("unit", [P, T])
    cum_ps = ps("cum_ps", [P, T, E1])
    tot_ps = ps("tot_ps", [P, T, E1])
    col = sems("s2_col")
    hot_ready = sems("s2_hot_ready")
    sums_made = sems("s2_sums_made")
    shifted_ready = sems("s2_shifted_ready")
    exp_ready = sems("s2_exp_ready")
    step = sems("s2_step")

    with nc.Block() as block:

        @block.gpsimd
        def _(pool):
            pool.iota(early[:, :], pattern=[[-1, E1]], base=E1, channel_multiplier=0,
                      allow_small_or_imprecise_dtypes=True).then_inc(col, 1)
            pool.iota(begin[:, :], pattern=[[CAP, E1]], base=0, channel_multiplier=0,
                      allow_small_or_imprecise_dtypes=True).then_inc(col, 1)

        @block.tensor
        def _(pe):
            pe.wait_ge(hot_ready, 1)
            flat = hot[:, :, :].rearrange("p t e -> p (t e)")
            pe.matmul(cum_ps[:, :, :].rearrange("p t e -> p (t e)"), c["prefix"][:, :], flat, start=True, stop=True)
            pe.matmul(tot_ps[:, :, :].rearrange("p t e -> p (t e)"), c["ones"][:, :], flat, start=True, stop=True)\
                .then_inc(sums_made, 1)

        @block.scalar
        def _(act):
            act.wait_ge(shifted_ready, 1)
            act.activation(shifted[:, :, :], shifted[:, :, :], ACT.Exp).then_inc(exp_ready, 1)

        @block.vector
        def _(dve):
            n = [0]

            def settle(ins):
                n[0] += 1
                ins.then_inc(step, 1)
                dve.wait_ge(step, n[0])

            by_tile = lambda t: broadcast_last(t[:, :], E1)
            dve.memset(unit[:, :], 1.0)
            settle(dve.tensor_reduce(best[:, :], logits[:, :, :], AX.X, ALU.max))
            dve.tensor_tensor(shifted[:, :, :], logits[:, :, :], by_tile(best), ALU.subtract)\
                .then_inc(shifted_ready, 1)
            settle(dve.tensor_tensor(eq[:, :, :], logits[:, :, :], by_tile(best), ALU.is_equal))
            dve.wait_ge(col, 2)
            settle(dve.tensor_tensor(eq[:, :, :], eq[:, :, :], broadcast_middle(early[:, :], T), ALU.mult))
            settle(dve.tensor_reduce(rank[:, :], eq[:, :, :], AX.X, ALU.max))
            settle(dve.tensor_tensor(hot[:, :, :], eq[:, :, :], by_tile(rank), ALU.is_equal))
            dve.sem_inc(hot_ready, 1)
            dve.wait_ge(sums_made, 1)
            settle(dve.tensor_copy(tot[:, :, :], tot_ps[:, :, :]))
            for e in range(E1):
                last = dve.tensor_tensor_scan(upto[:, :, e], unit[:, :], tot[:, :, e], 0.0, ALU.mult, ALU.add)
            settle(last)
            settle(dve.tensor_tensor(upto[:, :, :], upto[:, :, :], tot[:, :, :], ALU.subtract))
            settle(dve.tensor_tensor(place[:, :, :], upto[:, :, :], cum_ps[:, :, :], ALU.add))
            settle(dve.tensor_tensor(place[:, :, :], place[:, :, :], hot[:, :, :], ALU.mult))
            settle(dve.tensor_reduce(pos[:, :], place[:, :, :], AX.X, ALU.add))
            settle(dve.tensor_tensor(eq[:, :, :], hot[:, :, :], broadcast_middle(begin[:, :], T), ALU.mult))
            settle(dve.tensor_reduce(first_slot[:, :], eq[:, :, :], AX.X, ALU.add))
            settle(dve.tensor_scalar(kept[:, :], pos[:, :], float(CAP), None, ALU.is_le))
            settle(dve.scalar_tensor_tensor(slot[:, :], pos[:, :], FAR - 1.0, first_slot[:, :], ALU.add, ALU.add))
            settle(dve.scalar_tensor_tensor(slot[:, :], kept[:, :], -FAR, slot[:, :], ALU.mult, ALU.add))
            settle(dve.tensor_copy(slot_u[:, :], slot[:, :]))
            dve.wait_ge(exp_ready, 1)
            settle(dve.tensor_reduce(total[:, :], shifted[:, :, :], AX.X, ALU.add))
            settle(dve.reciprocal(factor[:, :], total[:, :]))
            settle(dve.scalar_tensor_tensor(factor[:, :], factor[:, :], -1.0, kept[:, :], ALU.add, ALU.mult))
            settle(dve.tensor_scalar(factor[:, :], factor[:, :], 1.0, None, ALU.add))

    slots, done = dram["slots"], dram["done"]
    dispatched = sems("s2_dispatched")
    with nc.Block() as block:

        @block.gpsimd
        def _(pool):
            for t in range(T):
                pool.indirect_dma_start(slots, bass.IndirectOffsetOnAxis(ap=slot_u[:, t:t + 1], axis=0), X[:, t, :], None,
                                        bounds_check=E1 * CAP - 1, oob_is_err=False).then_inc(dispatched, 16)
            pool.wait_ge(dispatched, 16 * T)

    w1 = [sb(f"w1{u}", [P, F1]) for u in range(2)]
    w2 = [sb(f"w2{u}", [P, F1 // P, D]) for u in range(2)]
    rows = [sb(f"rows{v}", [P, 2, D]) for v in range(2)]
    rT = [sb(f"rT{v}", [P, ROWS]) for v in range(2)]
    hid = [sb(f"hid{v}", [P, F1 // P, ROWS]) for v in range(2)]
    res = [sb(f"res{v}", [P, 2, D]) for v in range(2)]
    with ExitStack() as inner:
        def psi(name, shape):
            return inner.enter_context(nc.psum_tensor("s2_" + name, shape, F32))

        turn_out = [psi(f"turn_out{v}", [P, 512]) for v in range(1)]
        hid_ps = [psi(f"hid_ps{v}", [P, F1 // P, ROWS]) for v in range(2)]
        out_ps = psi("out_ps", [P, 2, D])
        w_loaded = [sems(f"s2_w_loaded{u}") for u in range(2)]
        r_loaded = [sems(f"s2_r_loaded{v}") for v in range(2)]
        r_turned = sems("s2_r_turned")
        rT_ready = sems("s2_rT_ready")
        hid_made = sems("s2_hid_made")
        hid_ready = sems("s2_hid_ready")
        out_made = sems("s2_out_made")
        out_ready = sems("s2_out_ready")
        stored = [sems(f"s2_stored{v}") for v in range(2)]
        GPE = CAP // ROWS
        groups = E1 * GPE
        src = slots.rearrange("(g t p) d -> g p t d", p=P, t=2)
        dst = done.rearrange("(g t p) d -> g p t d", p=P, t=2)
        PER = 2 * GPE

        with nc.Block() as block:

            def pairs(eng, body, tail):
                for j in range(PER):
                    body(j, j % 2, j // GPE, j < 2, 0, j)
                with eng.Fori(1, E1 // 2) as i:
                    for j in range(PER):
                        body(i * PER + j, j % 2, j // GPE, False, i, j)

            @block.sync
            def _(sp):
                def load_w(e, u):
                    sp.dma_start(w1[u][:, :], dram["L0_ffn_W1"][bass.ds(e, 1)].squeeze(0)).then_inc(w_loaded[u], 16)
                    sp.dma_start(w2[u][:, :, :], dram["L0_ffn_W2"].rearrange("e (f p) d -> e p f d", p=P)[bass.ds(e, 1)]
                                 .squeeze(0)).then_inc(w_loaded[u], 16)

                def body(g, v, u, first, i, j):
                    if j % GPE == 0:
                        if not (isinstance(i, int)):
                            sp.wait_ge(out_made, g - GPE)
                        load_w(i * 2 + u, u)
                    if not first:
                        sp.wait_ge(r_turned, g - 1)
                    sp.dma_start(rows[v][:, :, :], src[bass.ds(g, 1)].squeeze(0)).then_inc(r_loaded[v], 16)

                pairs(sp, body, None)

            @block.tensor
            def _(pe):
                def turn(g, v, first, loads):
                    pe.wait_ge(r_loaded[v], loads * 16)
                    if not first:
                        pe.wait_ge(rT_ready, g)
                    for t in range(2):
                        last = pe.transpose(turn_out[0][:, t * P:(t + 1) * P], rows[v][:, t, :], c["ident"][:, :])
                    last.then_inc(r_turned, 1)

                def down(g, v, u, first):
                    pe.wait_ge(hid_ready, g + 1)
                    if not first:
                        pe.wait_ge(out_ready, g)
                    for t in range(2):
                        for f in range(F1 // P):
                            last = pe.matmul(out_ps[:, t, :], hid[v][:, f, t * P:(t + 1) * P], w2[u][:, f, :],
                                             start=(f == 0), stop=(f == F1 // P - 1), skip_group_check=True)
                    last.then_inc(out_made, 1)

                def up(g, v, u, first, loads):
                    pe.wait_ge(w_loaded[u], loads * 32)
                    pe.wait_ge(rT_ready, g + 1)
                    if not first:
                        pe.wait_ge(hid_ready, g - 1)
                    for f in range(F1 // P):
                        last = pe.matmul(hid_ps[v][:, f, :], w1[u][:, f * P:(f + 1) * P], rT[v][:, :],
                                         start=True, stop=True)
                    last.then_inc(hid_made, 1)

                def body(g, v, u, first, i, j):
                    begins = isinstance(i, int) and j == 0
                    turn(g, v, begins, i * GPE + j // 2 + 1)
                    up(g, v, u, first, i + 1)
                    if not begins:
                        down(g - 1, 1 - v, (u if j % GPE else 1 - u), isinstance(i, int) and j == 1)

                pairs(pe, body, None)
                down(groups - 1, 1, 1, False)

            @block.scalar
            def _(act):
                def body(g, v, u, first, i, j):
                    act.wait_ge(r_turned, g + 1)
                    if not first:
                        act.wait_ge(hid_made, g - 1)
                    act.activation(rT[v][:, :], turn_out[0][:, 0:ROWS], ACT.Copy).then_inc(rT_ready, 1)
                    act.wait_ge(hid_made, g + 1)
                    if not first:
                        act.wait_ge(out_made, g - 1)
                    act.activation(hid[v][:, :, :], hid_ps[v][:, :, :], ACT.Relu).then_inc(hid_ready, 1)

                pairs(act, body, None)

            @block.vector
            def _(dve):
                def body(g, v, u, first, i, j):
                    dve.wait_ge(out_made, g + 1)
                    if not first:
                        dve.wait_ge(stored[v], (i * GPE + j // 2) * 16)
                    dve.tensor_copy(res[v][:, :, :], out_ps[:, :, :]).then_inc(out_ready, 1)

                pairs(dve, body, None)

            @block.gpsimd
            def _(pool):
                def body(g, v, u, first, i, j):
                    pool.wait_ge(out_ready, g + 1)
                    pool.dma_start(dst[bass.ds(g, 1)].squeeze(0), res[v][:, :, :]).then_inc(stored[v], 16)

                pairs(pool, body, None)
                for v in range(2):
                    pool.wait_ge(stored[v], 16 * groups // 2)

    G = sb("G", [P, T, D])
    own = sems("s2_own")
    GATHERS = 4
    gathered = [sems(f"s2_gathered{i}") for i in range(GATHERS)]
    lnst = sb("lnst", [P, T, 6])
    ln = sems("s2_ln")
    with nc.Block() as block:

        @block.scalar
        def _(act):
            for i in range(GATHERS):
                part = slice(i * T // GATHERS, (i + 1) * T // GATHERS)
                act.activation(G[:, part, :], X[:, part, :], ACT.Copy).then_inc(own, 1)

        @block.gpsimd
        def _(pool):
            for i in range(GATHERS):
                pool.wait_ge(own, i + 1)
                for t in range(i * T // GATHERS, (i + 1) * T // GATHERS):
                    pool.indirect_dma_start(G[:, t, :], None, done, bass.IndirectOffsetOnAxis(ap=slot_u[:, t:t + 1], axis=0),
                                            bounds_check=E1 * CAP - 1, oob_is_err=False).then_inc(gathered[i], 16)

        @block.vector
        def _(dve):
            for i in range(GATHERS):
                dve.wait_ge(gathered[i], 16 * (T // GATHERS))
                for t in range(i * T // GATHERS, (i + 1) * T // GATHERS):
                    last = dve.scalar_tensor_tensor(X[:, t, :], G[:, t, :], factor[:, t:t + 1], X[:, t, :],
                                                    ALU.mult, ALU.add)
                last.then_inc(ln, 1)
                dve.wait_ge(ln, 2 * i + 1)
                for t in range(i * T // GATHERS, (i + 1) * T // GATHERS):
                    last = dve.bn_stats(lnst[:, t, :], X[:, t, :])
                last.then_inc(ln, 1)
                dve.wait_ge(ln, 2 * i + 2)
                for t in range(i * T // GATHERS, (i + 1) * T // GATHERS):
                    dve.bn_aggr(stats[:, t, :], lnst[:, t, :])


def zero_slots(nc, ctx, sems, dram, c):
    zeros = ctx.enter_context(nc.sbuf_tensor("zeros", [P, 1280], F32))
    zeroed = sems("zeroed")
    slots_zeroed = sems("slots_zeroed")
    view = dram["slots"].rearrange("(c p r) d -> c p (r d)", p=P, r=10)
    with nc.Block() as block:

        @block.gpsimd
        def _(pool):
            make_constants(pool, c, c["const_step"])

        @block.vector
        def _(dve):
            dve.memset(zeros[:, :], 0.0).then_inc(zeroed, 1)

        @block.sync
        def _(sp):
            sp.wait_ge(zeroed, 1)
            for k in range(E1 * CAP // (10 * P)):
                sp.dma_start(view[k], zeros[:, :]).then_inc(slots_zeroed, 16)
            sp.wait_ge(slots_zeroed, 16 * (E1 * CAP // (10 * P)))



ATT_CHUNKS = [(0, 0, 8), (1, 0, 4), (1, 4, 4), (0, 8, 8), (1, 8, 4), (1, 12, 4)]
STEPS = len(ATT_CHUNKS)


def softmax_stage(nc, ctx, sems, name, X, kept, centre, scale, second_scale, stats, c, kind):
    def sb(n, shape, dt=F32):
        return ctx.enter_context(nc.sbuf_tensor(f"{name}_{n}", shape, dt))

    def ps(n, shape):
        return ctx.enter_context(nc.psum_tensor(f"{name}_{n}", shape, F32))

    rows = [sb(f"rows{u}", [P, 2, D]) for u in range(2)]
    lean_rows = [sb(f"lean_rows{u}", [P, 2, D]) for u in range(2)] if second_scale is not None else None
    scores = [ps(f"scores{s}", [P, 1024]) for s in range(2)]
    heads = [ps(f"heads{s}", [P, 512]) for s in range(2)]
    work = [ps(f"work{s}", [P, 512]) for s in range(2)]
    att = [sb(f"att{s}", [P, 1024]) for s in range(2)]
    attT = [sb(f"attT{s}", [P, 1024]) for s in range(2)]
    peak = [sb(f"peak{s}", [P, 8]) for s in range(2)]
    total = [sb(f"total{s}", [P, 8]) for s in range(2)]
    rinv = [sb(f"rinv{s}", [P, 8]) for s in range(2)]
    total_rows = sb("total_rows", [P, 2, D])
    lnst = sb("lnst", [P, 2, 6])
    agg = sb("agg", [P, 2, 2])

    weights_loaded = sems(name + "_weights_loaded")
    rows_ready = sems(name + "_rows_ready")
    rows_kept = sems(name + "_rows_kept")
    job_made = sems(name + "_job_made")
    job_read = sems(name + "_job_read")
    scored = [sems(f"{name}_scored{s}") for s in range(2)]
    peak_ready = [sems(f"{name}_peak_ready{s}") for s in range(2)]
    att_ready = [sems(f"{name}_att_ready{s}") for s in range(2)]
    turned = [sems(f"{name}_turned{s}") for s in range(2)]
    attT_ready = [sems(f"{name}_attT_ready{s}") for s in range(2)]
    heads_made = [sems(f"{name}_heads_made{s}") for s in range(2)]
    heads_read = [sems(f"{name}_heads_read{s}") for s in range(2)]
    rinv_ready = [sems(f"{name}_rinv_ready{s}") for s in range(2)]
    ln_step = sems(name + "_ln_step")

    k = kind(sb, c, rows if second_scale is None else lean_rows)
    project_jobs, finish_jobs = k["project"], k["finish"]
    NP, NF = len(project_jobs), len(finish_jobs)
    PROJECT_STEPS, FINISH_STEPS = k["project_steps"], k["finish_steps"]
    HDIM = k["head_dim"]

    def body_jobs(first=False, last=False):
        jobs = []
        for step in range(STEPS):
            jobs += [(step, True, a) for a, at in enumerate(PROJECT_STEPS) if at == step and not last]
            jobs += [(step, False, a) for a, at in enumerate(FINISH_STEPS) if at == step and not first]
        return jobs

    def jobs_before(n):
        return NP if isinstance(n, int) and n == 0 else (n + 1) * NP + (n - 1) * NF

    def bank_before(u, first):
        return NP if first else (u + 1) * (NP + NF)

    def projected(n):
        if isinstance(n, int) and n < 2:
            return (n + 1) * NP
        order = body_jobs()
        return jobs_before(n - 1) + max(i for i, (_, is_p, _) in enumerate(order) if is_p) + 1

    def run_step(n, u, step, first, last, run):
        for i, (at, is_p, a) in enumerate(body_jobs(first, last)):
            if at == step:
                run(n + 1 if is_p else n - 1, 1 - u, jobs_before(n) + i, (bank_before(u, first) + i) % 2, is_p, a)

    def run_tail(run):
        for a in range(NF):
            index = jobs_before(B - 1) + NF + a
            run(B - 1, (B - 1) % 2, index, index % 2, False, a)

    def bodies(eng, body):
        body(0, 0, first=True)
        body(1, 1)
        with eng.Fori(1, B // 2 - 1) as i:
            body(i * 2, 0)
            body(i * 2 + 1, 1)
        body(B - 2, 0)
        body(B - 1, 1, last=True)

    with nc.Block() as block:

        @block.sync
        def _(sp):
            for dst, src in k["loads"]:
                sp.dma_start(dst, src).then_inc(weights_loaded, 16)

        @block.gpsimd
        def _(pool):
            def keep(n, u):
                pool.wait_ge(rows_ready, n + 1)
                pool.tensor_copy(kept[:, bass.ds(n * 2, 2), :], rows[u][:, :, :]).then_inc(rows_kept, 1)

            keep(0, 0)
            keep(1, 1)
            with pool.Fori(1, B // 2) as i:
                keep(i * 2, 0)
                keep(i * 2 + 1, 1)

        @block.tensor
        def _(pe):
            pe.wait_ge(weights_loaded, 16 * len(k["loads"]))
            pe.wait_ge(c["const_step"], CONSTANTS)

            def job(n, u, index, b, is_p, a):
                work_of, _, waits_for_last = (project_jobs if is_p else finish_jobs)[a]
                if waits_for_last:
                    pe.wait_ge(job_read, index)
                elif not (isinstance(index, int) and index < 2):
                    pe.wait_ge(job_read, index - 1)
                if is_p and a == 0:
                    pe.wait_ge(rows_ready, n + 1)
                if not is_p and a == 0:
                    for s in range(2):
                        pe.wait_ge(heads_read[s], (n + 1) * (STEPS // 2))
                work_of(pe, work[b], u).then_inc(job_made, 1)

            def weigh(n, u, j):
                s = j % 2
                half, h0, nh = ATT_CHUNKS[j]
                use = n * 3 + j // 2
                pe.wait_ge(attT_ready[s], use + 1)
                if not (isinstance(n, int) and n == 0 and j < 2):
                    pe.wait_ge(heads_read[s], use)
                for a in range(nh):
                    h = k["head_at"](h0, nh, a)
                    for kb in range(half + 1):
                        col = (a * (half + 1) + kb) * P
                        last = pe.matmul(heads[s][:, a * HDIM:(a + 1) * HDIM], attT[s][:, col:col + P],
                                         k["v"](u, kb, h), start=(kb == 0), stop=(kb == half),
                                         skip_group_check=True)
                last.then_inc(heads_made[s], 1)

            def score(n, u, j):
                s = j % 2
                half, h0, nh = ATT_CHUNKS[j]
                keys = (half + 1) * P
                if j == 0:
                    pe.wait_ge(job_read, projected(n))
                for a in range(nh):
                    h = k["head_at"](h0, nh, a)
                    q, kk = k["qk"](u, half, h, keys)
                    pe.matmul(scores[s][:, a * keys:(a + 1) * keys], q, kk, start=(a * keys % 512 == 0), stop=False,
                              skip_group_check=True)
                for b in range(2):
                    out = scores[s][:, b * 512:(b + 1) * 512].rearrange("p (h k) -> p h k", k=keys)
                    last = pe.matmul(out[:, :, keys - P:keys], c["minus_ident_bf"][:, :],
                                     broadcast_middle(c["far_mask"][:, :], 512 // keys),
                                     start=False, stop=True, skip_group_check=True)
                last.then_inc(scored[s], 1)

            def turn(n, j):
                s = j % 2
                pe.wait_ge(att_ready[s], n * 3 + j // 2 + 1)
                for b in range(8):
                    last = pe.transpose(scores[s][:, b * P:(b + 1) * P], att[s][:, b * P:(b + 1) * P], c["ident"][:, :])
                last.then_inc(turned[s], 1)

            def body(n, u, first=False, last=False):
                for j in range(STEPS):
                    if j >= 2:
                        weigh(n, u, j - 2)
                    elif not first:
                        weigh(n - 1, 1 - u, j + STEPS - 2)
                    score(n, u, j)
                    if j >= 1:
                        turn(n, j - 1)
                    elif not first:
                        turn(n - 1, STEPS - 1)
                    run_step(n, u, j, first, last, job)
                if last:
                    weigh(n, u, STEPS - 2)
                    turn(n, STEPS - 1)
                    weigh(n, u, STEPS - 1)
                    run_tail(job)

            for a in range(NP):
                job(0, 0, a, a % 2, True, a)
            bodies(pe, body)

        @block.scalar
        def _(act):
            def exponentials(n, j):
                s = j % 2
                half, h0, nh = ATT_CHUNKS[j]
                keys = (half + 1) * P
                act.wait_ge(peak_ready[s], n * 3 + j // 2 + 1)
                for a in range(nh):
                    last = act.activation(att[s][:, a * keys:(a + 1) * keys], scores[s][:, a * keys:(a + 1) * keys],
                                          ACT.Exp, bias=peak[s][:, a:a + 1], accum_out=total[s][:, a:a + 1])
                last.then_inc(att_ready[s], 1)

            def copy(n, j):
                s = j % 2
                act.wait_ge(turned[s], n * 3 + j // 2 + 1)
                act.activation(attT[s][:, :], scores[s][:, :], ACT.Copy).then_inc(attT_ready[s], 1)

            def body(n, u, first=False, last=False):
                for j in range(STEPS):
                    exponentials(n, j)
                    if j >= 1:
                        copy(n, j - 1)
                    elif not first:
                        copy(n - 1, STEPS - 1)
                if last:
                    copy(n, STEPS - 1)

            bodies(act, body)

        @block.vector
        def _(dve):
            dve.wait_ge(weights_loaded, 16 * len(k["loads"]))
            dve.wait_ge(c["const_step"], CONSTANTS)

            def normalise_rows(n, u):
                for t in range(2):
                    tile = n * 2 + t
                    last = dve.tensor_scalar(rows[u][:, t, :], X[:, bass.ds(tile, 1), :].squeeze(1),
                                             centre[:, bass.ds(tile, 1), 0], scale[:, bass.ds(tile, 1)],
                                             ALU.subtract, ALU.mult)
                    if second_scale is not None:
                        last = dve.tensor_scalar(lean_rows[u][:, t, :], X[:, bass.ds(tile, 1), :].squeeze(1),
                                                 centre[:, bass.ds(tile, 1), 0], second_scale[:, bass.ds(tile, 1)],
                                                 ALU.subtract, ALU.mult)
                last.then_inc(rows_ready, 1)

            def job(n, u, index, b, is_p, a):
                if not is_p and a == NF - 1:
                    residual(n, u, index, b)
                    return
                dve.wait_ge(job_made, index + 1)
                (project_jobs if is_p else finish_jobs)[a][1](dve, work[b], u).then_inc(job_read, 1)

            def residual(n, u, index, b):
                dve.wait_ge(job_made, index + 1)
                dve.wait_ge(rows_kept, n + 1)
                pair = bass.ds(n * 2, 2)
                attended = work[b][:, 0:2 * D].rearrange("p (t d) -> p t d", t=2)
                dve.tensor_tensor(total_rows[:, :, :], attended, kept[:, pair, :], ALU.add).then_inc(ln_step, 1)
                dve.tensor_tensor(X[:, pair, :], attended, kept[:, pair, :], ALU.add).then_inc(job_read, 1)
                tile_statistics(dve, total_rows, lnst, agg, c["carrier"], stats, n, ln_step)

            def peaks(n, j):
                s = j % 2
                half, h0, nh = ATT_CHUNKS[j]
                dve.wait_ge(scored[s], n * 3 + j // 2 + 1)
                dve.tensor_reduce(peak[s][:, 0:nh], scores[s][:, :].rearrange("p (h k) -> p h k", h=nh), AX.X,
                                  ALU.max, negate=True).then_inc(peak_ready[s], 1)

            def sums(n, j):
                s = j % 2
                nh = ATT_CHUNKS[j][2]
                dve.wait_ge(att_ready[s], n * 3 + j // 2 + 1)
                dve.reciprocal(rinv[s][:, 0:nh], total[s][:, 0:nh]).then_inc(rinv_ready[s], 1)

            def normalise_heads(n, u, j):
                s = j % 2
                half, h0, nh = ATT_CHUNKS[j]
                dve.wait_ge(heads_made[s], n * 3 + j // 2 + 1)
                dve.wait_ge(rinv_ready[s], n * 3 + j // 2 + 1)
                for out, first_at, count in k["o"](u, half, h0, nh):
                    last = dve.tensor_tensor(out, heads[s][:, first_at * HDIM:(first_at + count) * HDIM]
                                             .rearrange("p (h d) -> p h d", d=HDIM),
                                             broadcast_last(rinv[s][:, first_at:first_at + count], HDIM), ALU.mult)
                last.then_inc(heads_read[s], 1)

            def body(n, u, first=False, last=False):
                for j in range(STEPS):
                    if j >= 2:
                        normalise_heads(n, u, j - 2)
                    elif not first:
                        normalise_heads(n - 1, 1 - u, j + STEPS - 2)
                    peaks(n, j)
                    if j >= 1:
                        sums(n, j - 1)
                    elif not first:
                        sums(n - 1, STEPS - 1)
                    if j == 0 and not last:
                        if not first:
                            dve.wait_ge(rows_kept, n)
                        normalise_rows(n + 1, 1 - u)
                    run_step(n, u, j, first, last, job)
                if last:
                    normalise_heads(n, u, STEPS - 2)
                    sums(n, STEPS - 1)
                    normalise_heads(n, u, STEPS - 1)
                    run_tail(job)

            normalise_rows(0, 0)
            for a in range(NP):
                job(0, 0, a, a % 2, True, a)
            bodies(dve, body)


def gqa(dram):
    HQ, HKV, HD = 16, 4, 64
    PAIRS = HQ * HD // P

    def kind(sb, c, rows):
        wq = sb("wq", [P, HQ * HD])
        wk = sb("wk", [P, HKV, 2, HD])
        wv = sb("wv", [P, HKV * HD])
        wo = sb("wo", [P, PAIRS, D])
        xT = sb("xT", [P, N])
        qT = [sb(f"qT{u}", [P, PAIRS, N]) for u in range(2)]
        kT = [sb(f"kT{u}", [P, HKV, N]) for u in range(2)]
        v = [sb(f"v{u}", [P, 2, HKV * HD]) for u in range(2)]
        o = [sb(f"o{u}", [P, 2, HQ, HD]) for u in range(2)]
        oT = sb("oT", [P, PAIRS, N])

        def halves(w):
            return w[:, :].rearrange("p (t n) -> p t n", t=2)

        def turn_rows(pe, w, u):
            for t in range(2):
                last = pe.transpose(w[:, t * P:(t + 1) * P], rows[u][:, t, :], c["ident"][:, :])
            return last

        def make_q(b):
            def pe_part(pe, w, u):
                for j in range(2):
                    last = pe.matmul(w[:, j * N:(j + 1) * N], wq[:, (2 * b + j) * P:(2 * b + j + 1) * P], xT[:, :],
                                     start=True, stop=True)
                return last
            return pe_part, lambda dve, w, u: dve.tensor_scalar(qT[u][:, 2 * b:2 * b + 2, :], halves(w),
                                                                float(HD) ** -0.5, None, ALU.mult), b == 0

        def make_k(b):
            def pe_part(pe, w, u):
                for j in range(2):
                    last = pe.matmul(w[:, j * N:(j + 1) * N], wk[:, 2 * b + j, :, :].rearrange("p t d -> p (t d)"),
                                     xT[:, :], start=True, stop=True)
                return last
            return pe_part, lambda dve, w, u: dve.tensor_copy(kT[u][:, 2 * b:2 * b + 2, :], halves(w)), False

        def make_v(pe, w, u):
            for t in range(2):
                last = pe.matmul(w[:, t * HKV * HD:(t + 1) * HKV * HD], xT[:, t * P:(t + 1) * P], wv[:, :],
                                 start=True, stop=True)
            return last

        def turn_heads(i):
            t, b = divmod(i, 2)

            def pe_part(pe, w, u):
                flat = o[u][:, t, :, :].rearrange("p h d -> p (h d)")
                for j in range(4):
                    last = pe.transpose(w[:, j * P:(j + 1) * P], flat[:, (4 * b + j) * P:(4 * b + j + 1) * P],
                                        c["ident"][:, :])
                return last
            return pe_part, lambda dve, w, u: dve.tensor_copy(
                oT[:, 4 * b:4 * b + 4, t * P:(t + 1) * P], w[:, :].rearrange("p (j q) -> p j q", j=4)), False

        def project_out(pe, w, u):
            for t in range(2):
                for b in range(PAIRS):
                    last = pe.matmul(w[:, t * D:(t + 1) * D], oT[:, b, t * P:(t + 1) * P], wo[:, b, :],
                                     start=(b == 0), stop=(b == PAIRS - 1), skip_group_check=True)
            return last

        def where(u, half, h0, nh):
            for r in range(2):
                yield o[u][:, half, h0 + r:h0 + nh:2, :], r * nh // 2, nh // 2

        return {
            "loads": [(wq[:, :], dram["Wq"]), (wk[:, :, 0, :], dram["Wk"].rearrange("p (h d) -> p h d", d=HD)),
                      (wk[:, :, 1, :], dram["Wk"].rearrange("p (h d) -> p h d", d=HD)), (wv[:, :], dram["Wv"]),
                      (wo[:, :, :], dram["Wo"].rearrange("(b p) d -> p b d", p=P))],
            "head_dim": HD,
            "head_at": lambda h0, nh, a: h0 + 2 * (a % (nh // 2)) + a // (nh // 2),
            "qk": lambda u, half, h, keys: (qT[u][64 * (h % 2):64 * (h % 2) + 64, h // 2, half * P:(half + 1) * P],
                                            kT[u][64 * (h % 2):64 * (h % 2) + 64, h // 4, 0:keys]),
            "v": lambda u, kb, h: v[u][:, kb, (h // 4) * HD:(h // 4 + 1) * HD],
            "o": where,
            "project": [(turn_rows, lambda dve, w, u: dve.tensor_copy(xT[:, :], w[:, 0:N]), False)]
            + [make_q(b) for b in range(4)] + [make_k(b) for b in range(2)]
            + [(make_v, lambda dve, w, u: dve.tensor_copy(v[u][:, :, :], halves(w)), False)],
            "project_steps": [0, 0, 0, 1, 1, 1, 2, 2],
            "finish": [turn_heads(i) for i in range(4)] + [(project_out, None, True)],
            "finish_steps": [3, 3, 4, 4, 5],
        }
    return kind


def latent(dram):
    LATENT = 64

    def kind(sb, c, rows):
        wq = sb("wq", [P, D])
        wdown = sb("wdown", [P, LATENT])
        wuk = sb("wuk", [LATENT, D])
        wuv = sb("wuv", [LATENT, D])
        wo = sb("wo", [P, D])
        gain = sb("gain", [P, 1])
        hT = sb("hT", [P, N])
        cT = sb("cT", [LATENT, N])
        qT = [sb(f"qT{u}", [P, N]) for u in range(2)]
        kM = [sb(f"kM{u}", [P, 4, N]) for u in range(2)]
        v = [sb(f"v{u}", [P, 2, D]) for u in range(2)]
        o = [sb(f"o{u}", [P, 2, H, DH]) for u in range(2)]
        oT = sb("oT", [P, N])

        def turn(source):
            def pe_part(pe, w, u):
                for t in range(2):
                    last = pe.transpose(w[:, t * P:(t + 1) * P], source(u, t), c["ident"][:, :])
                return last
            return pe_part

        def make_q_latent(pe, w, u):
            pe.matmul(w[:, 0:N], wq[:, :], hT[:, :], start=True, stop=True)
            return pe.matmul(w[0:LATENT, N:2 * N], wdown[:, :], hT[:, :], start=True, stop=True)

        def take_q_latent(dve, w, u):
            dve.tensor_scalar(qT[u][:, :], w[:, 0:N], float(DH) ** -0.5, None, ALU.mult)
            return dve.tensor_copy(cT[:, :], w[0:LATENT, N:2 * N])

        def make_kv(pe, w, u):
            pe.matmul(w[:, 0:N], wuk[:, :], cT[:, :], start=True, stop=True)
            for t in range(2):
                last = pe.matmul(w[:, N + t * D:N + (t + 1) * D], cT[:, t * P:(t + 1) * P], wuv[:, :],
                                 start=True, stop=True)
            return last

        def take_kv(dve, w, u):
            for m in range(4):
                dve.tensor_scalar(kM[u][:, m, :], w[:, 0:N], c["row_mask"][:, m:m + 1], None, ALU.mult)
            return dve.tensor_copy(v[u][:, :, :], w[:, N:2 * N].rearrange("p (t d) -> p t d", t=2))

        def project_out(pe, w, u):
            for t in range(2):
                last = pe.matmul(w[:, t * D:(t + 1) * D], oT[:, t * P:(t + 1) * P], wo[:, :], start=True, stop=True)
            return last

        return {
            "loads": [(wq[:, :], dram["Wq"]), (wdown[:, :], dram["Wdkv"]), (wuk[:, :], dram["Wuk"]),
                      (wuv[:, :], dram["Wuv"]), (wo[:, :], dram["Wo"]), (gain[:, :], dram["g1"])],
            "head_dim": DH,
            "head_at": lambda h0, nh, a: h0 + a,
            "qk": lambda u, half, h, keys: (qT[u][32 * (h // 4):32 * (h // 4) + 32, half * P:(half + 1) * P],
                                            kM[u][32 * (h // 4):32 * (h // 4) + 32, h % 4, 0:keys]),
            "v": lambda u, kb, h: v[u][:, kb, h * DH:(h + 1) * DH],
            "o": lambda u, half, h0, nh: [(o[u][:, half, h0:h0 + nh, :], 0, nh)],
            "project": [(turn(lambda u, t: rows[u][:, t, :]),
                         lambda dve, w, u: dve.tensor_scalar(hT[:, :], w[:, 0:N], gain[:, 0:1], None, ALU.mult), False),
                        (make_q_latent, take_q_latent, True), (make_kv, take_kv, True)],
            "project_steps": [0, 1, 2],
            "finish": [(turn(lambda u, t: o[u][:, t, :, :].rearrange("p h d -> p (h d)")),
                        lambda dve, w, u: dve.tensor_copy(oT[:, :], w[:, 0:N]), False),
                       (project_out, None, True)],
            "finish_steps": [3, 4],
        }
    return kind



E2 = 8
F2 = 256
SPAN = 512
SPAN_TILES = SPAN // P


def choose_two(nc, ctx, sems, logits, share):
    T = TILES

    def sb(name, shape):
        return ctx.enter_context(nc.sbuf_tensor("c2_" + name, shape, F32))

    first = sb("first", [P, T])
    second = sb("second", [P, T])
    rank = sb("rank", [P, T])
    eq = sb("eq", [P, T, E2])
    rest = sb("rest", [P, T, E2])
    hot1 = sb("hot1", [P, T, E2])
    hot2 = sb("hot2", [P, T, E2])
    early = sb("early", [P, E2])
    gap = sb("gap", [P, T])
    ratio = sb("ratio", [P, T])
    one = sb("one", [P, T])
    g1 = sb("g1", [P, T])
    early_ready = sems("c2_early_ready")
    gap_ready = sems("c2_gap_ready")
    ratio_ready = sems("c2_ratio_ready")
    step = sems("c2_step")

    with nc.Block() as block:

        @block.gpsimd
        def _(pool):
            pool.iota(early[:, :], pattern=[[-1, E2]], base=E2, channel_multiplier=0,
                      allow_small_or_imprecise_dtypes=True).then_inc(early_ready, 1)

        @block.scalar
        def _(act):
            act.wait_ge(gap_ready, 1)
            act.activation(ratio[:, :], gap[:, :], ACT.Exp).then_inc(ratio_ready, 1)

        @block.vector
        def _(dve):
            n = [0]

            def settle(ins):
                n[0] += 1
                ins.then_inc(step, 1)
                dve.wait_ge(step, n[0])

            by_tile = lambda t: broadcast_last(t[:, :], E2)

            def largest(values, top, hot):
                settle(dve.tensor_reduce(top[:, :], values[:, :, :], AX.X, ALU.max))
                settle(dve.tensor_tensor(eq[:, :, :], values[:, :, :], by_tile(top), ALU.is_equal))
                settle(dve.tensor_tensor(eq[:, :, :], eq[:, :, :], broadcast_middle(early[:, :], T), ALU.mult))
                settle(dve.tensor_reduce(rank[:, :], eq[:, :, :], AX.X, ALU.max))
                settle(dve.tensor_tensor(hot[:, :, :], eq[:, :, :], by_tile(rank), ALU.is_equal))

            dve.wait_ge(early_ready, 1)
            largest(logits, first, hot1)
            settle(dve.tensor_scalar(rest[:, :, :], hot1[:, :, :], -3e38, None, ALU.mult))
            settle(dve.tensor_tensor(rest[:, :, :], rest[:, :, :], logits[:, :, :], ALU.add))
            largest(rest, second, hot2)
            dve.tensor_tensor(gap[:, :], second[:, :], first[:, :], ALU.subtract).then_inc(gap_ready, 1)
            dve.wait_ge(ratio_ready, 1)
            settle(dve.tensor_scalar(one[:, :], ratio[:, :], 1.0, None, ALU.add))
            settle(dve.reciprocal(g1[:, :], one[:, :]))
            settle(dve.tensor_tensor(ratio[:, :], ratio[:, :], g1[:, :], ALU.mult))
            settle(dve.tensor_tensor(hot1[:, :, :], hot1[:, :, :], by_tile(g1), ALU.mult))
            settle(dve.tensor_tensor(hot2[:, :, :], hot2[:, :, :], by_tile(ratio), ALU.mult))
            dve.tensor_tensor(share[:, :, :], hot1[:, :, :], hot2[:, :, :], ALU.add)


def stage5(nc, ctx, sems, dram, X, rows3, hT_all, share, stats, c):
    def sb(name, shape, dt=F32):
        return ctx.enter_context(nc.sbuf_tensor("s5_" + name, shape, dt))

    def ps(name, shape):
        return ctx.enter_context(nc.psum_tensor("s5_" + name, shape, F32))

    FB = F2 // P
    SPANS = B * N // SPAN
    w1 = sb("w1", [P, E2, F2])
    w2 = sb("w2", [P, E2, FB, D])
    hid = [sb(f"hid{v}", [P, FB, SPAN]) for v in range(2)]
    acc = [sb(f"acc{v}", [P, SPAN_TILES, D]) for v in range(2)]
    part = sb("part", [P, SPAN_TILES, E2])
    lnst = sb("lnst", [P, SPAN_TILES, 6])
    agg = sb("agg", [P, SPAN_TILES, 2])
    summed = sems("s5_summed")
    hid_ps = [ps(f"hid_ps{v}", [P, FB, SPAN]) for v in range(2)]
    out_ps = [ps(f"out_ps{v}", [P, SPAN_TILES, D]) for v in range(2)]
    loaded = sems("s5_loaded")
    hid_made = sems("s5_hid_made")
    hid_ready = sems("s5_hid_ready")
    out_made = sems("s5_out_made")
    out_read = sems("s5_out_read")
    step = sems("s5_step")

    def spans(eng, body):
        body(0)
        with eng.Fori(1, SPANS) as i:
            body(i)

    with nc.Block() as block:

        @block.sync
        def _(sp):
            sp.dma_start(w1[:, :, :], dram["w1"].rearrange("e d f -> d e f")).then_inc(loaded, 16)
            sp.dma_start(w2[:, :, :, :], dram["w2"].rearrange("e (b p) d -> p e b d", p=P)).then_inc(loaded, 16)

        @block.tensor
        def _(pe):
            pe.wait_ge(loaded, 32)

            def up(i, e, start):
                v = e % 2
                k = i * E2 + e
                if not start:
                    pe.wait_ge(hid_ready, k - 1)
                for b in range(FB):
                    last = pe.matmul(hid_ps[v][:, b, :], w1[:, e, b * P:(b + 1) * P], hT_all[:, bass.ds(i * SPAN, SPAN)],
                                     start=True, stop=True)
                last.then_inc(hid_made, 1)

            def down(i, e, start):
                v = e % 2
                k = i * E2 + e
                pe.wait_ge(hid_ready, k + 1)
                if not start:
                    pe.wait_ge(out_read, k - 1)
                for t in range(SPAN_TILES):
                    for b in range(FB):
                        last = pe.matmul(out_ps[v][:, t, :], hid[v][:, b, t * P:(t + 1) * P], w2[:, e, b, :],
                                         start=(b == 0), stop=(b == FB - 1), skip_group_check=True)
                last.then_inc(out_made, 1)

            def body(i):
                start = isinstance(i, int)
                for e in range(E2):
                    up(i, e, start and e < 2)
                    if e:
                        down(i, e - 1, start and e < 3)
                    elif not start:
                        down(i - 1, E2 - 1, False)

            spans(pe, body)
            down(SPANS - 1, E2 - 1, False)

        @block.scalar
        def _(act):
            def body(i):
                for e in range(E2):
                    k = i * E2 + e
                    act.wait_ge(hid_made, k + 1)
                    if not (isinstance(i, int) and e < 2):
                        act.wait_ge(out_made, k - 1)
                    act.activation(hid[e % 2][:, :, :], hid_ps[e % 2][:, :, :], ACT.Silu).then_inc(hid_ready, 1)

            spans(act, body)

        @block.vector
        def _(dve):
            def body(i):
                X4 = X[:, bass.ds(i * SPAN_TILES, SPAN_TILES), :]
                dve.tensor_copy(part[:, :, :], share[:, bass.ds(i * SPAN_TILES, SPAN_TILES), :])
                dve.tensor_tensor(acc[1][:, :, :], X4, rows3[:, bass.ds(i * SPAN_TILES, SPAN_TILES), :], ALU.add)\
                    .then_inc(summed, 1)
                dve.wait_ge(summed, i + 1)
                for e in range(E2):
                    k = i * E2 + e
                    dve.wait_ge(out_made, k + 1)
                    for t in range(SPAN_TILES):
                        last = dve.scalar_tensor_tensor(acc[e % 2][:, t, :], out_ps[e % 2][:, t, :], part[:, t, e:e + 1],
                                                        acc[1 - e % 2][:, t, :], ALU.mult, ALU.add)
                    last.then_inc(out_read, 1)
                    dve.wait_ge(out_read, k + 1)
                dve.tensor_scalar(X4, acc[1][:, :, :], 1.0, None, ALU.mult).then_inc(step, 1)
                tile_statistics(dve, acc[1], lnst, agg, c["carrier"], stats, i, step)

            spans(dve, body)


def last_norm(nc, ctx, sems, X, stats, rstd, out):
    CHUNK = 8
    made = sems("ln_made")
    stored = sems("stored")
    view = out.rearrange("b (t p) d -> p (b t) d", p=P)
    with nc.Block() as block:

        @block.vector
        def _(dve):
            for t in range(TILES):
                last = dve.tensor_scalar(X[:, t, :], X[:, t, :], stats[:, t, 0:1], rstd[:, t:t + 1],
                                         ALU.subtract, ALU.mult)
                if t % CHUNK == CHUNK - 1:
                    last.then_inc(made, 1)

        @block.sync
        def _(sp):
            for k in range(TILES // CHUNK):
                sp.wait_ge(made, k + 1)
                sp.dma_start(view[:, k * CHUNK:(k + 1) * CHUNK, :], X[:, k * CHUNK:(k + 1) * CHUNK, :])\
                    .then_inc(stored, 16)
            sp.wait_ge(stored, 16 * (TILES // CHUNK))



def build(nc, dram):
    with ExitStack() as ctx:
        def sems(name):
            return ctx.enter_context(nc.semaphore(name))

        def sb(name, shape):
            return ctx.enter_context(nc.sbuf_tensor(name, shape, F32))

        c = constants(nc, ctx, sems)
        c["const_step"] = sems("const_step")
        X = sb("X", [P, TILES, D])
        stats = sb("stats", [P, TILES, 2])
        rstd = sb("rstd", [P, TILES])
        rms = sb("rms", [P, TILES])
        both = sb("both", [P, TILES])
        logits = sb("logits", [P, TILES, E1])
        share = sb("share", [P, TILES, E2])
        rows3 = sb("rows3", [P, TILES, D])
        if "slots" not in dram:
            for name in ("slots", "done"):
                dram[name] = nc.dram_tensor(name, (E1 * CAP, D), F32, kind="Internal").ap()

        def variance(dve, out):
            yield dve.tensor_copy(out[:, :], stats[:, :, 1])

        def square_of_rows(dve, out):
            yield dve.tensor_tensor(out[:, :], rstd[:, :], rstd[:, :], ALU.mult)
            yield dve.tensor_tensor(out[:, :], out[:, :], stats[:, :, 1], ALU.mult)

        def mean_square(dve, out):
            yield dve.tensor_tensor(out[:, :], stats[:, :, 0], stats[:, :, 0], ALU.mult)
            yield dve.tensor_tensor(out[:, :], out[:, :], stats[:, :, 1], ALU.add)

        norm = (variance, rstd, LN_EPS)
        with ExitStack() as inner:
            zero_slots(nc, inner, sems, dram, c)
        with ExitStack() as inner:
            stage1(nc, inner, sems, dram, X, stats, c)
        with ExitStack() as inner:
            inverse_roots(nc, inner, sems, "norm1", [norm])
        with ExitStack() as inner:
            router(nc, inner, sems, "route1", X, stats, rstd, None, True, None, dram["L0_ffn_Wr"], logits, c)
        with ExitStack() as inner:
            stage2(nc, inner, sems, dram, X, stats, logits, c)
        with ExitStack() as inner:
            inverse_roots(nc, inner, sems, "norm2", [norm])
        with ExitStack() as inner:
            softmax_stage(nc, inner, sems, "gqa", X, X, stats, rstd, None, stats, c, gqa(dram["gqa"]))
        with ExitStack() as inner:
            inverse_roots(nc, inner, sems, "norm3", [norm, (square_of_rows, rms, RMS_EPS)])
        with nc.Block() as block:

            @block.vector
            def _(dve):
                dve.tensor_tensor(both[:, :], rstd[:, :], rms[:, :], ALU.mult)

        with ExitStack() as inner:
            softmax_stage(nc, inner, sems, "mla", X, rows3, stats, rstd, both, stats, c, latent(dram["mla"]))
        with ExitStack() as outer:
            hT_all = outer.enter_context(nc.sbuf_tensor("hT_all", [P, B * N], F32))
            with ExitStack() as inner:
                inverse_roots(nc, inner, sems, "norm4", [(mean_square, rms, RMS_EPS)])
            with ExitStack() as inner:
                router(nc, inner, sems, "route2", X, None, rms, dram["g2"], False, hT_all, dram["gate_w"], logits, c)
            with ExitStack() as inner:
                choose_two(nc, inner, sems, logits, share)
            with ExitStack() as inner:
                stage5(nc, inner, sems, dram, X, rows3, hT_all, share, stats, c)
        with ExitStack() as inner:
            inverse_roots(nc, inner, sems, "norm5", [norm])
        with ExitStack() as inner:
            last_norm(nc, inner, sems, X, stats, rstd, dram["out"])


def named(given):
    return given | {
        "WqkvT": given["L0_attn_Wqkv"], "WoT": given["L0_attn_Wo"], "g2": given["L1_ffn_g2"],
        "gate_w": given["L1_ffn_gate_w"], "w1": given["L1_ffn_w1"], "w2": given["L1_ffn_w2"],
        "gqa": {n: given["L1_attn_" + n] for n in ("Wq", "Wk", "Wv", "Wo")},
        "mla": {n: given["L1_ffn_" + n] for n in ("Wq", "Wdkv", "Wuk", "Wuv", "Wo", "g1")},
    }


_NAMES = ["L0_attn_x", "L0_attn_Wqkv", "L0_attn_Wo", "L0_ffn_Wr", "L0_ffn_W1", "L0_ffn_W2", "L1_attn_Wq", "L1_attn_Wk",
          "L1_attn_Wv", "L1_attn_Wo", "L1_ffn_g1", "L1_ffn_Wq", "L1_ffn_Wdkv", "L1_ffn_Wuk", "L1_ffn_Wuv", "L1_ffn_Wo",
          "L1_ffn_g2", "L1_ffn_gate_w", "L1_ffn_w1", "L1_ffn_w2"]


def kernel(**inputs):
    import concourse.bacc as _bacc
    from concourse.bass_utils import run_bass_kernel_spmd as _run

    nc = _bacc.Bacc("TRN2", target_bir_lowering=False, num_devices=1)
    arrays, given = {}, {}
    for name in _NAMES:
        a = np.asarray(inputs[name])
        if name in ("L0_attn_Wqkv", "L0_attn_Wo"):
            a = a.T
        if name in ("L1_ffn_g1", "L1_ffn_g2"):
            a = a.reshape(D, 1)
        a = np.ascontiguousarray(a)
        arrays[f"in_{name}"] = a
        given[name] = nc.dram_tensor(f"in_{name}", a.shape, mybir.dt.from_np(a.dtype), kind="ExternalInput").ap()
    given["out"] = nc.dram_tensor("out_0", (B, N, D), F32, kind="ExternalOutput").ap()
    build(nc, named(given))
    r = _run(nc, [arrays], core_ids=[0])
    return r.results[0]["out_0"]
```

```python
from contextlib import ExitStack

import numpy as np
import concourse.bass as bass
from concourse import mybir

F32 = mybir.dt.float32
BF16 = mybir.dt.bfloat16
F16 = mybir.dt.float16
I32 = mybir.dt.int32
U32 = mybir.dt.uint32
ALU = mybir.AluOpType
ACT = mybir.ActivationFunctionType
AX = mybir.AxisListType

P = 128
B, N, D = 32, 256, 128
TILES = B * N // P
H = 16
DH = D // H
LN_EPS = 1e-5
RMS_EPS = 1e-6


def broadcast_last(ap, n):
    return ap.unsqueeze(2).to_broadcast([ap.shape[0], ap.shape[1], n])


def broadcast_middle(ap, n):
    return ap.unsqueeze(1).to_broadcast([ap.shape[0], n, ap.shape[1]])


def constants(nc, ctx, sem):
    c = {}

    def sb(name, shape, dt):
        c[name] = ctx.enter_context(nc.sbuf_tensor(name, shape, dt))
        return c[name]

    sb("ident", [P, P], F32)
    sb("ident_bf", [P, P], BF16)
    sb("ident_h", [P, P], F16)
    sb("far_mask", [P, P], BF16)
    sb("row_mask", [P, 4], F32)
    sb("prefix", [P, P], F32)
    sb("ones", [P, P], F32)
    sb("carrier", [P, 1], F32)
    sb("minus_ident_bf", [P, P], BF16)
    return c


def make_constants(pool, c, const_step):
    n = 0
    for t, v in ((c["ident"], 0.0), (c["ident_bf"], 0.0), (c["ident_h"], 0.0), (c["far_mask"], 0.0),
                 (c["row_mask"], 1.0), (c["prefix"], 1.0), (c["ones"], 1.0), (c["minus_ident_bf"], 0.0)):
        pool.memset(t[:, :], v).then_inc(const_step, 1)
        n += 1
    pool.wait_ge(const_step, n)
    for t in (c["ident"], c["ident_bf"], c["ident_h"]):
        pool.affine_select(out=t[:, :], in_=t[:, :], compare_op=ALU.not_equal, fill=1.0, base=0,
                           pattern=[[-1, P]], channel_multiplier=1).then_inc(const_step, 1)
    pool.affine_select(out=c["minus_ident_bf"][:, :], in_=c["minus_ident_bf"][:, :], compare_op=ALU.not_equal,
                       fill=-1.0, base=0, pattern=[[-1, P]], channel_multiplier=1).then_inc(const_step, 1)
    pool.affine_select(out=c["far_mask"][:, :], in_=c["far_mask"][:, :], compare_op=ALU.is_ge, fill=1e28,
                       base=0, pattern=[[-1, P]], channel_multiplier=1).then_inc(const_step, 1)
    pool.affine_select(out=c["prefix"][:, :], in_=c["prefix"][:, :], compare_op=ALU.is_ge, fill=0.0,
                       base=0, pattern=[[1, P]], channel_multiplier=-1).then_inc(const_step, 1)
    n += 6
    rows = c["row_mask"]
    for g in range(4):
        part = rows[32 * g:32 * g + 32, :]
        pool.affine_select(out=part, in_=part, compare_op=ALU.is_ge, fill=0.0, base=0,
                           pattern=[[-8, 4]], channel_multiplier=1).then_inc(const_step, 1)
        n += 1
        pool.wait_ge(const_step, n)
        pool.affine_select(out=part, in_=part, compare_op=ALU.is_ge, fill=0.0, base=7,
                           pattern=[[8, 4]], channel_multiplier=-1).then_inc(const_step, 1)
        n += 1
    return n


CONSTANTS = 8 + 6 + 8


def tile_statistics(dve, rows, lnst, agg, carrier, stats, n, step):
    tiles = rows.shape[1]
    dve.wait_ge(step, n * 4 + 1)
    for t in range(tiles):
        last = dve.bn_stats(lnst[:, t, :], rows[:, t, :])
    last.then_inc(step, 1)
    dve.wait_ge(step, n * 4 + 2)
    dve.memset(carrier[:, :], 0.0)
    for t in range(tiles):
        last = dve.bn_aggr(agg[:, t, :], lnst[:, t, :])
    last.then_inc(step, 1)
    dve.wait_ge(step, n * 4 + 3)
    dve.tensor_scalar(stats[:, bass.ds(n * tiles, tiles), :], agg[:, :, :], 1.0, None, ALU.mult).then_inc(step, 1)



CHUNKS = [[(0, 0, 8), (1, 0, 4), (1, 4, 4)], [(0, 8, 8), (1, 8, 4), (1, 12, 4)]]
SLOTS, GROUPS = 3, 2
NEWTON = 4
LENGTH = NEWTON + 3
OFFSETS = (0, 2, 4)
STEPS1 = GROUPS * LENGTH
TURN_X, MAKE_QK, TURN_SUMS, PROJECT_OUT, MAKE_V = 1, 2, 4, 6, 7
NORMALISE = 5
BANK = 512


def standing(h):
    return h % 4 * 4 + h // 4


def slots_at(step):
    out = []
    for s in range(SLOTS):
        local = step - OFFSETS[s]
        back = 1 if local < 0 else 0
        g, phase = divmod(local + back * STEPS1, LENGTH)
        out.append((s, back, g, phase))
    return out


def stage1(nc, ctx, sems, dram, X, stats, c):
    def sb(name, shape, dt=F32):
        return ctx.enter_context(nc.sbuf_tensor("s1_" + name, shape, dt))

    def sem(name):
        return sems("s1_" + name)

    wqkv = sb("wqkv", [P, 3 * D])
    wo = sb("wo", [P, D])
    xin = [sb(f"xin{u}", [P, 2, D]) for u in range(2)]
    xres = [sb(f"xres{u}", [P, 2, D]) for u in range(2)]
    xT = sb("xT", [P, N])
    qT = [sb(f"qT{u}", [P, N]) for u in range(2)]
    kT = [sb(f"kT{u}", [P, N]) for u in range(2)]
    kM = [sb(f"kM{u}", [P, H, N]) for u in range(2)]
    vM = [sb(f"vM{u}", [P, 2, 4, 4 * (4 * DH + DH)]) for u in range(2)]
    root = [sb(f"root{s}", [P, 1024]) for s in range(SLOTS)]
    w = [sb(f"w{s}", [P, 1024]) for s in range(SLOTS)]
    wT = [sb(f"wT{s}", [P, 1024]) for s in range(SLOTS)]
    low = [sb(f"low{s}", [P, 8]) for s in range(SLOTS)]
    lam = [sb(f"lam{s}", [P, 8]) for s in range(SLOTS)]
    st = [sb(f"st{s}", [P, 8, 3]) for s in range(SLOTS)]
    sq = [sb(f"sq{s}", [P, 8]) for s in range(SLOTS)]
    s2 = [sb(f"s2{s}", [P, 8]) for s in range(SLOTS)]
    rs2 = [sb(f"rs2{s}", [P, 8]) for s in range(SLOTS)]
    step_at = [sb(f"step{s}", [P, 8]) for s in range(SLOTS)]
    step_hi = [sb(f"step_hi{s}", [P, 8], F16) for s in range(SLOTS)]
    step_lo = [sb(f"step_lo{s}", [P, 8], F16) for s in range(SLOTS)]
    rinv = [sb(f"rinv{u}", [P, 2, D]) for u in range(2)]
    rinvT = sb("rinvT", [P, N])
    oT = sb("oT", [P, N])
    total = sb("total", [P, 2, D])
    lnst = sb("lnst", [P, 2, 6])
    agg = sb("agg", [P, 2, 2])
    dist = [ctx.enter_context(nc.psum_tensor(f"s1_dist{s}", [P, 2 * BANK], F32)) for s in range(SLOTS)]
    work = ctx.enter_context(nc.psum_tensor("s1_work", [P, BANK], F32))
    heads_out = ctx.enter_context(nc.psum_tensor("s1_heads_out", [P, N], F32))

    def each_slot(name):
        return [sem(f"{name}{s}") for s in range(SLOTS)]

    weights_loaded = sem("weights_loaded")
    zeroed = sem("zeroed")
    x_loaded = [sem(f"x_loaded{u}") for u in range(2)]
    xres_loaded = [sem(f"xres_loaded{u}") for u in range(2)]
    x_turned = sem("x_turned")
    xT_ready = sem("xT_ready")
    qk_made = sem("qk_made")
    q_ready = sem("q_ready")
    k_ready = sem("k_ready")
    k_spread = [sem(f"k_spread{u}") for u in range(2)]
    v_made = sem("v_made")
    v_ready = sem("v_ready")
    scores_ready = each_slot("scores_ready")
    lam_ready = each_slot("lam_ready")
    step_ready = each_slot("step_ready")
    dist_ready = each_slot("dist_ready")
    root_ready = each_slot("root_ready")
    w0_ready = each_slot("w0_ready")
    w1_ready = each_slot("w1_ready")
    w_turned = each_slot("w_turned")
    wT_ready = each_slot("wT_ready")
    dve_step = each_slot("dve_step")
    sums_ready = sem("sums_ready")
    sums_turned = sem("sums_turned")
    rinvT_ready = sem("rinvT_ready")
    heads_made = sem("heads_made")
    o_ready = sem("o_ready")
    out_made = sem("out_made")
    added = sem("added")
    ln_step = sem("ln_step")

    CHUNK_STEPS = 1 + 5 * NEWTON + 2

    def keys_of(g, s):
        return (CHUNKS[g][s][0] + 1) * P

    def per_head(ap, keys):
        return ap.rearrange("p (h k) -> p h k", k=keys)

    def paired(ap, keys):
        return ap.rearrange("p (a k t) -> p a t k", k=keys, t=2)

    def unpaired(ap, keys):
        return ap.rearrange("p (a t k) -> p a t k", k=keys, t=2)

    def bodies(eng, body):
        body(0, 0, 0, True, False)
        body(1, 1, 0, False, False)
        with eng.Fori(1, B // 2 - 1) as i:
            body(i * 2, 0, i, False, False)
            body(i * 2 + 1, 1, i, False, False)
        body(B - 2, 0, B // 2 - 1, False, False)
        body(B - 1, 1, B // 2 - 1, False, True)
        body(B, 0, B // 2, False, True)

    def active(n, u, step, first):
        for s, back, g, phase in slots_at(step):
            if (first and back) or (isinstance(n, int) and n == B and not back):
                continue
            m = n - back
            yield s, m * GROUPS + g, m, (u + back) % 2, g, phase

    def ended(n, step):
        return isinstance(n, int) and n == B and step > PROJECT_OUT

    with nc.Block() as block:

        @block.gpsimd
        def _(pool):
            for u in range(2):
                pool.memset(kM[u][:, :, :], 0.0)
                pool.memset(vM[u][:, :, :, :], 0.0).then_inc(zeroed, 1)

            def body(n, u, i, first, last):
                for step in range(STEPS1):
                    if ended(n, step):
                        break
                    for s, use, m, v, g, phase in active(n, u, step, first):
                        if 1 <= phase <= NEWTON + 1:
                            keys = keys_of(g, s)
                            r = unpaired(root[s][:, BANK:], keys)
                            pool.wait_ge(root_ready[s], (use * (NEWTON + 1) + phase) * 2 - 1)
                            pool.tensor_tensor(paired(w[s][:, BANK:], keys), r, r, ALU.mult).then_inc(w1_ready[s], 1)

            bodies(pool, body)

        @block.sync
        def _(sp):
            sp.dma_start(wqkv[:, :], dram["WqkvT"]).then_inc(weights_loaded, 16)
            sp.dma_start(wo[:, :], dram["WoT"]).then_inc(weights_loaded, 16)
            src = dram["L0_attn_x"].rearrange("b (t p) d -> b p t d", p=P)
            for u in range(2):
                sp.dma_start(xin[u][:, :, :], src[u]).then_inc(x_loaded[u], 16)
                sp.dma_start(xres[u][:, :, :], src[u]).then_inc(xres_loaded[u], 16)
            sp.wait_ge(zeroed, 2)

            def spread(n, u):
                sp.wait_ge(k_ready, n + 1)
                for h in range(H):
                    rows = slice(h * DH, (h + 1) * DH)
                    sp.dma_start(kM[u][rows, standing(h), :], kT[u][rows, :]).then_inc(k_spread[u], 16)

            def load(n, u):
                x = src[bass.ds(n, 1)].squeeze(0)
                sp.wait_ge(x_turned, n - 1)
                sp.dma_start(xin[u][:, :, :], x).then_inc(x_loaded[u], 16)

            def load_res(n, u):
                x = src[bass.ds(n, 1)].squeeze(0)
                sp.wait_ge(added, n - 1)
                sp.dma_start(xres[u][:, :, :], x).then_inc(xres_loaded[u], 16)

            spread(0, 0)
            load(2, 0)
            spread(1, 1)
            load(3, 1)
            with sp.Fori(1, B // 2 - 1) as i:
                for u in range(2):
                    spread(i * 2 + u, u)
                    load_res(i * 2 + u, u)
                    load(i * 2 + u + 2, u)
            for n in (B - 2, B - 1):
                spread(n, n % 2)
                load_res(n, n % 2)

        @block.tensor
        def _(pe):
            pe.wait_ge(weights_loaded, 32)

            def turn_x(n, u, loads):
                pe.wait_ge(x_loaded[u], loads * 16)
                if not (isinstance(n, int) and n == 0):
                    pe.wait_ge(v_ready, n)
                for t in range(2):
                    last = pe.transpose(work[:, t * P:(t + 1) * P], xin[u][:, t, :], c["ident"][:, :])
                last.then_inc(x_turned, 1)

            def make_qk(n):
                pe.wait_ge(xT_ready, n + 1)
                for j in range(2):
                    last = pe.matmul(work[:, j * N:(j + 1) * N], wqkv[:, j * D:(j + 1) * D], xT[:, :],
                                     start=True, stop=True)
                last.then_inc(qk_made, 1)

            def make_v(n, start):
                if start:
                    pe.wait_ge(q_ready, n + 1)
                    pe.wait_ge(k_ready, n + 1)
                else:
                    pe.wait_ge(added, n - 1)
                for t in range(2):
                    last = pe.matmul(work[:, t * D:(t + 1) * D], xT[:, t * P:(t + 1) * P], wqkv[:, 2 * D:],
                                     start=True, stop=True)
                last.then_inc(v_made, 1)

            def turn_sums(n, u, last_one):
                pe.wait_ge(sums_ready, (n + 1) * GROUPS * SLOTS)
                if not last_one:
                    pe.wait_ge(q_ready, n + 3)
                    pe.wait_ge(k_ready, n + 3)
                for t in range(2):
                    last = pe.transpose(work[:, t * P:(t + 1) * P], rinv[u][:, t, :], c["ident"][:, :])
                last.then_inc(sums_turned, 1)

            def project_out(n):
                pe.wait_ge(o_ready, n + 1)
                for t in range(2):
                    last = pe.matmul(work[:, t * D:(t + 1) * D], oT[:, t * P:(t + 1) * P], wo[:, :],
                                     start=True, stop=True)
                last.then_inc(out_made, 1)

            def weigh_values(n, u, g, s, use, start):
                half, h0, nh = CHUNKS[g][s]
                pe.wait_ge(wT_ready[s], use + 1)
                pe.wait_ge(v_ready, n + 1)
                begins = g == 0 and s == 0
                if begins and not start:
                    pe.wait_ge(o_ready, n)
                for kb in range(half + 1):
                    for a in range(nh):
                        m, group = divmod(h0 + a, 4)
                        col = (a * (half + 1) + kb) * P
                        last = pe.matmul(heads_out[32 * group:32 * group + 32, half * P:(half + 1) * P],
                                         vM[u][:, kb, group, 32 * m:32 * m + 32], wT[s][:, col:col + P],
                                         start=(begins and a < 4), stop=False, tile_position=(0, 32 * group),
                                         skip_group_check=True)
                if g == GROUPS - 1 and s == SLOTS - 1:
                    last.then_inc(heads_made, 1)

            def score(n, u, g, s, spreads):
                half, h0, nh = CHUNKS[g][s]
                keys = keys_of(g, s)
                pe.wait_ge(q_ready, n + 1)
                pe.wait_ge(k_spread[u], spreads * 16 * H)
                per = BANK // keys
                for bank in range(2):
                    pe.matmul(dist[s][:, bank * BANK:(bank + 1) * BANK], qT[u][:, half * P:(half + 1) * P],
                              kM[u][:, h0 + bank * per:h0 + (bank + 1) * per, 0:keys],
                              start=True, stop=False, skip_group_check=True)
                    out = per_head(dist[s][:, bank * BANK:(bank + 1) * BANK], keys)
                    last = pe.matmul(out[:, :, keys - P:keys], c["ident_bf"][:, :],
                                     broadcast_middle(c["far_mask"][:, :], per),
                                     start=False, stop=False, skip_group_check=True)
                last.then_inc(scores_ready[s], 1)

            def move(g, s, identity, parts):
                keys = keys_of(g, s)
                per = BANK // keys
                for bank in (1, 0):
                    out = per_head(dist[s][:, bank * BANK:(bank + 1) * BANK], keys)
                    for part in parts:
                        last = pe.matmul(out, identity[:, :], broadcast_last(part[:, bank * per:(bank + 1) * per], keys),
                                         start=False, stop=False, skip_group_check=True)
                    last.then_inc(dist_ready[s], 1)

            def body(n, u, i, first, last):
                for step in range(STEPS1):
                    if ended(n, step):
                        break
                    for s, use, m, v, g, phase in active(n, u, step, first):
                        if phase == 0:
                            if g:
                                weigh_values(m, v, 0, s, use - 1, first and m is n)
                            elif not first:
                                weigh_values(m - 1, 1 - v, 1, s, use - 1, False)
                            score(m, v, g, s, i if v != u and not u else i + 1)
                        elif phase == 1:
                            pe.wait_ge(lam_ready[s], use + 1)
                            move(g, s, c["ident"], [lam[s]])
                        elif phase <= NEWTON + 1:
                            pe.wait_ge(step_ready[s], use * NEWTON + phase - 1)
                            move(g, s, c["ident_h"], [step_hi[s], step_lo[s]])
                        else:
                            keys = keys_of(g, s)
                            pe.wait_ge(w0_ready[s], (use + 1) * (NEWTON + 1))
                            pe.wait_ge(w1_ready[s], (use + 1) * (NEWTON + 1))
                            wv = w[s][:, :].rearrange("p (a k t) -> p a t k", k=keys, t=2)
                            for b in range(8):
                                h, kb = divmod(b, keys // P)
                                last_one = pe.transpose(dist[s][:, b * P:(b + 1) * P],
                                                        wv[:, h // 2, h % 2, kb * P:(kb + 1) * P], c["ident"][:, :])
                            last_one.then_inc(w_turned[s], 1)
                    if isinstance(n, int) and n == B and step in [OFFSETS[s] for s in range(SLOTS)]:
                        s = OFFSETS.index(step)
                        weigh_values(B - 1, 1 - u, 1, s, B * GROUPS - 1, False)
                    if step == TURN_X and not last:
                        turn_x(n + 1, 1 - u, i + 1 + u)
                    if step == MAKE_QK and not last:
                        make_qk(n + 1)
                    if step == TURN_SUMS and not first:
                        turn_sums(n - 1, 1 - u, last)
                    if step == PROJECT_OUT and not first:
                        project_out(n - 1)
                    if step == MAKE_V and not last:
                        make_v(n + 1, first)

            turn_x(0, 0, 1)
            make_qk(0)
            make_v(0, True)
            bodies(pe, body)

        @block.scalar
        def _(act):
            act.wait_ge(zeroed, 2)

            def take_x(n):
                act.wait_ge(x_turned, n + 1)
                act.activation(xT[:, :], work[:, 0:N], ACT.Copy).then_inc(xT_ready, 1)

            def take_q(n, u):
                act.wait_ge(qk_made, n + 1)
                act.activation(qT[u][:, :], work[:, 0:N], ACT.Copy, scale=-float(DH) ** -0.5).then_inc(q_ready, 1)

            def take_v(n, u):
                act.wait_ge(v_made, n + 1)
                for t in range(2):
                    strips = vM[u][:, t, :, :].rearrange("p g (m c) -> p g m c", m=4)
                    last = act.activation(strips[:, :, :, 0:DH],
                                          work[:, t * D:(t + 1) * D].rearrange("p (g m d) -> p g m d", g=4, m=4),
                                          ACT.Copy)
                last.then_inc(v_ready, 1)

            def take_sums(n):
                act.wait_ge(sums_turned, n + 1)
                act.activation(rinvT[:, :], work[:, 0:N], ACT.Copy).then_inc(rinvT_ready, 1)

            def roots(k, s):
                for j, bank in enumerate((1, 0)):
                    act.wait_ge(dist_ready[s], k * 2 - 1 + j)
                    part = slice(bank * BANK, (bank + 1) * BANK)
                    act.activation(root[s][:, part], dist[s][:, part], ACT.Abs_reciprocal_sqrt)\
                        .then_inc(root_ready[s], 1)

            def square(k, s, keys):
                act.wait_ge(root_ready[s], k * 2)
                act.activation(paired(w[s][:, 0:BANK], keys), unpaired(root[s][:, 0:BANK], keys), ACT.Square)\
                    .then_inc(w0_ready[s], 1)

            def body(n, u, i, first, last):
                for step in range(STEPS1):
                    if ended(n, step):
                        break
                    for s, use, m, v, g, phase in active(n, u, step, first):
                        if 1 <= phase <= NEWTON + 1:
                            roots(use * (NEWTON + 1) + phase, s)
                            square(use * (NEWTON + 1) + phase, s, keys_of(g, s))
                        elif phase == LENGTH - 1:
                            act.wait_ge(w_turned[s], use + 1)
                            act.activation(wT[s][:, :], dist[s][:, :], ACT.Copy).then_inc(wT_ready[s], 1)
                    if step == TURN_X and not last:
                        take_x(n + 1)
                    if step == MAKE_QK and not last:
                        take_q(n + 1, 1 - u)
                    if step == TURN_SUMS and not first:
                        take_sums(n - 1)
                    if step == MAKE_V and not last:
                        take_v(n + 1, 1 - u)

            take_x(0)
            take_q(0, 0)
            take_v(0, 0)
            bodies(act, body)

        @block.vector
        def _(dve):
            def settle(s, use, count, ins):
                ins.then_inc(dve_step[s], 1)
                dve.wait_ge(dve_step[s], use * CHUNK_STEPS + count)

            def take_k(n, u):
                dve.wait_ge(q_ready, n + 1)
                dve.tensor_copy(kT[u][:, :], work[:, N:2 * N]).then_inc(k_ready, 1)

            def first_lambda(use, g, s):
                nh = CHUNKS[g][s][2]
                dve.wait_ge(scores_ready[s], use + 1)
                settle(s, use, 1, dve.tensor_reduce(low[s][:, 0:nh], per_head(dist[s][:, :], keys_of(g, s)),
                                                    AX.X, ALU.min))
                dve.tensor_scalar(lam[s][:, 0:nh], low[s][:, 0:nh], -1.0, 1.0, ALU.mult, ALU.add)\
                    .then_inc(lam_ready[s], 1)

            def moments(use, g, s, phase):
                keys = keys_of(g, s)
                pairs = BANK // (2 * keys)
                k = use * (NEWTON + 1) + phase
                for bank, ready in enumerate((w0_ready, w1_ready)):
                    for a in range(pairs):
                        if a == 0:
                            dve.wait_ge(ready[s], k)
                        at = bank * pairs + a
                        ins = dve.bn_stats(st[s][:, 2 * at:2 * at + 2, :].rearrange("p h c -> p (h c)"),
                                           w[s][:, at * 2 * keys:(at + 1) * 2 * keys])
                        yield ins

            def newton(use, g, s, phase):
                nh, keys = CHUNKS[g][s][2], keys_of(g, s)
                at = 1 + 5 * (phase - 1)
                mean, spread = st[s][:, 0:nh, 1], st[s][:, 0:nh, 2]
                dve.wait_ge(dve_step[s], use * CHUNK_STEPS + at + 1)
                dve.tensor_tensor(sq[s][:, 0:nh], mean, mean, ALU.mult).then_inc(dve_step[s], 1)
                yield
                dve.wait_ge(dve_step[s], use * CHUNK_STEPS + at + 2)
                dve.scalar_tensor_tensor(s2[s][:, 0:nh], spread, 1.0 / keys, sq[s][:, 0:nh], ALU.mult, ALU.add)\
                    .then_inc(dve_step[s], 1)
                yield
                dve.wait_ge(dve_step[s], use * CHUNK_STEPS + at + 3)
                dve.reciprocal(rs2[s][:, 0:nh], s2[s][:, 0:nh]).then_inc(dve_step[s], 1)
                yield
                dve.wait_ge(dve_step[s], use * CHUNK_STEPS + at + 4)
                dve.scalar_tensor_tensor(step_at[s][:, 0:nh], mean, -1.0 / keys, rs2[s][:, 0:nh], ALU.add, ALU.mult)
                dve.scalar_tensor_tensor(step_hi[s][:, 0:nh], mean, -1.0 / keys, rs2[s][:, 0:nh], ALU.add, ALU.mult)\
                    .then_inc(dve_step[s], 1)
                yield
                dve.wait_ge(dve_step[s], use * CHUNK_STEPS + at + 5)
                dve.tensor_tensor(step_lo[s][:, 0:nh], step_at[s][:, 0:nh], step_hi[s][:, 0:nh], ALU.subtract)\
                    .then_inc(step_ready[s], 1)

            def row_sums(use, g, s, phase, u):
                half, h0, nh = CHUNKS[g][s]
                at = 1 + 5 * NEWTON
                dve.wait_ge(dve_step[s], use * CHUNK_STEPS + at + 1)
                dve.reciprocal(rs2[s][:, 0:nh], st[s][:, 0:nh, 1]).then_inc(dve_step[s], 1)
                yield
                dve.wait_ge(dve_step[s], use * CHUNK_STEPS + at + 2)
                columns = rinv[u][:, half, :].rearrange("p (g m d) -> p m g d", g=4, m=4)
                for a in range(0, nh, 4):
                    last = dve.tensor_scalar(columns[:, (h0 + a) // 4, :, :], broadcast_last(rs2[s][:, a:a + 4], DH),
                                             1.0 / keys_of(g, s), None, ALU.mult)
                last.then_inc(sums_ready, 1)

            def normalise(n):
                dve.wait_ge(heads_made, n + 1)
                dve.wait_ge(rinvT_ready, n + 1)
                dve.tensor_tensor(oT[:, :], heads_out[:, :], rinvT[:, :], ALU.mult).then_inc(o_ready, 1)

            def add(n, u, loads):
                dve.wait_ge(out_made, n + 1)
                dve.wait_ge(xres_loaded[u], loads * 16)
                attended = work[:, 0:2 * D].rearrange("p (t d) -> p t d", t=2)
                dve.tensor_tensor(total[:, :, :], attended, xres[u][:, :, :], ALU.add).then_inc(ln_step, 1)
                dve.tensor_tensor(X[:, bass.ds(n * 2, 2), :], attended, xres[u][:, :, :], ALU.add).then_inc(added, 1)
                tile_statistics(dve, total, lnst, agg, c["carrier"], stats, n, ln_step)

            def through(small):
                for _ in small:
                    pass

            def body(n, u, i, first, last):
                for step in range(STEPS1):
                    if ended(n, step):
                        break
                    small = iter(())
                    for s, use, m, v, g, phase in active(n, u, step, first):
                        if phase == 0:
                            through(small)
                            first_lambda(use, g, s)
                        elif phase <= NEWTON + 1:
                            for ins in moments(use, g, s, phase):
                                next(small, None)
                            ins.then_inc(dve_step[s], 1)
                            through(small)
                            small = newton(use, g, s, phase) if phase <= NEWTON else row_sums(use, g, s, phase, v)
                    through(small)
                    if step == MAKE_QK and not last:
                        take_k(n + 1, 1 - u)
                    if step == NORMALISE and not first:
                        normalise(n - 1)
                    if step == PROJECT_OUT and not first:
                        add(n - 1, 1 - u, i + u)

            take_k(0, 0)
            bodies(dve, body)



def inverse_roots(nc, ctx, counted, name, chains):
    ends = []
    made, rooted, before, rooted_before = counted
    shift = [ctx.enter_context(nc.sbuf_tensor(f"{name}_shift{i}", [P, TILES], F32)) for i in range(len(chains))]
    with nc.Block() as block:

        @block.vector
        def _(dve):
            n = before
            for i, (source, out, eps) in enumerate(chains):
                if i:
                    dve.wait_ge(rooted, rooted_before + i)
                for ins in source(dve, shift[i]):
                    n += 1
                    ins.then_inc(made, 1)
                    dve.wait_ge(made, n)
                n += 1
                dve.tensor_scalar(shift[i][:, :], shift[i][:, :], eps, None, ALU.add).then_inc(made, 1)
                ends.append(n)

        @block.scalar
        def _(act):
            for i, (source, out, eps) in enumerate(chains):
                act.wait_ge(made, ends[i])
                act.activation(out[:, :], shift[i][:, :], ACT.Abs_reciprocal_sqrt).then_inc(rooted, 1)

    counted[2:] = ends[-1], rooted_before + len(chains)



def router(nc, ctx, sems, counted, base, name, X, centre, scale, gain, keep_rows, hT_all, weights, logits, c):
    def sb(n, shape, dt=F32):
        return ctx.enter_context(nc.sbuf_tensor(f"{name}_{n}", shape, dt))

    E = weights.shape[1]
    wr = sb("wr", [P, E])
    rows = [sb(f"rows{u}", [P, 2, D]) for u in range(2)]
    rT = [sb(f"rT{u}", [P, N]) for u in range(2)]
    gcol = sb("gcol", [P, 1]) if gain is not None else None
    turn = [ctx.enter_context(nc.psum_tensor(f"{name}_turn{u}", [P, 512], F32)) for u in range(2)]
    lg = [ctx.enter_context(nc.psum_tensor(f"{name}_lg{u}", [P, 2, E], F32)) for u in range(2)]
    loaded = sems(name + "_loaded")
    rows_ready, rows_kept, turned, rT_ready, lg_made, lg_read = counted
    NB = B

    def pairs(eng, body):
        body(0, 0, True)
        body(1, 1, True)
        with eng.Fori(1, NB // 2) as i:
            body(i * 2, 0, False)
            body(i * 2 + 1, 1, False)

    with nc.Block() as block:

        @block.sync
        def _(sp):
            sp.dma_start(wr[:, :], weights).then_inc(loaded, 16)
            if gain is not None:
                sp.dma_start(gcol[:, :], gain).then_inc(loaded, 16)

        @block.vector
        def _(dve):
            def normalise(n, u, first):
                if not first:
                    dve.wait_ge(turned, base + n - 1)
                    if keep_rows:
                        dve.wait_ge(rows_kept, n - 1)
                for t in range(2):
                    tile = n * 2 + t
                    x = X[:, bass.ds(tile, 1), :].squeeze(1)
                    s = scale[:, bass.ds(tile, 1)]
                    if centre is None:
                        last = dve.tensor_scalar(rows[u][:, t, :], x, s, None, ALU.mult)
                    else:
                        last = dve.tensor_scalar(rows[u][:, t, :], x, centre[:, bass.ds(tile, 1), 0], s,
                                                 ALU.subtract, ALU.mult)
                last.then_inc(rows_ready, 1)

            def body(n, u, first):
                if first and u == 0:
                    normalise(0, 0, True)
                if first and u == 0:
                    normalise(1, 1, True)
                elif first:
                    normalise(2, 0, False)
                else:
                    normalise_next(n, u)
                dve.wait_ge(lg_made, base + n + 1)
                dve.tensor_scalar(logits[:, bass.ds(n * 2, 2), :], lg[u][:, :, :], 1.0, None, ALU.mult)\
                    .then_inc(lg_read, 1)

            def normalise_next(n, u):
                normalise(n + 1, 1 - u, False)

            body(0, 0, True)
            body(1, 1, True)
            with dve.Fori(1, NB // 2 - 1) as i:
                body(i * 2, 0, False)
                body(i * 2 + 1, 1, False)
            body(NB - 2, 0, False)
            dve.wait_ge(lg_made, base + NB)
            dve.tensor_copy(logits[:, 2 * NB - 2:2 * NB, :], lg[1][:, :, :]).then_inc(lg_read, 1)

        @block.gpsimd
        def _(pool):
            def body(n, u, first):
                if keep_rows:
                    pool.wait_ge(rows_ready, base + n + 1)
                    pool.tensor_copy(X[:, bass.ds(n * 2, 2), :], rows[u][:, :, :]).then_inc(rows_kept, 1)
            if keep_rows:
                pairs(pool, body)

        @block.tensor
        def _(pe):
            pe.wait_ge(loaded, 32 if gain is not None else 16)

            def body(n, u, first):
                pe.wait_ge(rows_ready, base + n + 1)
                if not first:
                    pe.wait_ge(rT_ready, base + n - 1)
                for t in range(2):
                    last = pe.transpose(turn[u][:, t * P:(t + 1) * P], rows[u][:, t, :], c["ident"][:, :])
                last.then_inc(turned, 1)
                if not first:
                    pe.wait_ge(lg_read, base + n - 1)
                pe.wait_ge(rT_ready, base + n + 1)
                for t in range(2):
                    last = pe.matmul(lg[u][:, t, :], rT[u][:, t * P:(t + 1) * P], wr[:, :], start=True, stop=True)
                last.then_inc(lg_made, 1)

            pairs(pe, body)

        @block.scalar
        def _(act):
            act.wait_ge(loaded, 32 if gain is not None else 16)

            def body(n, u, first):
                if not first:
                    act.wait_ge(lg_made, base + n - 1)
                act.wait_ge(turned, base + n + 1)
                g = gcol[:, 0:1] if gain is not None else 1.0
                act.activation(rT[u][:, :], turn[u][:, 0:N], ACT.Identity, scale=g).then_inc(rT_ready, 1)
                if hT_all is not None:
                    act.wait_ge(rT_ready, base + n + 1)
                    act.activation(hT_all[:, bass.ds(n * N, N)], rT[u][:, :], ACT.Copy)

            pairs(act, body)



E1 = 8
F1 = 512
CAP = int(1.25 * B * N / E1)
ROWS = 256
FAR = float(1 << 20)


def stage2(nc, ctx, sems, dram, X, stats, logits, c):
    def sb(name, shape, dt=F32):
        return ctx.enter_context(nc.sbuf_tensor("s2_" + name, shape, dt))

    def ps(name, shape):
        return ctx.enter_context(nc.psum_tensor("s2_" + name, shape, F32))

    T = TILES
    best = sb("best", [P, T])
    eq = sb("eq", [P, T, E1])
    hot = sb("hot", [P, T, E1])
    shifted = sb("shifted", [P, T, E1])
    tot = sb("tot", [P, T, E1])
    upto = sb("upto", [P, T, E1])
    place = sb("place", [P, T, E1])
    rank = sb("rank", [P, T])
    pos = sb("pos", [P, T])
    first_slot = sb("first_slot", [P, T])
    kept = sb("kept", [P, T])
    total = sb("total", [P, T])
    factor = sb("factor", [P, T])
    slot = sb("slot", [P, T])
    slot_u = sb("slot_u", [P, T], U32)
    early = sb("early", [P, E1])
    begin = sb("begin", [P, E1])
    unit = sb("unit", [P, T])
    cum_ps = ps("cum_ps", [P, T, E1])
    tot_ps = ps("tot_ps", [P, T, E1])
    col = sems("s2_col")
    hot_ready = sems("s2_hot_ready")
    sums_made = sems("s2_sums_made")
    shifted_ready = sems("s2_shifted_ready")
    exp_ready = sems("s2_exp_ready")
    step = sems("s2_step")

    with nc.Block() as block:

        @block.gpsimd
        def _(pool):
            pool.iota(early[:, :], pattern=[[-1, E1]], base=E1, channel_multiplier=0,
                      allow_small_or_imprecise_dtypes=True).then_inc(col, 1)
            pool.iota(begin[:, :], pattern=[[CAP, E1]], base=0, channel_multiplier=0,
                      allow_small_or_imprecise_dtypes=True).then_inc(col, 1)

        @block.tensor
        def _(pe):
            pe.wait_ge(hot_ready, 1)
            flat = hot[:, :, :].rearrange("p t e -> p (t e)")
            pe.matmul(cum_ps[:, :, :].rearrange("p t e -> p (t e)"), c["prefix"][:, :], flat, start=True, stop=True)
            pe.matmul(tot_ps[:, :, :].rearrange("p t e -> p (t e)"), c["ones"][:, :], flat, start=True, stop=True)\
                .then_inc(sums_made, 1)

        @block.scalar
        def _(act):
            act.wait_ge(shifted_ready, 1)
            act.activation(shifted[:, :, :], shifted[:, :, :], ACT.Exp).then_inc(exp_ready, 1)

        @block.vector
        def _(dve):
            n = [0]

            def settle(ins):
                n[0] += 1
                ins.then_inc(step, 1)
                dve.wait_ge(step, n[0])

            by_tile = lambda t: broadcast_last(t[:, :], E1)
            dve.memset(unit[:, :], 1.0)
            settle(dve.tensor_reduce(best[:, :], logits[:, :, :], AX.X, ALU.max))
            dve.tensor_tensor(shifted[:, :, :], logits[:, :, :], by_tile(best), ALU.subtract)\
                .then_inc(shifted_ready, 1)
            settle(dve.tensor_tensor(eq[:, :, :], logits[:, :, :], by_tile(best), ALU.is_equal))
            dve.wait_ge(col, 2)
            settle(dve.tensor_tensor(eq[:, :, :], eq[:, :, :], broadcast_middle(early[:, :], T), ALU.mult))
            settle(dve.tensor_reduce(rank[:, :], eq[:, :, :], AX.X, ALU.max))
            settle(dve.tensor_tensor(hot[:, :, :], eq[:, :, :], by_tile(rank), ALU.is_equal))
            dve.sem_inc(hot_ready, 1)
            dve.wait_ge(sums_made, 1)
            settle(dve.tensor_copy(tot[:, :, :], tot_ps[:, :, :]))
            for e in range(E1):
                last = dve.tensor_tensor_scan(upto[:, :, e], unit[:, :], tot[:, :, e], 0.0, ALU.mult, ALU.add)
            settle(last)
            settle(dve.tensor_tensor(upto[:, :, :], upto[:, :, :], tot[:, :, :], ALU.subtract))
            settle(dve.tensor_tensor(place[:, :, :], upto[:, :, :], cum_ps[:, :, :], ALU.add))
            settle(dve.tensor_tensor(place[:, :, :], place[:, :, :], hot[:, :, :], ALU.mult))
            settle(dve.tensor_reduce(pos[:, :], place[:, :, :], AX.X, ALU.add))
            settle(dve.tensor_tensor(eq[:, :, :], hot[:, :, :], broadcast_middle(begin[:, :], T), ALU.mult))
            settle(dve.tensor_reduce(first_slot[:, :], eq[:, :, :], AX.X, ALU.add))
            settle(dve.tensor_scalar(kept[:, :], pos[:, :], float(CAP), None, ALU.is_le))
            settle(dve.scalar_tensor_tensor(slot[:, :], pos[:, :], FAR - 1.0, first_slot[:, :], ALU.add, ALU.add))
            settle(dve.scalar_tensor_tensor(slot[:, :], kept[:, :], -FAR, slot[:, :], ALU.mult, ALU.add))
            settle(dve.tensor_copy(slot_u[:, :], slot[:, :]))
            dve.wait_ge(exp_ready, 1)
            settle(dve.tensor_reduce(total[:, :], shifted[:, :, :], AX.X, ALU.add))
            settle(dve.reciprocal(factor[:, :], total[:, :]))
            settle(dve.scalar_tensor_tensor(factor[:, :], factor[:, :], -1.0, kept[:, :], ALU.add, ALU.mult))
            settle(dve.tensor_scalar(factor[:, :], factor[:, :], 1.0, None, ALU.add))

    slots, done = dram["slots"], dram["done"]
    dispatched = sems("s2_dispatched")
    with nc.Block() as block:

        @block.gpsimd
        def _(pool):
            for t in range(T):
                pool.indirect_dma_start(slots, bass.IndirectOffsetOnAxis(ap=slot_u[:, t:t + 1], axis=0), X[:, t, :], None,
                                        bounds_check=E1 * CAP - 1, oob_is_err=False).then_inc(dispatched, 16)
            pool.wait_ge(dispatched, 16 * T)

    w1 = [sb(f"w1{u}", [P, F1]) for u in range(2)]
    w2 = [sb(f"w2{u}", [P, F1 // P, D]) for u in range(2)]
    rows = [sb(f"rows{v}", [P, 2, D]) for v in range(2)]
    rT = [sb(f"rT{v}", [P, ROWS]) for v in range(2)]
    hid = [sb(f"hid{v}", [P, F1 // P, ROWS]) for v in range(2)]
    res = [sb(f"res{v}", [P, 2, D]) for v in range(2)]
    with ExitStack() as inner:
        def psi(name, shape):
            return inner.enter_context(nc.psum_tensor("s2_" + name, shape, F32))

        turn_out = [psi(f"turn_out{v}", [P, 512]) for v in range(1)]
        hid_ps = [psi(f"hid_ps{v}", [P, F1 // P, ROWS]) for v in range(2)]
        out_ps = psi("out_ps", [P, 2, D])
        w_loaded = [sems(f"s2_w_loaded{u}") for u in range(2)]
        r_loaded = [sems(f"s2_r_loaded{v}") for v in range(2)]
        r_turned = sems("s2_r_turned")
        rT_ready = sems("s2_rT_ready")
        hid_made = sems("s2_hid_made")
        hid_ready = sems("s2_hid_ready")
        out_made = sems("s2_out_made")
        out_ready = sems("s2_out_ready")
        stored = [sems(f"s2_stored{v}") for v in range(2)]
        GPE = CAP // ROWS
        groups = E1 * GPE
        src = slots.rearrange("(g t p) d -> g p t d", p=P, t=2)
        dst = done.rearrange("(g t p) d -> g p t d", p=P, t=2)
        PER = 2 * GPE

        with nc.Block() as block:

            def pairs(eng, body, tail):
                for j in range(PER):
                    body(j, j % 2, j // GPE, j < 2, 0, j)
                with eng.Fori(1, E1 // 2) as i:
                    for j in range(PER):
                        body(i * PER + j, j % 2, j // GPE, False, i, j)

            @block.sync
            def _(sp):
                def load_w(e, u):
                    sp.dma_start(w1[u][:, :], dram["L0_ffn_W1"][bass.ds(e, 1)].squeeze(0)).then_inc(w_loaded[u], 16)
                    sp.dma_start(w2[u][:, :, :], dram["L0_ffn_W2"].rearrange("e (f p) d -> e p f d", p=P)[bass.ds(e, 1)]
                                 .squeeze(0)).then_inc(w_loaded[u], 16)

                def body(g, v, u, first, i, j):
                    if j % GPE == 0:
                        if not (isinstance(i, int)):
                            sp.wait_ge(out_made, g - GPE)
                        load_w(i * 2 + u, u)
                    if not first:
                        sp.wait_ge(r_turned, g - 1)
                    sp.dma_start(rows[v][:, :, :], src[bass.ds(g, 1)].squeeze(0)).then_inc(r_loaded[v], 16)

                pairs(sp, body, None)

            @block.tensor
            def _(pe):
                def turn(g, v, first, loads):
                    pe.wait_ge(r_loaded[v], loads * 16)
                    if not first:
                        pe.wait_ge(rT_ready, g)
                    for t in range(2):
                        last = pe.transpose(turn_out[0][:, t * P:(t + 1) * P], rows[v][:, t, :], c["ident"][:, :])
                    last.then_inc(r_turned, 1)

                def down(g, v, u, first):
                    pe.wait_ge(hid_ready, g + 1)
                    if not first:
                        pe.wait_ge(out_ready, g)
                    for t in range(2):
                        for f in range(F1 // P):
                            last = pe.matmul(out_ps[:, t, :], hid[v][:, f, t * P:(t + 1) * P], w2[u][:, f, :],
                                             start=(f == 0), stop=(f == F1 // P - 1), skip_group_check=True)
                    last.then_inc(out_made, 1)

                def up(g, v, u, first, loads):
                    pe.wait_ge(w_loaded[u], loads * 32)
                    pe.wait_ge(rT_ready, g + 1)
                    if not first:
                        pe.wait_ge(hid_ready, g - 1)
                    for f in range(F1 // P):
                        last = pe.matmul(hid_ps[v][:, f, :], w1[u][:, f * P:(f + 1) * P], rT[v][:, :],
                                         start=True, stop=True)
                    last.then_inc(hid_made, 1)

                def body(g, v, u, first, i, j):
                    begins = isinstance(i, int) and j == 0
                    turn(g, v, begins, i * GPE + j // 2 + 1)
                    up(g, v, u, first, i + 1)
                    if not begins:
                        down(g - 1, 1 - v, (u if j % GPE else 1 - u), isinstance(i, int) and j == 1)

                pairs(pe, body, None)
                down(groups - 1, 1, 1, False)

            @block.scalar
            def _(act):
                def body(g, v, u, first, i, j):
                    act.wait_ge(r_turned, g + 1)
                    if not first:
                        act.wait_ge(hid_made, g - 1)
                    act.activation(rT[v][:, :], turn_out[0][:, 0:ROWS], ACT.Copy).then_inc(rT_ready, 1)
                    act.wait_ge(hid_made, g + 1)
                    if not first:
                        act.wait_ge(out_made, g - 1)
                    act.activation(hid[v][:, :, :], hid_ps[v][:, :, :], ACT.Relu).then_inc(hid_ready, 1)

                pairs(act, body, None)

            @block.vector
            def _(dve):
                def body(g, v, u, first, i, j):
                    dve.wait_ge(out_made, g + 1)
                    if not first:
                        dve.wait_ge(stored[v], (i * GPE + j // 2) * 16)
                    dve.tensor_copy(res[v][:, :, :], out_ps[:, :, :]).then_inc(out_ready, 1)

                pairs(dve, body, None)

            @block.gpsimd
            def _(pool):
                def body(g, v, u, first, i, j):
                    pool.wait_ge(out_ready, g + 1)
                    pool.dma_start(dst[bass.ds(g, 1)].squeeze(0), res[v][:, :, :]).then_inc(stored[v], 16)

                pairs(pool, body, None)
                for v in range(2):
                    pool.wait_ge(stored[v], 16 * groups // 2)

    G = sb("G", [P, T, D])
    own = sems("s2_own")
    GATHERS = 4
    gathered = [sems(f"s2_gathered{i}") for i in range(GATHERS)]
    lnst = sb("lnst", [P, T, 6])
    ln = sems("s2_ln")
    with nc.Block() as block:

        @block.scalar
        def _(act):
            for i in range(GATHERS):
                part = slice(i * T // GATHERS, (i + 1) * T // GATHERS)
                act.activation(G[:, part, :], X[:, part, :], ACT.Copy).then_inc(own, 1)

        @block.gpsimd
        def _(pool):
            for i in range(GATHERS):
                pool.wait_ge(own, i + 1)
                for t in range(i * T // GATHERS, (i + 1) * T // GATHERS):
                    pool.indirect_dma_start(G[:, t, :], None, done, bass.IndirectOffsetOnAxis(ap=slot_u[:, t:t + 1], axis=0),
                                            bounds_check=E1 * CAP - 1, oob_is_err=False).then_inc(gathered[i], 16)

        @block.vector
        def _(dve):
            for i in range(GATHERS):
                dve.wait_ge(gathered[i], 16 * (T // GATHERS))
                for t in range(i * T // GATHERS, (i + 1) * T // GATHERS):
                    last = dve.scalar_tensor_tensor(X[:, t, :], G[:, t, :], factor[:, t:t + 1], X[:, t, :],
                                                    ALU.mult, ALU.add)
                last.then_inc(ln, 1)
                dve.wait_ge(ln, 2 * i + 1)
                for t in range(i * T // GATHERS, (i + 1) * T // GATHERS):
                    last = dve.bn_stats(lnst[:, t, :], X[:, t, :])
                last.then_inc(ln, 1)
                dve.wait_ge(ln, 2 * i + 2)
                for t in range(i * T // GATHERS, (i + 1) * T // GATHERS):
                    dve.bn_aggr(stats[:, t, :], lnst[:, t, :])


def zero_slots(nc, ctx, sems, dram, c):
    zeros = ctx.enter_context(nc.sbuf_tensor("zeros", [P, 1280], F32))
    zeroed = sems("zeroed")
    slots_zeroed = sems("slots_zeroed")
    view = dram["slots"].rearrange("(c p r) d -> c p (r d)", p=P, r=10)
    with nc.Block() as block:

        @block.gpsimd
        def _(pool):
            make_constants(pool, c, c["const_step"])

        @block.vector
        def _(dve):
            dve.memset(zeros[:, :], 0.0).then_inc(zeroed, 1)

        @block.sync
        def _(sp):
            sp.wait_ge(zeroed, 1)
            for k in range(E1 * CAP // (10 * P)):
                sp.dma_start(view[k], zeros[:, :]).then_inc(slots_zeroed, 16)
            sp.wait_ge(slots_zeroed, 16 * (E1 * CAP // (10 * P)))



ATT_CHUNKS = [(0, 0, 8), (1, 0, 4), (1, 4, 4), (0, 8, 8), (1, 8, 4), (1, 12, 4)]
STEPS = len(ATT_CHUNKS)


def softmax_stage(nc, ctx, sems, name, X, kept, centre, scale, second_scale, stats, c, kind):
    def sb(n, shape, dt=F32):
        return ctx.enter_context(nc.sbuf_tensor(f"{name}_{n}", shape, dt))

    def ps(n, shape):
        return ctx.enter_context(nc.psum_tensor(f"{name}_{n}", shape, F32))

    rows = [sb(f"rows{u}", [P, 2, D]) for u in range(2)]
    lean_rows = [sb(f"lean_rows{u}", [P, 2, D]) for u in range(2)] if second_scale is not None else None
    SLOTS, WORK, HEADS = kind.slots, kind.work_banks, kind.heads_banks
    scores = [ps(f"scores{s}", [P, 1024]) for s in range(SLOTS)]
    heads = [ps(f"heads{s}", [P, 512]) for s in range(HEADS)]
    work = [ps(f"work{s}", [P, 512]) for s in range(WORK)]
    att = [sb(f"att{s}", [P, 1024]) for s in range(SLOTS)]
    attT = [sb(f"attT{s}", [P, 1024]) for s in range(SLOTS)]
    peak = [sb(f"peak{s}", [P, 8]) for s in range(SLOTS)]
    total = [sb(f"total{s}", [P, 8]) for s in range(SLOTS)]
    rinv = [sb(f"rinv{s}", [P, 8]) for s in range(SLOTS)]
    diagonal = [sb(f"diagonal{s}", [P, 8, P]) for s in range(SLOTS)]
    total_rows = sb("total_rows", [P, 2, D])
    lnst = sb("lnst", [P, 2, 6])
    agg = sb("agg", [P, 2, 2])

    weights_loaded = sems(name + "_weights_loaded")
    rows_ready = sems(name + "_rows_ready")
    rows_kept = sems(name + "_rows_kept")
    job_made = sems(name + "_job_made")
    job_read = sems(name + "_job_read")
    scored = [sems(f"{name}_scored{s}") for s in range(SLOTS)]
    peak_ready = [sems(f"{name}_peak_ready{s}") for s in range(SLOTS)]
    att_ready = [sems(f"{name}_att_ready{s}") for s in range(SLOTS)]
    diagonal_ready = [sems(f"{name}_diagonal_ready{s}") for s in range(SLOTS)]
    turned = [sems(f"{name}_turned{s}") for s in range(SLOTS)]
    attT_ready = [sems(f"{name}_attT_ready{s}") for s in range(SLOTS)]
    heads_made = [sems(f"{name}_heads_made{s}") for s in range(HEADS)]
    heads_read = [sems(f"{name}_heads_read{s}") for s in range(HEADS)]
    ln_step = sems(name + "_ln_step")

    k = kind(sb, sems, c, rows if second_scale is None else lean_rows)
    project_jobs, finish_jobs = k["project"], k["finish"]
    NP, NF = len(project_jobs), len(finish_jobs)
    PROJECT_STEPS, FINISH_STEPS = k["project_steps"], k["finish_steps"]
    PER_SLOT = STEPS // SLOTS
    TAKES = STEPS // HEADS if k["heads_per_chunk"] else 1

    def body_jobs(first=False, last=False):
        jobs = []
        for step in range(STEPS):
            jobs += [(step, True, a) for a, at in enumerate(PROJECT_STEPS) if at == step and not last]
            jobs += [(step, False, a) for a, at in enumerate(FINISH_STEPS) if at == step and not first]
        return jobs

    def jobs_before(n):
        return NP if isinstance(n, int) and n == 0 else (n + 1) * NP + (n - 1) * NF

    def bank_before(u, first):
        return NP if first else (u + 1) * (NP + NF)

    def projected(n):
        if isinstance(n, int) and n < 2:
            return (n + 1) * NP
        order = body_jobs()
        return jobs_before(n - 1) + max(i for i, (_, is_p, _) in enumerate(order) if is_p) + 1

    def run_step(n, u, step, first, last, run):
        for i, (at, is_p, a) in enumerate(body_jobs(first, last)):
            if at == step:
                run(n + 1 if is_p else n - 1, 1 - u, jobs_before(n) + i, (bank_before(u, first) + i) % WORK, is_p, a)

    def run_tail(run):
        for a in range(NF):
            index = jobs_before(B - 1) + NF + a
            run(B - 1, (B - 1) % 2, index, index % WORK, False, a)

    def bodies(eng, body):
        body(0, 0, 0, first=True)
        body(1, 1, 0)
        with eng.Fori(1, B // 2 - 1) as i:
            body(i * 2, 0, i)
            body(i * 2 + 1, 1, i)
        body(B - 2, 0, B // 2 - 1)
        body(B - 1, 1, B // 2 - 1, last=True)

    def behind(n, u, j, lag):
        return (n, u, j - lag) if j >= lag else (n - 1, 1 - u, j - lag + STEPS)

    def exists(j, lag, first):
        return j >= lag or not first

    def used(n, j):
        return n * PER_SLOT + j // SLOTS

    with nc.Block() as block:

        @block.sync
        def _(sp):
            for dst, src in k["loads"]:
                sp.dma_start(dst, src).then_inc(weights_loaded, 16)
            if k["spread"]:
                k["spread"](sp, job_read, projected, bodies)

        @block.gpsimd
        def _(pool):
            for zeros in k["zeros"]:
                pool.memset(zeros, 0.0).then_inc(k["zeroed"], 1)

            def keep(n, u):
                pool.wait_ge(rows_ready, n + 1)
                pool.tensor_copy(kept[:, bass.ds(n * 2, 2), :], rows[u][:, :, :]).then_inc(rows_kept, 1)

            keep(0, 0)
            keep(1, 1)
            with pool.Fori(1, B // 2) as i:
                keep(i * 2, 0)
                keep(i * 2 + 1, 1)

        @block.tensor
        def _(pe):
            pe.wait_ge(weights_loaded, 16 * len(k["loads"]))
            pe.wait_ge(c["const_step"], CONSTANTS)

            def job(n, u, index, b, is_p, a):
                work_of, _, waits_for_last = (project_jobs if is_p else finish_jobs)[a]
                if waits_for_last:
                    pe.wait_ge(job_read, index)
                elif not (isinstance(index, int) and index < WORK):
                    pe.wait_ge(job_read, index + 1 - WORK)
                if is_p and a == 0:
                    pe.wait_ge(rows_ready, n + 1)
                if not is_p and a == 0:
                    for s in range(HEADS):
                        pe.wait_ge(heads_read[s], (n + 1) * TAKES)
                work_of(pe, work[b], u).then_inc(job_made, 1)

            def weigh(n, u, j):
                s = j % SLOTS
                half, h0, nh = ATT_CHUNKS[j]
                pe.wait_ge(attT_ready[s], (used(n, j) + 1) * 2)
                b = j % HEADS
                if k["heads_per_chunk"]:
                    if not (isinstance(n, int) and n == 0 and j < HEADS):
                        pe.wait_ge(heads_read[b], n * TAKES + j // HEADS)
                elif j == 0 and not (isinstance(n, int) and n == 0):
                    pe.wait_ge(heads_read[0], n)
                last = k["weigh"](pe, u, j, half, h0, nh, attT[s], heads[b])
                if k["heads_per_chunk"] or j == STEPS - 1:
                    last.then_inc(heads_made[b], 1)

            def score(n, u, i, j):
                s = j % SLOTS
                half, h0, nh = ATT_CHUNKS[j]
                keys = (half + 1) * P
                if j == 0:
                    pe.wait_ge(job_read, projected(n))
                    if k["spread"]:
                        pe.wait_ge(k["spread_done"][u], (i + 1) * k["spread_count"])
                k["score"](pe, u, half, h0, nh, keys, scores[s])
                for b in range(2):
                    out = scores[s][:, b * 512:(b + 1) * 512].rearrange("p (h k) -> p h k", k=keys)
                    last = pe.matmul(out[:, :, keys - P:keys], c["minus_ident_bf"][:, :],
                                     broadcast_middle(c["far_mask"][:, :], 512 // keys),
                                     start=False, stop=True, skip_group_check=True)
                last.then_inc(scored[s], 1)

            def turn(n, u, j):
                s = j % SLOTS
                blocks = ATT_CHUNKS[j][0] + 1
                for bank in range(2):
                    pe.wait_ge(diagonal_ready[s], used(n, j) * 3 + bank + 2)
                    for b in range(bank * 4, bank * 4 + 4):
                        last = pe.matmul(scores[s][:, b * P:(b + 1) * P], att[s][:, b * P:(b + 1) * P],
                                         diagonal[s][:, b // blocks, :], start=True, stop=True, skip_group_check=True)
                    last.then_inc(turned[s], 1)

            def body(n, u, i, first=False, last=False):
                for j in range(STEPS):
                    if exists(j, SLOTS, first):
                        weigh(*behind(n, u, j, SLOTS))
                    score(n, u, i, j)
                    run_step(n, u, j, first, last, job)
                    if exists(j, SLOTS - 1, first):
                        turn(*behind(n, u, j, SLOTS - 1))
                if last:
                    for j in range(STEPS, STEPS + SLOTS):
                        weigh(n, u, j - SLOTS)
                        if j < STEPS + SLOTS - 1:
                            turn(n, u, j - SLOTS + 1)
                    run_tail(job)

            pe.wait_ge(k["zeroed"], len(k["zeros"]))
            for a in range(NP):
                job(0, 0, a, a % WORK, True, a)
            bodies(pe, body)

        @block.scalar
        def _(act):
            def exponentials(n, j):
                s = j % SLOTS
                half, h0, nh = ATT_CHUNKS[j]
                keys = (half + 1) * P
                act.wait_ge(peak_ready[s], used(n, j) + 1)
                for a in range(nh):
                    last = act.activation(att[s][:, a * keys:(a + 1) * keys], scores[s][:, a * keys:(a + 1) * keys],
                                          ACT.Exp, bias=peak[s][:, a:a + 1], accum_out=total[s][:, a:a + 1])
                last.then_inc(att_ready[s], 1)

            def copy(n, u, j):
                s = j % SLOTS
                for bank in range(2):
                    part = slice(bank * 512, (bank + 1) * 512)
                    act.wait_ge(turned[s], used(n, j) * 2 + bank + 1)
                    act.activation(attT[s][:, part], scores[s][:, part], ACT.Copy).then_inc(attT_ready[s], 1)

            def body(n, u, i, first=False, last=False):
                for j in range(STEPS):
                    if exists(j, SLOTS - 1, first):
                        copy(*behind(n, u, j, SLOTS - 1))
                    exponentials(n, j)
                if last:
                    for j in range(STEPS - SLOTS + 1, STEPS):
                        copy(n, u, j)

            bodies(act, body)

        @block.vector
        def _(dve):
            dve.wait_ge(weights_loaded, 16 * len(k["loads"]))
            dve.wait_ge(c["const_step"], CONSTANTS)
            dve.wait_ge(k["zeroed"], len(k["zeros"]))

            def normalise_rows(n, u):
                for t in range(2):
                    tile = n * 2 + t
                    last = dve.tensor_scalar(rows[u][:, t, :], X[:, bass.ds(tile, 1), :].squeeze(1),
                                             centre[:, bass.ds(tile, 1), 0], scale[:, bass.ds(tile, 1)],
                                             ALU.subtract, ALU.mult)
                    if second_scale is not None:
                        last = dve.tensor_scalar(lean_rows[u][:, t, :], X[:, bass.ds(tile, 1), :].squeeze(1),
                                                 centre[:, bass.ds(tile, 1), 0], second_scale[:, bass.ds(tile, 1)],
                                                 ALU.subtract, ALU.mult)
                last.then_inc(rows_ready, 1)

            def job(n, u, index, b, is_p, a):
                if not is_p and a == NF - 1:
                    residual(n, u, index, b)
                    return
                dve.wait_ge(job_made, index + 1)
                (project_jobs if is_p else finish_jobs)[a][1](dve, work[b], u).then_inc(job_read, 1)

            def residual(n, u, index, b):
                dve.wait_ge(job_made, index + 1)
                dve.wait_ge(rows_kept, n + 1)
                pair = bass.ds(n * 2, 2)
                attended = work[b][:, 0:2 * D].rearrange("p (t d) -> p t d", t=2)
                dve.tensor_tensor(total_rows[:, :, :], attended, kept[:, pair, :], ALU.add).then_inc(ln_step, 1)
                dve.tensor_tensor(X[:, pair, :], attended, kept[:, pair, :], ALU.add).then_inc(job_read, 1)
                tile_statistics(dve, total_rows, lnst, agg, c["carrier"], stats, n, ln_step)

            def peaks(n, j):
                s = j % SLOTS
                half, h0, nh = ATT_CHUNKS[j]
                dve.wait_ge(scored[s], used(n, j) + 1)
                dve.tensor_reduce(peak[s][:, 0:nh], scores[s][:, :].rearrange("p (h k) -> p h k", h=nh), AX.X,
                                  ALU.max, negate=True).then_inc(peak_ready[s], 1)

            def sums(n, u, j):
                s = j % SLOTS
                nh = ATT_CHUNKS[j][2]
                dve.wait_ge(att_ready[s], used(n, j) + 1)
                dve.reciprocal(rinv[s][:, 0:nh], total[s][:, 0:nh]).then_inc(diagonal_ready[s], 1)
                dve.wait_ge(diagonal_ready[s], used(n, j) * 3 + 1)
                for bank in range(2):
                    part = slice(bank * nh // 2, (bank + 1) * nh // 2)
                    dve.tensor_tensor(diagonal[s][:, part, :], broadcast_middle(c["ident"][:, :], nh // 2),
                                      broadcast_last(rinv[s][:, part], P), ALU.mult).then_inc(diagonal_ready[s], 1)

            def take_heads(n, u, j):
                half, h0, nh = ATT_CHUNKS[j]
                b = j % HEADS
                if k["heads_per_chunk"]:
                    dve.wait_ge(heads_made[b], n * TAKES + j // HEADS + 1)
                elif j < STEPS - 1:
                    return
                else:
                    b = 0
                    dve.wait_ge(heads_made[0], n + 1)
                k["take_heads"](dve, u, half, h0, nh, heads[b]).then_inc(heads_read[b], 1)

            def body(n, u, i, first=False, last=False):
                for j in range(STEPS):
                    if exists(j, SLOTS - 1, first):
                        sums(*behind(n, u, j, SLOTS - 1))
                    if exists(j, SLOTS, first):
                        take_heads(*behind(n, u, j, SLOTS))
                    peaks(n, j)
                    if j == 0 and not last:
                        if not first:
                            dve.wait_ge(rows_kept, n)
                        normalise_rows(n + 1, 1 - u)
                    run_step(n, u, j, first, last, job)
                if last:
                    for j in range(STEPS, STEPS + SLOTS):
                        take_heads(n, u, j - SLOTS)
                        if j < STEPS + SLOTS - 1:
                            sums(n, u, j - SLOTS + 1)
                    run_tail(job)

            normalise_rows(0, 0)
            for a in range(NP):
                job(0, 0, a, a % WORK, True, a)
            bodies(dve, body)


def gqa(dram):
    HQ, HKV, HD = 16, 4, 64
    PAIRS = HQ * HD // P

    def kind(sb, sems, c, rows):
        wq = sb("wq", [P, HQ * HD])
        wk = sb("wk", [P, HKV, 2, HD])
        wv = sb("wv", [P, HKV * HD])
        wo = sb("wo", [P, PAIRS, D])
        xT = sb("xT", [P, N])
        qT = [sb(f"qT{u}", [P, PAIRS, N]) for u in range(2)]
        kT = [sb(f"kT{u}", [P, HKV, 2, N]) for u in range(2)]
        v = [sb(f"v{u}", [P, 2, HKV * HD]) for u in range(2)]
        oT = [sb(f"oT{u}", [P, PAIRS, N]) for u in range(2)]

        def halves(w):
            return w[:, :].rearrange("p (t n) -> p t n", t=2)

        def turn_rows(pe, w, u):
            for t in range(2):
                last = pe.transpose(w[:, t * P:(t + 1) * P], rows[u][:, t, :], c["ident"][:, :])
            return last

        def make_q(b):
            def pe_part(pe, w, u):
                for j in range(2):
                    last = pe.matmul(w[:, j * N:(j + 1) * N], wq[:, (2 * b + j) * P:(2 * b + j + 1) * P], xT[:, :],
                                     start=True, stop=True)
                return last
            return pe_part, lambda dve, w, u: dve.tensor_scalar(qT[u][:, 2 * b:2 * b + 2, :], halves(w),
                                                                float(HD) ** -0.5, None, ALU.mult), b == 0

        def make_k(b):
            def pe_part(pe, w, u):
                for j in range(2):
                    last = pe.matmul(w[:, j * N:(j + 1) * N], wk[:, 2 * b + j, :, :].rearrange("p t d -> p (t d)"),
                                     xT[:, :], start=True, stop=True)
                return last

            def dve_part(dve, w, u):
                for r in range(2):
                    rows_of = slice(r * HD, (r + 1) * HD)
                    last = dve.tensor_copy(kT[u][rows_of, 2 * b:2 * b + 2, r, :], halves(w)[rows_of, :, :])
                return last
            return pe_part, dve_part, False

        def make_v(pe, w, u):
            for t in range(2):
                last = pe.matmul(w[:, t * HKV * HD:(t + 1) * HKV * HD], xT[:, t * P:(t + 1) * P], wv[:, :],
                                 start=True, stop=True)
            return last

        def score(pe, u, half, h0, nh, keys, out):
            for a in range(0, nh, 2):
                b = (h0 + a) // 2
                pe.matmul(out[:, a * keys:(a + 2) * keys], qT[u][:, b, half * P:(half + 1) * P],
                          kT[u][:, (h0 + a) // 4, :, 0:keys], start=(a * keys % 512 == 0), stop=False,
                          skip_group_check=True)

        def weigh(pe, u, j, half, h0, nh, attT, out):
            blocks = half + 1
            turned = attT[:, :].rearrange("p (a r kb q) -> p r kb a q", r=2, kb=blocks, q=P)
            for g in range(nh // 4):
                for kb in range(blocks):
                    for r in range(2):
                        last = pe.matmul(out[r * HD:(r + 1) * HD, g * 2 * P:(g + 1) * 2 * P],
                                         v[u][:, kb, (h0 // 4 + g) * HD:(h0 // 4 + g + 1) * HD],
                                         turned[:, r, kb, 2 * g:2 * g + 2, :], start=(g == 0 and kb == 0),
                                         stop=(kb == half), tile_position=(0, r * HD), skip_group_check=True)
            return last

        def take_heads(dve, u, half, h0, nh, heads):
            return dve.tensor_copy(oT[u][:, h0 // 2:(h0 + nh) // 2, half * P:(half + 1) * P],
                                   heads[:, 0:nh // 2 * P].rearrange("p (b q) -> p b q", q=P))

        def project_out(pe, w, u):
            for t in range(2):
                for b in range(PAIRS):
                    last = pe.matmul(w[:, t * D:(t + 1) * D], oT[u][:, b, t * P:(t + 1) * P], wo[:, b, :],
                                     start=(b == 0), stop=(b == PAIRS - 1), skip_group_check=True)
            return last

        return {
            "loads": [(wq[:, :], dram["Wq"]), (wk[:, :, 0, :], dram["Wk"].rearrange("p (h d) -> p h d", d=HD)),
                      (wk[:, :, 1, :], dram["Wk"].rearrange("p (h d) -> p h d", d=HD)), (wv[:, :], dram["Wv"]),
                      (wo[:, :, :], dram["Wo"].rearrange("(b p) d -> p b d", p=P))],
            "zeros": [kT[u][(1 - r) * HD:(2 - r) * HD, :, r, :] for u in range(2) for r in range(2)],
            "zeroed": sems("gqa_zeroed"),
            "spread": None,
            "score": score, "weigh": weigh, "take_heads": take_heads, "heads_per_chunk": True,
            "project": [(turn_rows, lambda dve, w, u: dve.tensor_copy(xT[:, :], w[:, 0:N]), False)]
            + [make_q(b) for b in range(4)] + [make_k(b) for b in range(2)]
            + [(make_v, lambda dve, w, u: dve.tensor_copy(v[u][:, :, :], halves(w)), False)],
            "project_steps": [0, 0, 0, 1, 1, 1, 2, 2],
            "finish": [(project_out, None, False)],
            "finish_steps": [3],
        }

    kind.slots, kind.work_banks, kind.heads_banks = 2, 2, 2
    return kind


def latent(dram):
    LATENT = 64

    def order(h):
        return h % 4 * 4 + h // 4

    def kind(sb, sems, c, rows):
        wq = sb("wq", [P, D])
        wdown = sb("wdown", [P, LATENT])
        wuk = sb("wuk", [LATENT, D])
        wuv = sb("wuv", [LATENT, D])
        wo = sb("wo", [P, D])
        gain = sb("gain", [P, 1])
        hT = sb("hT", [P, N])
        cT = sb("cT", [LATENT, N])
        qT = [sb(f"qT{u}", [P, N]) for u in range(2)]
        kT = [sb(f"kT{u}", [P, N]) for u in range(2)]
        kM = [sb(f"kM{u}", [P, H, N]) for u in range(2)]
        vM = [sb(f"vM{u}", [P, 2, 4, 4 * (4 * DH + DH)]) for u in range(2)]
        oT = [sb(f"oT{u}", [P, N]) for u in range(2)]
        spread_done = [sems(f"mla_spread{u}") for u in range(2)]

        def turn(source):
            def pe_part(pe, w, u):
                for t in range(2):
                    last = pe.transpose(w[:, t * P:(t + 1) * P], source(u, t), c["ident"][:, :])
                return last
            return pe_part

        def make_q_latent(pe, w, u):
            pe.matmul(w[:, 0:N], wq[:, :], hT[:, :], start=True, stop=True)
            return pe.matmul(w[0:LATENT, N:2 * N], wdown[:, :], hT[:, :], start=True, stop=True)

        def take_q_latent(dve, w, u):
            dve.tensor_scalar(qT[u][:, :], w[:, 0:N], float(DH) ** -0.5, None, ALU.mult)
            return dve.tensor_copy(cT[:, :], w[0:LATENT, N:2 * N])

        def make_kv(pe, w, u):
            pe.matmul(w[:, 0:N], wuk[:, :], cT[:, :], start=True, stop=True)
            for t in range(2):
                last = pe.matmul(w[:, N + t * D:N + (t + 1) * D], cT[:, t * P:(t + 1) * P], wuv[:, :],
                                 start=True, stop=True)
            return last

        def take_kv(dve, w, u):
            for t in range(2):
                strips = vM[u][:, t, :, :].rearrange("p g (m c) -> p g m c", m=4)
                dve.tensor_copy(strips[:, :, :, 0:DH],
                                w[:, N + t * D:N + (t + 1) * D].rearrange("p (g m d) -> p g m d", g=4, m=4))
            return dve.tensor_copy(kT[u][:, :], w[:, 0:N])

        def spread(sp, job_read, projected, bodies):
            sp.wait_ge(zeroed, 4)

            def body(n, u, i, first=False, last=False):
                sp.wait_ge(job_read, projected(n))
                for h in range(H):
                    rows_of = slice(h * DH, (h + 1) * DH)
                    sp.dma_start(kM[u][rows_of, order(h), :], kT[u][rows_of, :]).then_inc(spread_done[u], 16)
            bodies(sp, body)

        def score(pe, u, half, h0, nh, keys, out):
            per = 512 // keys
            for b in range(2):
                pe.matmul(out[:, b * 512:(b + 1) * 512], qT[u][:, half * P:(half + 1) * P],
                          kM[u][:, h0 + b * per:h0 + (b + 1) * per, 0:keys], start=True, stop=False,
                          skip_group_check=True)

        def weigh(pe, u, j, half, h0, nh, attT, out):
            for kb in range(half + 1):
                for a in range(nh):
                    m, g = divmod(h0 + a, 4)
                    col = (a * (half + 1) + kb) * P
                    last = pe.matmul(out[32 * g:32 * g + 32, half * P:(half + 1) * P],
                                     vM[u][:, kb, g, 32 * m:32 * m + 32], attT[:, col:col + P],
                                     start=(j == 0 and a < 4), stop=False, tile_position=(0, 32 * g),
                                     skip_group_check=True)
            return last

        def take_heads(dve, u, half, h0, nh, heads):
            return dve.tensor_copy(oT[u][:, :], heads[:, 0:N])

        def project_out(pe, w, u):
            for t in range(2):
                last = pe.matmul(w[:, t * D:(t + 1) * D], oT[u][:, t * P:(t + 1) * P], wo[:, :], start=True, stop=True)
            return last

        zeroed = sems("mla_zeroed")
        return {
            "loads": [(wq[:, :], dram["Wq"]), (wdown[:, :], dram["Wdkv"]), (wuk[:, :], dram["Wuk"]),
                      (wuv[:, :], dram["Wuv"]), (wo[:, :], dram["Wo"]), (gain[:, :], dram["g1"])],
            "zeros": [kM[u][:, :, :] for u in range(2)] + [vM[u][:, :, :, :] for u in range(2)],
            "zeroed": zeroed,
            "spread": spread, "spread_done": spread_done, "spread_count": 16 * H,
            "score": score, "weigh": weigh, "take_heads": take_heads, "heads_per_chunk": False,
            "project": [(turn(lambda u, t: rows[u][:, t, :]),
                         lambda dve, w, u: dve.tensor_scalar(hT[:, :], w[:, 0:N], gain[:, 0:1], None, ALU.mult), False),
                        (make_q_latent, take_q_latent, True), (make_kv, take_kv, True)],
            "project_steps": [0, 1, 2],
            "finish": [(project_out, None, True)],
            "finish_steps": [4],
        }

    kind.slots, kind.work_banks, kind.heads_banks = 3, 1, 1
    return kind



E2 = 8
F2 = 256
SPAN = 512
SPAN_TILES = SPAN // P


def choose_two(nc, ctx, sems, logits, share):
    T = TILES

    def sb(name, shape):
        return ctx.enter_context(nc.sbuf_tensor("c2_" + name, shape, F32))

    first = sb("first", [P, T])
    second = sb("second", [P, T])
    rank = sb("rank", [P, T])
    eq = sb("eq", [P, T, E2])
    rest = sb("rest", [P, T, E2])
    hot1 = sb("hot1", [P, T, E2])
    hot2 = sb("hot2", [P, T, E2])
    early = sb("early", [P, E2])
    gap = sb("gap", [P, T])
    ratio = sb("ratio", [P, T])
    one = sb("one", [P, T])
    g1 = sb("g1", [P, T])
    early_ready = sems("c2_early_ready")
    gap_ready = sems("c2_gap_ready")
    ratio_ready = sems("c2_ratio_ready")
    step = sems("c2_step")

    with nc.Block() as block:

        @block.gpsimd
        def _(pool):
            pool.iota(early[:, :], pattern=[[-1, E2]], base=E2, channel_multiplier=0,
                      allow_small_or_imprecise_dtypes=True).then_inc(early_ready, 1)

        @block.scalar
        def _(act):
            act.wait_ge(gap_ready, 1)
            act.activation(ratio[:, :], gap[:, :], ACT.Exp).then_inc(ratio_ready, 1)

        @block.vector
        def _(dve):
            n = [0]

            def settle(ins):
                n[0] += 1
                ins.then_inc(step, 1)
                dve.wait_ge(step, n[0])

            by_tile = lambda t: broadcast_last(t[:, :], E2)

            def largest(values, top, hot):
                settle(dve.tensor_reduce(top[:, :], values[:, :, :], AX.X, ALU.max))
                settle(dve.tensor_tensor(eq[:, :, :], values[:, :, :], by_tile(top), ALU.is_equal))
                settle(dve.tensor_tensor(eq[:, :, :], eq[:, :, :], broadcast_middle(early[:, :], T), ALU.mult))
                settle(dve.tensor_reduce(rank[:, :], eq[:, :, :], AX.X, ALU.max))
                settle(dve.tensor_tensor(hot[:, :, :], eq[:, :, :], by_tile(rank), ALU.is_equal))

            dve.wait_ge(early_ready, 1)
            largest(logits, first, hot1)
            settle(dve.tensor_scalar(rest[:, :, :], hot1[:, :, :], -3e38, None, ALU.mult))
            settle(dve.tensor_tensor(rest[:, :, :], rest[:, :, :], logits[:, :, :], ALU.add))
            largest(rest, second, hot2)
            dve.tensor_tensor(gap[:, :], second[:, :], first[:, :], ALU.subtract).then_inc(gap_ready, 1)
            dve.wait_ge(ratio_ready, 1)
            settle(dve.tensor_scalar(one[:, :], ratio[:, :], 1.0, None, ALU.add))
            settle(dve.reciprocal(g1[:, :], one[:, :]))
            settle(dve.tensor_tensor(ratio[:, :], ratio[:, :], g1[:, :], ALU.mult))
            settle(dve.tensor_tensor(hot1[:, :, :], hot1[:, :, :], by_tile(g1), ALU.mult))
            settle(dve.tensor_tensor(hot2[:, :, :], hot2[:, :, :], by_tile(ratio), ALU.mult))
            dve.tensor_tensor(share[:, :, :], hot1[:, :, :], hot2[:, :, :], ALU.add)


def stage5(nc, ctx, sems, dram, X, rows3, hT_all, share, stats, c):
    def sb(name, shape, dt=F32):
        return ctx.enter_context(nc.sbuf_tensor("s5_" + name, shape, dt))

    def ps(name, shape):
        return ctx.enter_context(nc.psum_tensor("s5_" + name, shape, F32))

    FB = F2 // P
    SPANS = B * N // SPAN
    w1 = sb("w1", [P, E2, F2])
    w2 = sb("w2", [P, E2, FB, D])
    hid = [sb(f"hid{v}", [P, FB, SPAN]) for v in range(2)]
    acc = [sb(f"acc{v}", [P, SPAN_TILES, D]) for v in range(2)]
    part = sb("part", [P, SPAN_TILES, E2])
    lnst = sb("lnst", [P, SPAN_TILES, 6])
    agg = sb("agg", [P, SPAN_TILES, 2])
    summed = sems("s5_summed")
    hid_ps = [ps(f"hid_ps{v}", [P, FB, SPAN]) for v in range(2)]
    out_ps = [ps(f"out_ps{v}", [P, SPAN_TILES, D]) for v in range(2)]
    loaded = sems("s5_loaded")
    hid_made = sems("s5_hid_made")
    hid_ready = sems("s5_hid_ready")
    out_made = sems("s5_out_made")
    out_read = sems("s5_out_read")
    step = sems("s5_step")

    def spans(eng, body):
        body(0)
        with eng.Fori(1, SPANS) as i:
            body(i)

    with nc.Block() as block:

        @block.sync
        def _(sp):
            sp.dma_start(w1[:, :, :], dram["w1"].rearrange("e d f -> d e f")).then_inc(loaded, 16)
            sp.dma_start(w2[:, :, :, :], dram["w2"].rearrange("e (b p) d -> p e b d", p=P)).then_inc(loaded, 16)

        @block.tensor
        def _(pe):
            pe.wait_ge(loaded, 32)

            def up(i, e, start):
                v = e % 2
                k = i * E2 + e
                if not start:
                    pe.wait_ge(hid_ready, k - 1)
                for b in range(FB):
                    last = pe.matmul(hid_ps[v][:, b, :], w1[:, e, b * P:(b + 1) * P], hT_all[:, bass.ds(i * SPAN, SPAN)],
                                     start=True, stop=True)
                last.then_inc(hid_made, 1)

            def down(i, e, start):
                v = e % 2
                k = i * E2 + e
                pe.wait_ge(hid_ready, k + 1)
                if not start:
                    pe.wait_ge(out_read, k - 1)
                for t in range(SPAN_TILES):
                    for b in range(FB):
                        last = pe.matmul(out_ps[v][:, t, :], hid[v][:, b, t * P:(t + 1) * P], w2[:, e, b, :],
                                         start=(b == 0), stop=(b == FB - 1), skip_group_check=True)
                last.then_inc(out_made, 1)

            def body(i):
                start = isinstance(i, int)
                for e in range(E2):
                    up(i, e, start and e < 2)
                    if e:
                        down(i, e - 1, start and e < 3)
                    elif not start:
                        down(i - 1, E2 - 1, False)

            spans(pe, body)
            down(SPANS - 1, E2 - 1, False)

        @block.scalar
        def _(act):
            def body(i):
                for e in range(E2):
                    k = i * E2 + e
                    act.wait_ge(hid_made, k + 1)
                    if not (isinstance(i, int) and e < 2):
                        act.wait_ge(out_made, k - 1)
                    act.activation(hid[e % 2][:, :, :], hid_ps[e % 2][:, :, :], ACT.Silu).then_inc(hid_ready, 1)

            spans(act, body)

        @block.vector
        def _(dve):
            def body(i):
                X4 = X[:, bass.ds(i * SPAN_TILES, SPAN_TILES), :]
                dve.tensor_copy(part[:, :, :], share[:, bass.ds(i * SPAN_TILES, SPAN_TILES), :])
                dve.tensor_tensor(acc[1][:, :, :], X4, rows3[:, bass.ds(i * SPAN_TILES, SPAN_TILES), :], ALU.add)\
                    .then_inc(summed, 1)
                dve.wait_ge(summed, i + 1)
                for e in range(E2):
                    k = i * E2 + e
                    dve.wait_ge(out_made, k + 1)
                    for t in range(SPAN_TILES):
                        last = dve.scalar_tensor_tensor(acc[e % 2][:, t, :], out_ps[e % 2][:, t, :], part[:, t, e:e + 1],
                                                        acc[1 - e % 2][:, t, :], ALU.mult, ALU.add)
                    last.then_inc(out_read, 1)
                    dve.wait_ge(out_read, k + 1)
                dve.tensor_scalar(X4, acc[1][:, :, :], 1.0, None, ALU.mult).then_inc(step, 1)
                tile_statistics(dve, acc[1], lnst, agg, c["carrier"], stats, i, step)

            spans(dve, body)


def last_norm(nc, ctx, sems, X, stats, rstd, out):
    CHUNK = 8
    made = sems("ln_made")
    stored = sems("stored")
    view = out.rearrange("b (t p) d -> p (b t) d", p=P)
    with nc.Block() as block:

        @block.vector
        def _(dve):
            for t in range(TILES):
                last = dve.tensor_scalar(X[:, t, :], X[:, t, :], stats[:, t, 0:1], rstd[:, t:t + 1],
                                         ALU.subtract, ALU.mult)
                if t % CHUNK == CHUNK - 1:
                    last.then_inc(made, 1)

        @block.sync
        def _(sp):
            for k in range(TILES // CHUNK):
                sp.wait_ge(made, k + 1)
                sp.dma_start(view[:, k * CHUNK:(k + 1) * CHUNK, :], X[:, k * CHUNK:(k + 1) * CHUNK, :])\
                    .then_inc(stored, 16)
            sp.wait_ge(stored, 16 * (TILES // CHUNK))



def build(nc, dram):
    with ExitStack() as ctx:
        def sems(name):
            return ctx.enter_context(nc.semaphore(name))

        def sb(name, shape):
            return ctx.enter_context(nc.sbuf_tensor(name, shape, F32))

        c = constants(nc, ctx, sems)
        c["const_step"] = sems("const_step")
        routed = [sems("routed_" + of) for of in ("rows_ready", "rows_kept", "turned", "rT_ready", "lg_made",
                                                  "lg_read")]
        counted = [sems("mean_square_made"), sems("mean_square_rooted"), 0, 0]
        X = sb("X", [P, TILES, D])
        stats = sb("stats", [P, TILES, 2])
        rstd = sb("rstd", [P, TILES])
        rms = sb("rms", [P, TILES])
        both = sb("both", [P, TILES])
        logits = sb("logits", [P, TILES, E1])
        share = sb("share", [P, TILES, E2])
        rows3 = sb("rows3", [P, TILES, D])
        if "slots" not in dram:
            for name in ("slots", "done"):
                dram[name] = nc.dram_tensor(name, (E1 * CAP, D), F32, kind="Internal").ap()

        def variance(dve, out):
            yield dve.tensor_copy(out[:, :], stats[:, :, 1])

        def square_of_rows(dve, out):
            yield dve.tensor_tensor(out[:, :], rstd[:, :], rstd[:, :], ALU.mult)
            yield dve.tensor_tensor(out[:, :], out[:, :], stats[:, :, 1], ALU.mult)

        def mean_square(dve, out):
            yield dve.tensor_tensor(out[:, :], stats[:, :, 0], stats[:, :, 0], ALU.mult)
            yield dve.tensor_tensor(out[:, :], out[:, :], stats[:, :, 1], ALU.add)

        norm = (variance, rstd, LN_EPS)
        with ExitStack() as inner:
            zero_slots(nc, inner, sems, dram, c)
        with ExitStack() as inner:
            stage1(nc, inner, sems, dram, X, stats, c)
        with ExitStack() as inner:
            inverse_roots(nc, inner, counted, "norm1", [norm])
        with ExitStack() as inner:
            router(nc, inner, sems, routed, 0, "route1", X, stats, rstd, None, True, None, dram["L0_ffn_Wr"], logits, c)
        with ExitStack() as inner:
            stage2(nc, inner, sems, dram, X, stats, logits, c)
        with ExitStack() as inner:
            inverse_roots(nc, inner, counted, "norm2", [norm])
        with ExitStack() as inner:
            softmax_stage(nc, inner, sems, "gqa", X, X, stats, rstd, None, stats, c, gqa(dram["gqa"]))
        with ExitStack() as inner:
            inverse_roots(nc, inner, counted, "norm3", [norm, (square_of_rows, rms, RMS_EPS)])
        with nc.Block() as block:

            @block.vector
            def _(dve):
                dve.tensor_tensor(both[:, :], rstd[:, :], rms[:, :], ALU.mult)

        with ExitStack() as inner:
            softmax_stage(nc, inner, sems, "mla", X, rows3, stats, rstd, both, stats, c, latent(dram["mla"]))
        with ExitStack() as outer:
            hT_all = outer.enter_context(nc.sbuf_tensor("hT_all", [P, B * N], F32))
            with ExitStack() as inner:
                inverse_roots(nc, inner, counted, "norm4", [(mean_square, rms, RMS_EPS)])
            with ExitStack() as inner:
                router(nc, inner, sems, routed, B, "route2", X, None, rms, dram["g2"], False, hT_all, dram["gate_w"], logits, c)
            with ExitStack() as inner:
                choose_two(nc, inner, sems, logits, share)
            with ExitStack() as inner:
                stage5(nc, inner, sems, dram, X, rows3, hT_all, share, stats, c)
        with ExitStack() as inner:
            inverse_roots(nc, inner, counted, "norm5", [norm])
        with ExitStack() as inner:
            last_norm(nc, inner, sems, X, stats, rstd, dram["out"])


def named(given):
    return given | {
        "WqkvT": given["L0_attn_Wqkv"], "WoT": given["L0_attn_Wo"], "g2": given["L1_ffn_g2"],
        "gate_w": given["L1_ffn_gate_w"], "w1": given["L1_ffn_w1"], "w2": given["L1_ffn_w2"],
        "gqa": {n: given["L1_attn_" + n] for n in ("Wq", "Wk", "Wv", "Wo")},
        "mla": {n: given["L1_ffn_" + n] for n in ("Wq", "Wdkv", "Wuk", "Wuv", "Wo", "g1")},
    }


_NAMES = ["L0_attn_x", "L0_attn_Wqkv", "L0_attn_Wo", "L0_ffn_Wr", "L0_ffn_W1", "L0_ffn_W2", "L1_attn_Wq", "L1_attn_Wk",
          "L1_attn_Wv", "L1_attn_Wo", "L1_ffn_g1", "L1_ffn_Wq", "L1_ffn_Wdkv", "L1_ffn_Wuk", "L1_ffn_Wuv", "L1_ffn_Wo",
          "L1_ffn_g2", "L1_ffn_gate_w", "L1_ffn_w1", "L1_ffn_w2"]


def kernel(**inputs):
    import concourse.bacc as _bacc
    from concourse.bass_utils import run_bass_kernel_spmd as _run

    nc = _bacc.Bacc("TRN2", target_bir_lowering=False, num_devices=1)
    arrays, given = {}, {}
    for name in _NAMES:
        a = np.asarray(inputs[name])
        if name in ("L0_attn_Wqkv", "L0_attn_Wo"):
            a = a.T
        if name in ("L1_ffn_g1", "L1_ffn_g2"):
            a = a.reshape(D, 1)
        a = np.ascontiguousarray(a)
        arrays[f"in_{name}"] = a
        given[name] = nc.dram_tensor(f"in_{name}", a.shape, mybir.dt.from_np(a.dtype), kind="ExternalInput").ap()
    given["out"] = nc.dram_tensor("out_0", (B, N, D), F32, kind="ExternalOutput").ap()
    build(nc, named(given))
    r = _run(nc, [arrays], core_ids=[0])
    return r.results[0]["out_0"]
```

```python
from contextlib import ExitStack

import numpy as np
import concourse.bass as bass
from concourse import mybir

F32 = mybir.dt.float32
BF16 = mybir.dt.bfloat16
F16 = mybir.dt.float16
I32 = mybir.dt.int32
U32 = mybir.dt.uint32
ALU = mybir.AluOpType
ACT = mybir.ActivationFunctionType
AX = mybir.AxisListType

P = 128
B, N, D = 32, 256, 128
TILES = B * N // P
H = 16
DH = D // H
LN_EPS = 1e-5
RMS_EPS = 1e-6


def broadcast_last(ap, n):
    return ap.unsqueeze(2).to_broadcast([ap.shape[0], ap.shape[1], n])


def broadcast_middle(ap, n):
    return ap.unsqueeze(1).to_broadcast([ap.shape[0], n, ap.shape[1]])


def constants(nc, ctx, sem):
    c = {}

    def sb(name, shape, dt):
        c[name] = ctx.enter_context(nc.sbuf_tensor(name, shape, dt))
        return c[name]

    sb("ident", [P, P], F32)
    sb("ident_bf", [P, P], BF16)
    sb("ident_h", [P, P], F16)
    sb("far_mask", [P, P], BF16)
    sb("prefix", [P, P], F32)
    sb("ones", [P, P], F32)
    sb("carrier", [P, 1], F32)
    sb("minus_ident_bf", [P, P], BF16)
    sb("head_ones", [P, 4, 4 * DH], F32)
    return c


def make_constants(pool, c, const_step):
    n = 0
    for t, v in ((c["ident"], 0.0), (c["ident_bf"], 0.0), (c["ident_h"], 0.0), (c["far_mask"], 0.0),
                 (c["prefix"], 1.0), (c["ones"], 1.0), (c["minus_ident_bf"], 0.0)):
        pool.memset(t[:, :], v).then_inc(const_step, 1)
        n += 1
    pool.memset(c["head_ones"][:, :, :], 0.0).then_inc(const_step, 1)
    n += 1
    pool.wait_ge(const_step, n)
    for m in range(4):
        pool.memset(c["head_ones"][:, m, m * DH:(m + 1) * DH], 1.0).then_inc(const_step, 1)
    for t in (c["ident"], c["ident_bf"], c["ident_h"]):
        pool.affine_select(out=t[:, :], in_=t[:, :], compare_op=ALU.not_equal, fill=1.0, base=0,
                           pattern=[[-1, P]], channel_multiplier=1).then_inc(const_step, 1)
    pool.affine_select(out=c["minus_ident_bf"][:, :], in_=c["minus_ident_bf"][:, :], compare_op=ALU.not_equal,
                       fill=-1.0, base=0, pattern=[[-1, P]], channel_multiplier=1).then_inc(const_step, 1)
    pool.affine_select(out=c["far_mask"][:, :], in_=c["far_mask"][:, :], compare_op=ALU.is_ge, fill=1e28,
                       base=0, pattern=[[-1, P]], channel_multiplier=1).then_inc(const_step, 1)
    pool.affine_select(out=c["prefix"][:, :], in_=c["prefix"][:, :], compare_op=ALU.is_ge, fill=0.0,
                       base=0, pattern=[[1, P]], channel_multiplier=-1).then_inc(const_step, 1)
    n += 4 + 6
    return n


CONSTANTS = 8 + 4 + 6


def tile_statistics(dve, rows, lnst, agg, carrier, stats, n, step):
    tiles = rows.shape[1]
    dve.wait_ge(step, n * 4 + 1)
    for t in range(tiles):
        last = dve.bn_stats(lnst[:, t, :], rows[:, t, :])
    last.then_inc(step, 1)
    dve.wait_ge(step, n * 4 + 2)
    dve.memset(carrier[:, :], 0.0)
    for t in range(tiles):
        last = dve.bn_aggr(agg[:, t, :], lnst[:, t, :])
    last.then_inc(step, 1)
    dve.wait_ge(step, n * 4 + 3)
    dve.tensor_scalar(stats[:, bass.ds(n * tiles, tiles), :], agg[:, :, :], 1.0, None, ALU.mult).then_inc(step, 1)




CHUNKS = [[(0, 0, 8), (1, 0, 4), (1, 4, 4)], [(0, 8, 8), (1, 8, 4), (1, 12, 4)]]
SLOTS, GROUPS = 3, 2
NEWTON = 4
LENGTH = NEWTON + 3
OFFSETS = (0, 3, 5)
STEPS1 = GROUPS * LENGTH
TURN_X, MAKE_QK, NORMALISE, PROJECT_OUT, MAKE_V = 1, 2, 5, 6, 8
BANK = 512


def standing(h):
    return h % 4 * 4 + h // 4


def slots_at(step):
    out = []
    for s in range(SLOTS):
        local = step - OFFSETS[s]
        back = 1 if local < 0 else 0
        g, phase = divmod(local + back * STEPS1, LENGTH)
        out.append((s, back, g, phase))
    return out


def stage1(nc, ctx, sems, dram, X, stats, c):
    def sb(name, shape, dt=F32):
        return ctx.enter_context(nc.sbuf_tensor("s1_" + name, shape, dt))

    def sem(name):
        return sems("s1_" + name)

    wqkv = sb("wqkv", [P, 3 * D])
    wo = sb("wo", [P, D])
    xin = [sb(f"xin{u}", [P, 2, D]) for u in range(2)]
    xres = [sb(f"xres{u}", [P, 2, D]) for u in range(2)]
    xT = sb("xT", [P, N])
    qT = [sb(f"qT{u}", [P, N]) for u in range(2)]
    kT = [sb(f"kT{u}", [P, N]) for u in range(2)]
    kM = [sb(f"kM{u}", [P, H, N]) for u in range(2)]
    vM = [sb(f"vM{u}", [P, 2, 4, 4 * (4 * DH + DH)]) for u in range(2)]
    root = [sb(f"root{s}", [P, 1024]) for s in range(SLOTS)]
    w = [sb(f"w{s}", [P, 1024]) for s in range(SLOTS)]
    wT = [sb(f"wT{s}", [P, 1024]) for s in range(SLOTS)]
    low = [sb(f"low{s}", [P, 8]) for s in range(SLOTS)]
    lam = [sb(f"lam{s}", [P, 8]) for s in range(SLOTS)]
    st = [sb(f"st{s}", [P, 8, 3]) for s in range(SLOTS)]
    sq = [sb(f"sq{s}", [P, 8]) for s in range(SLOTS)]
    s2 = [sb(f"s2{s}", [P, 8]) for s in range(SLOTS)]
    rs2 = [sb(f"rs2{s}", [P, 8]) for s in range(SLOTS)]
    step_at = [sb(f"step{s}", [P, 8]) for s in range(SLOTS)]
    step_hi = [sb(f"step_hi{s}", [P, 8], F16) for s in range(SLOTS)]
    step_lo = [sb(f"step_lo{s}", [P, 8], F16) for s in range(SLOTS)]
    root_sums = sb("root_sums", [P, N])
    rsums = sb("rsums", [P, N])
    mend, o1 = sb("mend", [P, N]), sb("o1", [P, N])
    oT = sb("oT", [P, N])
    total = sb("total", [P, 2, D])
    lnst = sb("lnst", [P, 2, 6])
    agg = sb("agg", [P, 2, 2])
    dist = [ctx.enter_context(nc.psum_tensor(f"s1_dist{s}", [P, 2 * BANK], F32)) for s in range(SLOTS)]
    work = ctx.enter_context(nc.psum_tensor("s1_work", [P, BANK], F32))
    heads_out = ctx.enter_context(nc.psum_tensor("s1_heads_out", [P, 2, N], F32))

    def each_slot(name):
        return [sem(f"{name}{s}") for s in range(SLOTS)]

    weights_loaded = sem("weights_loaded")
    zeroed = sem("zeroed")
    x_loaded = [sem(f"x_loaded{u}") for u in range(2)]
    xres_loaded = [sem(f"xres_loaded{u}") for u in range(2)]
    x_turned = sem("x_turned")
    xT_ready = sem("xT_ready")
    qk_made = sem("qk_made")
    q_ready = sem("q_ready")
    k_ready = sem("k_ready")
    k_spread = [sem(f"k_spread{u}") for u in range(2)]
    v_made = sem("v_made")
    v_ready = sem("v_ready")
    scores_ready = each_slot("scores_ready")
    lam_ready = each_slot("lam_ready")
    hi_ready = each_slot("hi_ready")
    lo_ready = each_slot("lo_ready")
    dist_ready = each_slot("dist_ready")
    root_ready = each_slot("root_ready")
    w0_ready = each_slot("w0_ready")
    w1_ready = each_slot("w1_ready")
    w_turned = each_slot("w_turned")
    wT_ready = each_slot("wT_ready")
    dve_step = each_slot("dve_step")
    root_sums_ready = sem("root_sums_ready")
    rsums_ready = sem("rsums_ready")
    scaled = sem("scaled")
    heads_made = sem("heads_made")
    o_ready = sem("o_ready")
    out_made = sem("out_made")
    added = sem("added")
    ln_step = sem("ln_step")

    CHUNK_STEPS = 1 + 4 * NEWTON

    ZERO_ROWS = 10
    ZERO_DMAS = dram["slots"].shape[0] // (ZERO_ROWS * P)
    slots = dram["slots"].rearrange("(c p r) d -> c p (r d)", p=P, r=ZERO_ROWS)
    slot_zeros = sb("slot_zeros", [P, ZERO_ROWS * D])
    slot_zeros_ready = sem("slot_zeros_ready")
    slots_zeroed = sem("slots_zeroed")

    def keys_of(g, s):
        return (CHUNKS[g][s][0] + 1) * P

    def per_head(ap, keys):
        return ap.rearrange("p (h k) -> p h k", k=keys)

    def paired(ap, keys):
        return ap.rearrange("p (a k t) -> p a t k", k=keys, t=2)

    def unpaired(ap, keys):
        return ap.rearrange("p (a t k) -> p a t k", k=keys, t=2)

    def bodies(eng, body):
        body(0, 0, 0, True, False)
        body(1, 1, 0, False, False)
        with eng.Fori(1, B // 2 - 1) as i:
            body(i * 2, 0, i, False, False)
            body(i * 2 + 1, 1, i, False, False)
        body(B - 2, 0, B // 2 - 1, False, False)
        body(B - 1, 1, B // 2 - 1, False, True)
        body(B, 0, B // 2, False, True)

    def active(n, u, step, first):
        for s, back, g, phase in slots_at(step):
            if (first and back) or (isinstance(n, int) and n == B and not back):
                continue
            m = n - back
            yield s, m * GROUPS + g, m, (u + back) % 2, g, phase

    def ended(n, step):
        return isinstance(n, int) and n == B and step > PROJECT_OUT

    with nc.Block() as block:

        @block.gpsimd
        def _(pool):
            make_constants(pool, c, c["const_step"])
            pool.memset(kM[1][:, :, :], 0.0)
            pool.memset(vM[1][:, :, :, :], 0.0).then_inc(zeroed, 1)

            def body(n, u, i, first, last):
                for step in range(STEPS1):
                    if ended(n, step):
                        break
                    for s, use, m, v, g, phase in active(n, u, step, first):
                        if 1 <= phase <= NEWTON + 1:
                            keys = keys_of(g, s)
                            r = unpaired(root[s][:, BANK:], keys)
                            pool.wait_ge(root_ready[s], (use * (NEWTON + 1) + phase) * 2 - 1)
                            pool.tensor_tensor(paired(w[s][:, BANK:], keys), r, r, ALU.mult).then_inc(w1_ready[s], 1)

            bodies(pool, body)

        @block.sync
        def _(sp):
            sp.dma_start(wqkv[:, :], dram["WqkvT"]).then_inc(weights_loaded, 16)
            sp.dma_start(wo[:, :], dram["WoT"]).then_inc(weights_loaded, 16)
            src = dram["L0_attn_x"].rearrange("b (t p) d -> b p t d", p=P)
            for u in range(2):
                sp.dma_start(xin[u][:, :, :], src[u]).then_inc(x_loaded[u], 16)
                sp.dma_start(xres[u][:, :, :], src[u]).then_inc(xres_loaded[u], 16)
            sp.wait_ge(zeroed, 2)

            def spread(n, u):
                sp.wait_ge(k_ready, n + 1)
                for h in range(H):
                    rows = slice(h * DH, (h + 1) * DH)
                    sp.dma_start(kM[u][rows, standing(h), :], kT[u][rows, :]).then_inc(k_spread[u], 16)

            def load(n, u):
                x = src[bass.ds(n, 1)].squeeze(0)
                sp.wait_ge(x_turned, n - 1)
                sp.dma_start(xin[u][:, :, :], x).then_inc(x_loaded[u], 16)

            def load_res(n, u):
                x = src[bass.ds(n, 1)].squeeze(0)
                sp.wait_ge(added, n - 1)
                sp.dma_start(xres[u][:, :, :], x).then_inc(xres_loaded[u], 16)

            spread(0, 0)
            load(2, 0)
            spread(1, 1)
            load(3, 1)
            with sp.Fori(1, B // 2 - 1) as i:
                for u in range(2):
                    spread(i * 2 + u, u)
                    load_res(i * 2 + u, u)
                    load(i * 2 + u + 2, u)
            for n in (B - 2, B - 1):
                spread(n, n % 2)
                load_res(n, n % 2)
            sp.wait_ge(slot_zeros_ready, 1)
            for k in range(ZERO_DMAS):
                sp.dma_start(slots[k], slot_zeros[:, :]).then_inc(slots_zeroed, 16)
            sp.wait_ge(slots_zeroed, 16 * ZERO_DMAS)

        @block.tensor
        def _(pe):
            pe.wait_ge(weights_loaded, 32)
            pe.wait_ge(c["const_step"], CONSTANTS)

            def turn_x(n, u, loads):
                pe.wait_ge(x_loaded[u], loads * 16)
                if not (isinstance(n, int) and n == 0):
                    pe.wait_ge(v_ready, n)
                for t in range(2):
                    last = pe.transpose(work[:, t * P:(t + 1) * P], xin[u][:, t, :], c["ident"][:, :])
                last.then_inc(x_turned, 1)

            def make_qk(n):
                pe.wait_ge(xT_ready, n + 1)
                for j in range(2):
                    last = pe.matmul(work[:, j * N:(j + 1) * N], wqkv[:, j * D:(j + 1) * D], xT[:, :],
                                     start=True, stop=True)
                last.then_inc(qk_made, 1)

            def make_v(n, start):
                if start:
                    pe.wait_ge(q_ready, n + 1)
                    pe.wait_ge(k_ready, n + 1)
                else:
                    pe.wait_ge(added, n - 1)
                for t in range(2):
                    last = pe.matmul(work[:, t * D:(t + 1) * D], xT[:, t * P:(t + 1) * P], wqkv[:, 2 * D:],
                                     start=True, stop=True)
                last.then_inc(v_made, 1)

            def project_out(n, last_one):
                pe.wait_ge(o_ready, n + 1)
                if not last_one:
                    pe.wait_ge(q_ready, n + 3)
                    pe.wait_ge(k_ready, n + 3)
                for t in range(2):
                    last = pe.matmul(work[:, t * D:(t + 1) * D], oT[:, t * P:(t + 1) * P], wo[:, :],
                                     start=True, stop=True)
                last.then_inc(out_made, 1)

            def weigh_values(n, u, g, s, use, start):
                half, h0, nh = CHUNKS[g][s]
                pe.wait_ge(wT_ready[s], use + 1)
                pe.wait_ge(v_ready, n + 1)
                begins = g == 0 and s == 0
                if begins and not start:
                    pe.wait_ge(o_ready, n)
                for kb in range(half + 1):
                    for a in range(nh):
                        m, group = divmod(h0 + a, 4)
                        col = (a * (half + 1) + kb) * P
                        rows = slice(32 * group, 32 * group + 32)
                        for which, values in enumerate((vM[u][:, kb, group, 32 * m:32 * m + 32],
                                                        c["head_ones"][:, m, :])):
                            last = pe.matmul(heads_out[rows, which, half * P:(half + 1) * P], values,
                                             wT[s][:, col:col + P], start=(begins and a < 4 and which == 0),
                                             stop=False, tile_position=(0, 32 * group), skip_group_check=True)
                if g == GROUPS - 1 and s == SLOTS - 1:
                    last.then_inc(heads_made, 1)

            def score(n, u, g, s, spreads):
                half, h0, nh = CHUNKS[g][s]
                keys = keys_of(g, s)
                pe.wait_ge(q_ready, n + 1)
                pe.wait_ge(k_spread[u], spreads * 16 * H)
                per = BANK // keys
                for bank in range(2):
                    pe.matmul(dist[s][:, bank * BANK:(bank + 1) * BANK], qT[u][:, half * P:(half + 1) * P],
                              kM[u][:, h0 + bank * per:h0 + (bank + 1) * per, 0:keys],
                              start=True, stop=False, skip_group_check=True)
                    out = per_head(dist[s][:, bank * BANK:(bank + 1) * BANK], keys)
                    last = pe.matmul(out[:, :, keys - P:keys], c["ident_bf"][:, :],
                                     broadcast_middle(c["far_mask"][:, :], per),
                                     start=False, stop=False, skip_group_check=True)
                last.then_inc(scores_ready[s], 1)

            def move(g, s, identity, values, bank):
                keys = keys_of(g, s)
                per = BANK // keys
                return pe.matmul(per_head(dist[s][:, bank * BANK:(bank + 1) * BANK], keys), identity[:, :],
                                 broadcast_last(values[:, bank * per:(bank + 1) * per], keys),
                                 start=False, stop=False, skip_group_check=True)

            def body(n, u, i, first, last):
                for step in range(STEPS1):
                    if ended(n, step):
                        break
                    for s, use, m, v, g, phase in active(n, u, step, first):
                        if phase == 0:
                            if g or not first:
                                pe.wait_ge(wT_ready[s], use)
                            score(m, v, g, s, i if v != u and not u else i + 1)
                        elif phase == 1:
                            pe.wait_ge(lam_ready[s], use + 1)
                            for bank in (1, 0):
                                move(g, s, c["ident"], lam[s], bank).then_inc(dist_ready[s], 1)
                        elif phase <= NEWTON + 1:
                            pe.wait_ge(hi_ready[s], use * NEWTON + phase - 1)
                            for bank in (1, 0):
                                move(g, s, c["ident_h"], step_hi[s], bank)
                            pe.wait_ge(lo_ready[s], use * NEWTON + phase - 1)
                            for bank in (1, 0):
                                move(g, s, c["ident_h"], step_lo[s], bank).then_inc(dist_ready[s], 1)
                        else:
                            keys = keys_of(g, s)
                            pe.wait_ge(w0_ready[s], (use + 1) * (NEWTON + 1))
                            pe.wait_ge(w1_ready[s], (use + 1) * (NEWTON + 1))
                            wv = w[s][:, :].rearrange("p (a k t) -> p a t k", k=keys, t=2)
                            for b in range(8):
                                h, kb = divmod(b, keys // P)
                                last_one = pe.transpose(dist[s][:, b * P:(b + 1) * P],
                                                        wv[:, h // 2, h % 2, kb * P:(kb + 1) * P], c["ident"][:, :])
                            last_one.then_inc(w_turned[s], 1)
                    for s, use, m, v, g, phase in active(n, u, step, first):
                        if phase == 0:
                            if g:
                                weigh_values(m, v, 0, s, use - 1, first and m is n)
                            elif not first:
                                weigh_values(m - 1, 1 - v, 1, s, use - 1, False)
                    if isinstance(n, int) and n == B and step in [OFFSETS[s] for s in range(SLOTS)]:
                        s = OFFSETS.index(step)
                        weigh_values(B - 1, 1 - u, 1, s, B * GROUPS - 1, False)
                    if step == TURN_X and not last:
                        turn_x(n + 1, 1 - u, i + 1 + u)
                    if step == MAKE_QK and not last:
                        make_qk(n + 1)
                    if step == PROJECT_OUT and not first:
                        project_out(n - 1, last)
                    if step == MAKE_V and not last:
                        make_v(n + 1, first)

            turn_x(0, 0, 1)
            make_qk(0)
            make_v(0, True)
            bodies(pe, body)

        @block.scalar
        def _(act):
            def take_x(n):
                act.wait_ge(x_turned, n + 1)
                act.activation(xT[:, :], work[:, 0:N], ACT.Copy).then_inc(xT_ready, 1)

            def take_q(n, u):
                act.wait_ge(qk_made, n + 1)
                act.activation(qT[u][:, :], work[:, 0:N], ACT.Copy, scale=-float(DH) ** -0.5).then_inc(q_ready, 1)

            def take_v(n, u):
                act.wait_ge(v_made, n + 1)
                for t in range(2):
                    strips = vM[u][:, t, :, :].rearrange("p g (m c) -> p g m c", m=4)
                    last = act.activation(strips[:, :, :, 0:DH],
                                          work[:, t * D:(t + 1) * D].rearrange("p (g m d) -> p g m d", g=4, m=4),
                                          ACT.Copy)
                last.then_inc(v_ready, 1)

            def invert_sums(n):
                act.wait_ge(heads_made, n + 1)
                act.activation(root_sums[:, :], heads_out[:, 1, :], ACT.Abs_reciprocal_sqrt).then_inc(root_sums_ready, 1)
                act.wait_ge(root_sums_ready, n + 1)
                act.activation(rsums[:, :], root_sums[:, :], ACT.Square).then_inc(rsums_ready, 1)

            def roots(k, s):
                for j, bank in enumerate((1, 0)):
                    act.wait_ge(dist_ready[s], k * 2 - 1 + j)
                    part = slice(bank * BANK, (bank + 1) * BANK)
                    act.activation(root[s][:, part], dist[s][:, part], ACT.Abs_reciprocal_sqrt)\
                        .then_inc(root_ready[s], 1)

            def square(k, s, keys):
                act.wait_ge(root_ready[s], k * 2)
                act.activation(paired(w[s][:, 0:BANK], keys), unpaired(root[s][:, 0:BANK], keys), ACT.Square)\
                    .then_inc(w0_ready[s], 1)

            def body(n, u, i, first, last):
                for step in range(STEPS1):
                    if ended(n, step):
                        break
                    for s, use, m, v, g, phase in active(n, u, step, first):
                        if 1 <= phase <= NEWTON + 1:
                            roots(use * (NEWTON + 1) + phase, s)
                            square(use * (NEWTON + 1) + phase, s, keys_of(g, s))
                        elif phase == LENGTH - 1:
                            act.wait_ge(w_turned[s], use + 1)
                            act.activation(wT[s][:, :], dist[s][:, :], ACT.Copy).then_inc(wT_ready[s], 1)
                    if step == TURN_X and not last:
                        take_x(n + 1)
                    if step == MAKE_QK and not last:
                        take_q(n + 1, 1 - u)
                    if step == NORMALISE and not first:
                        invert_sums(n - 1)
                    if step == MAKE_V and not last:
                        take_v(n + 1, 1 - u)

            take_x(0)
            take_q(0, 0)
            act.wait_ge(zeroed, 2)
            take_v(0, 0)
            bodies(act, body)

        @block.vector
        def _(dve):
            def settle(s, use, count, ins):
                ins.then_inc(dve_step[s], 1)
                dve.wait_ge(dve_step[s], use * CHUNK_STEPS + count)

            def take_k(n, u):
                dve.wait_ge(q_ready, n + 1)
                dve.tensor_copy(kT[u][:, :], work[:, N:2 * N]).then_inc(k_ready, 1)

            def first_lambda(use, g, s):
                nh = CHUNKS[g][s][2]
                dve.wait_ge(scores_ready[s], use + 1)
                settle(s, use, 1, dve.tensor_reduce(low[s][:, 0:nh], per_head(dist[s][:, :], keys_of(g, s)),
                                                    AX.X, ALU.min))
                dve.tensor_scalar(lam[s][:, 0:nh], low[s][:, 0:nh], -1.0, 1.0, ALU.mult, ALU.add)\
                    .then_inc(lam_ready[s], 1)

            def moments(use, g, s, phase):
                keys = keys_of(g, s)
                pairs = BANK // (2 * keys)
                k = use * (NEWTON + 1) + phase
                for bank, ready in enumerate((w0_ready, w1_ready)):
                    for a in range(pairs):
                        if a == 0:
                            dve.wait_ge(ready[s], k)
                        at = bank * pairs + a
                        last = dve.bn_stats(st[s][:, 2 * at:2 * at + 2, :].rearrange("p h c -> p (h c)"),
                                            w[s][:, at * 2 * keys:(at + 1) * 2 * keys])
                return last

            def newton(use, g, s, phase):
                nh, keys = CHUNKS[g][s][2], keys_of(g, s)
                at = 1 + 4 * (phase - 1)
                mean, spread = st[s][:, 0:nh, 1], st[s][:, 0:nh, 2]
                settle(s, use, at + 1, moments(use, g, s, phase))
                settle(s, use, at + 2, dve.tensor_tensor(sq[s][:, 0:nh], mean, mean, ALU.mult))
                settle(s, use, at + 3, dve.scalar_tensor_tensor(s2[s][:, 0:nh], spread, 1.0 / keys, sq[s][:, 0:nh],
                                                                ALU.mult, ALU.add))
                settle(s, use, at + 4, dve.reciprocal(rs2[s][:, 0:nh], s2[s][:, 0:nh]))
                dve.scalar_tensor_tensor(step_at[s][:, 0:nh], mean, -1.0 / keys, rs2[s][:, 0:nh], ALU.add, ALU.mult)
                dve.scalar_tensor_tensor(step_hi[s][:, 0:nh], mean, -1.0 / keys, rs2[s][:, 0:nh], ALU.add, ALU.mult)\
                    .then_inc(hi_ready[s], 1)
                dve.wait_ge(hi_ready[s], use * NEWTON + phase)
                dve.tensor_tensor(step_lo[s][:, 0:nh], step_at[s][:, 0:nh], step_hi[s][:, 0:nh],
                                  ALU.subtract).then_inc(lo_ready[s], 1)

            def normalise(n):
                dve.wait_ge(rsums_ready, n + 1)
                dve.scalar_tensor_tensor(mend[:, :], heads_out[:, 1, :], -1.0, rsums[:, :], ALU.mult, ALU.mult)
                dve.tensor_tensor(o1[:, :], heads_out[:, 0, :], rsums[:, :], ALU.mult).then_inc(scaled, 1)
                dve.wait_ge(scaled, n + 1)
                dve.scalar_tensor_tensor(oT[:, :], mend[:, :], 2.0, o1[:, :], ALU.add, ALU.mult).then_inc(o_ready, 1)

            def add(n, u, loads):
                dve.wait_ge(out_made, n + 1)
                dve.wait_ge(xres_loaded[u], loads * 16)
                attended = work[:, 0:2 * D].rearrange("p (t d) -> p t d", t=2)
                dve.tensor_tensor(total[:, :, :], attended, xres[u][:, :, :], ALU.add).then_inc(ln_step, 1)
                dve.tensor_tensor(X[:, bass.ds(n * 2, 2), :], attended, xres[u][:, :, :], ALU.add).then_inc(added, 1)
                tile_statistics(dve, total, lnst, agg, c["carrier"], stats, n, ln_step)

            def body(n, u, i, first, last):
                for step in range(STEPS1):
                    if ended(n, step):
                        break
                    for s, use, m, v, g, phase in active(n, u, step, first):
                        if phase == 0:
                            first_lambda(use, g, s)
                        elif phase <= NEWTON:
                            newton(use, g, s, phase)
                    if step == MAKE_QK and not last:
                        take_k(n + 1, 1 - u)
                    if step == NORMALISE and not first:
                        normalise(n - 1)
                    if step == PROJECT_OUT and not first:
                        add(n - 1, 1 - u, i + u)

            dve.memset(kM[0][:, :, :], 0.0)
            dve.memset(vM[0][:, :, :, :], 0.0).then_inc(zeroed, 1)
            dve.memset(slot_zeros[:, :], 0.0).then_inc(slot_zeros_ready, 1)
            take_k(0, 0)
            bodies(dve, body)



def inverse_roots(nc, ctx, counted, name, chains):
    ends = []
    made, rooted, before, rooted_before = counted
    shift = [ctx.enter_context(nc.sbuf_tensor(f"{name}_shift{i}", [P, TILES], F32)) for i in range(len(chains))]
    with nc.Block() as block:

        @block.vector
        def _(dve):
            n = before
            for i, (source, out, eps) in enumerate(chains):
                if i:
                    dve.wait_ge(rooted, rooted_before + i)
                for ins in source(dve, shift[i]):
                    n += 1
                    ins.then_inc(made, 1)
                    dve.wait_ge(made, n)
                n += 1
                dve.tensor_scalar(shift[i][:, :], shift[i][:, :], eps, None, ALU.add).then_inc(made, 1)
                ends.append(n)

        @block.scalar
        def _(act):
            for i, (source, out, eps) in enumerate(chains):
                act.wait_ge(made, ends[i])
                act.activation(out[:, :], shift[i][:, :], ACT.Abs_reciprocal_sqrt).then_inc(rooted, 1)

    counted[2:] = ends[-1], rooted_before + len(chains)



def router(nc, ctx, sems, counted, base, name, X, centre, scale, gain, keep_rows, hT_all, weights, logits, c):
    def sb(n, shape, dt=F32):
        return ctx.enter_context(nc.sbuf_tensor(f"{name}_{n}", shape, dt))

    E = weights.shape[1]
    wr = sb("wr", [P, E])
    rows = [sb(f"rows{u}", [P, 2, D]) for u in range(2)]
    rT = [sb(f"rT{u}", [P, N]) for u in range(2)]
    gcol = sb("gcol", [P, 1]) if gain is not None else None
    turn = [ctx.enter_context(nc.psum_tensor(f"{name}_turn{u}", [P, 512], F32)) for u in range(2)]
    lg = [ctx.enter_context(nc.psum_tensor(f"{name}_lg{u}", [P, 2, E], F32)) for u in range(2)]
    loaded = sems(name + "_loaded")
    rows_ready, rows_kept, turned, rT_ready, lg_made, lg_read = counted
    NB = B

    def pairs(eng, body):
        body(0, 0, True)
        body(1, 1, True)
        with eng.Fori(1, NB // 2) as i:
            body(i * 2, 0, False)
            body(i * 2 + 1, 1, False)

    with nc.Block() as block:

        @block.sync
        def _(sp):
            sp.dma_start(wr[:, :], weights).then_inc(loaded, 16)
            if gain is not None:
                sp.dma_start(gcol[:, :], gain).then_inc(loaded, 16)

        @block.vector
        def _(dve):
            def normalise(n, u, first):
                if not first:
                    dve.wait_ge(turned, base + n - 1)
                    if keep_rows:
                        dve.wait_ge(rows_kept, n - 1)
                for t in range(2):
                    tile = n * 2 + t
                    x = X[:, bass.ds(tile, 1), :].squeeze(1)
                    s = scale[:, bass.ds(tile, 1)]
                    if centre is None:
                        last = dve.tensor_scalar(rows[u][:, t, :], x, s, None, ALU.mult)
                    else:
                        last = dve.tensor_scalar(rows[u][:, t, :], x, centre[:, bass.ds(tile, 1), 0], s,
                                                 ALU.subtract, ALU.mult)
                last.then_inc(rows_ready, 1)

            def body(n, u, more=True):
                if more:
                    normalise(n + 2, u, False)
                dve.wait_ge(lg_made, base + n + 1)
                dve.tensor_scalar(logits[:, bass.ds(n * 2, 2), :], lg[u][:, :, :], 1.0, None, ALU.mult)\
                    .then_inc(lg_read, 1)

            normalise(0, 0, True)
            normalise(1, 1, True)
            with dve.Fori(0, NB // 2 - 1) as i:
                body(i * 2, 0)
                body(i * 2 + 1, 1)
            body(NB - 2, 0, False)
            body(NB - 1, 1, False)

        @block.gpsimd
        def _(pool):
            def body(n, u, first):
                if keep_rows:
                    pool.wait_ge(rows_ready, base + n + 1)
                    pool.tensor_copy(X[:, bass.ds(n * 2, 2), :], rows[u][:, :, :]).then_inc(rows_kept, 1)
            if keep_rows:
                pairs(pool, body)

        @block.tensor
        def _(pe):
            pe.wait_ge(loaded, 32 if gain is not None else 16)

            def turn_rows(n, u, first):
                pe.wait_ge(rows_ready, base + n + 1)
                if not first:
                    pe.wait_ge(rT_ready, base + n - 1)
                for t in range(2):
                    last = pe.transpose(turn[u][:, t * P:(t + 1) * P], rows[u][:, t, :], c["ident"][:, :])
                last.then_inc(turned, 1)

            def make_logits(n, u, first):
                if not first:
                    pe.wait_ge(lg_read, base + n - 1)
                pe.wait_ge(rT_ready, base + n + 1)
                for t in range(2):
                    last = pe.matmul(lg[u][:, t, :], rT[u][:, t * P:(t + 1) * P], wr[:, :], start=True, stop=True)
                last.then_inc(lg_made, 1)

            turn_rows(0, 0, True)
            turn_rows(1, 1, True)
            make_logits(0, 0, True)
            turn_rows(2, 0, False)
            make_logits(1, 1, True)
            with pe.Fori(1, NB // 2 - 1) as i:
                for u in range(2):
                    turn_rows(i * 2 + u + 1, 1 - u, False)
                    make_logits(i * 2 + u, u, False)
            turn_rows(NB - 1, 1, False)
            make_logits(NB - 2, 0, False)
            make_logits(NB - 1, 1, False)

        @block.scalar
        def _(act):
            act.wait_ge(loaded, 32 if gain is not None else 16)

            def body(n, u, first):
                if not first:
                    act.wait_ge(lg_made, base + n - 1)
                act.wait_ge(turned, base + n + 1)
                g = gcol[:, 0:1] if gain is not None else 1.0
                act.activation(rT[u][:, :], turn[u][:, 0:N], ACT.Identity, scale=g).then_inc(rT_ready, 1)
                if hT_all is not None:
                    act.wait_ge(rT_ready, base + n + 1)
                    act.activation(hT_all[:, bass.ds(n * N, N)], rT[u][:, :], ACT.Copy)

            pairs(act, body)



E1 = 8
F1 = 512
CAP = int(1.25 * B * N / E1)
ROWS = 256
FAR = float(1 << 20)


def stage2(nc, ctx, sems, dram, X, stats, logits, c):
    def sb(name, shape, dt=F32):
        return ctx.enter_context(nc.sbuf_tensor("s2_" + name, shape, dt))

    def ps(name, shape):
        return ctx.enter_context(nc.psum_tensor("s2_" + name, shape, F32))

    T = TILES
    best = sb("best", [P, T])
    eq = sb("eq", [P, T, E1])
    hot = sb("hot", [P, T, E1])
    shifted = sb("shifted", [P, T, E1])
    tot = sb("tot", [P, T, E1])
    upto = sb("upto", [P, T, E1])
    place = sb("place", [P, T, E1])
    rank = sb("rank", [P, T])
    pos = sb("pos", [P, T])
    first_slot = sb("first_slot", [P, T])
    kept = sb("kept", [P, T])
    total = sb("total", [P, T])
    factor = sb("factor", [P, T])
    slot = sb("slot", [P, T])
    slot_u = sb("slot_u", [P, T], U32)
    early = sb("early", [P, E1])
    begin = sb("begin", [P, E1])
    unit = sb("unit", [P, T])
    cum_ps = ps("cum_ps", [P, T, E1])
    tot_ps = ps("tot_ps", [P, T, E1])
    col = sems("s2_col")
    hot_ready = sems("s2_hot_ready")
    sums_made = sems("s2_sums_made")
    shifted_ready = sems("s2_shifted_ready")
    exp_ready = sems("s2_exp_ready")
    step = sems("s2_step")

    with nc.Block() as block:

        @block.gpsimd
        def _(pool):
            pool.iota(early[:, :], pattern=[[-1, E1]], base=E1, channel_multiplier=0,
                      allow_small_or_imprecise_dtypes=True).then_inc(col, 1)
            pool.iota(begin[:, :], pattern=[[CAP, E1]], base=0, channel_multiplier=0,
                      allow_small_or_imprecise_dtypes=True).then_inc(col, 1)

        @block.tensor
        def _(pe):
            pe.wait_ge(hot_ready, 1)
            flat = hot[:, :, :].rearrange("p t e -> p (t e)")
            pe.matmul(cum_ps[:, :, :].rearrange("p t e -> p (t e)"), c["prefix"][:, :], flat, start=True, stop=True)
            pe.matmul(tot_ps[:, :, :].rearrange("p t e -> p (t e)"), c["ones"][:, :], flat, start=True, stop=True)\
                .then_inc(sums_made, 1)

        @block.scalar
        def _(act):
            act.wait_ge(shifted_ready, 1)
            act.activation(shifted[:, :, :], shifted[:, :, :], ACT.Exp).then_inc(exp_ready, 1)

        @block.vector
        def _(dve):
            n = [0]

            def settle(ins):
                n[0] += 1
                ins.then_inc(step, 1)
                dve.wait_ge(step, n[0])

            by_tile = lambda t: broadcast_last(t[:, :], E1)
            dve.memset(unit[:, :], 1.0)
            settle(dve.tensor_reduce(best[:, :], logits[:, :, :], AX.X, ALU.max))
            dve.tensor_tensor(shifted[:, :, :], logits[:, :, :], by_tile(best), ALU.subtract)\
                .then_inc(shifted_ready, 1)
            settle(dve.tensor_tensor(eq[:, :, :], logits[:, :, :], by_tile(best), ALU.is_equal))
            dve.wait_ge(col, 2)
            settle(dve.tensor_tensor(eq[:, :, :], eq[:, :, :], broadcast_middle(early[:, :], T), ALU.mult))
            settle(dve.tensor_reduce(rank[:, :], eq[:, :, :], AX.X, ALU.max))
            settle(dve.tensor_tensor(hot[:, :, :], eq[:, :, :], by_tile(rank), ALU.is_equal))
            dve.sem_inc(hot_ready, 1)
            dve.wait_ge(sums_made, 1)
            settle(dve.tensor_copy(tot[:, :, :], tot_ps[:, :, :]))
            for e in range(E1):
                last = dve.tensor_tensor_scan(upto[:, :, e], unit[:, :], tot[:, :, e], 0.0, ALU.mult, ALU.add)
            settle(last)
            settle(dve.tensor_tensor(upto[:, :, :], upto[:, :, :], tot[:, :, :], ALU.subtract))
            settle(dve.tensor_tensor(place[:, :, :], upto[:, :, :], cum_ps[:, :, :], ALU.add))
            settle(dve.tensor_tensor(place[:, :, :], place[:, :, :], hot[:, :, :], ALU.mult))
            settle(dve.tensor_reduce(pos[:, :], place[:, :, :], AX.X, ALU.add))
            settle(dve.tensor_tensor(eq[:, :, :], hot[:, :, :], broadcast_middle(begin[:, :], T), ALU.mult))
            settle(dve.tensor_reduce(first_slot[:, :], eq[:, :, :], AX.X, ALU.add))
            settle(dve.tensor_scalar(kept[:, :], pos[:, :], float(CAP), None, ALU.is_le))
            settle(dve.scalar_tensor_tensor(slot[:, :], pos[:, :], FAR - 1.0, first_slot[:, :], ALU.add, ALU.add))
            settle(dve.scalar_tensor_tensor(slot[:, :], kept[:, :], -FAR, slot[:, :], ALU.mult, ALU.add))
            settle(dve.tensor_copy(slot_u[:, :], slot[:, :]))
            dve.wait_ge(exp_ready, 1)
            settle(dve.tensor_reduce(total[:, :], shifted[:, :, :], AX.X, ALU.add))
            settle(dve.reciprocal(factor[:, :], total[:, :]))
            settle(dve.scalar_tensor_tensor(factor[:, :], factor[:, :], -1.0, kept[:, :], ALU.add, ALU.mult))
            settle(dve.tensor_scalar(factor[:, :], factor[:, :], 1.0, None, ALU.add))

    slots, done = dram["slots"], dram["done"]
    dispatched = sems("s2_dispatched")
    with nc.Block() as block:

        @block.gpsimd
        def _(pool):
            for t in range(T):
                pool.indirect_dma_start(slots, bass.IndirectOffsetOnAxis(ap=slot_u[:, t:t + 1], axis=0), X[:, t, :], None,
                                        bounds_check=E1 * CAP - 1, oob_is_err=False).then_inc(dispatched, 16)
            pool.wait_ge(dispatched, 16 * T)

    w1 = [sb(f"w1{u}", [P, F1]) for u in range(2)]
    w2 = [sb(f"w2{u}", [P, F1 // P, D]) for u in range(2)]
    rows = [sb(f"rows{v}", [P, 2, D]) for v in range(2)]
    rT = [sb(f"rT{v}", [P, ROWS]) for v in range(2)]
    hid = [sb(f"hid{v}", [P, F1 // P, ROWS]) for v in range(2)]
    res = [sb(f"res{v}", [P, 2, D]) for v in range(2)]
    with ExitStack() as inner:
        def psi(name, shape):
            return inner.enter_context(nc.psum_tensor("s2_" + name, shape, F32))

        turn_out = psi("turn_out", [P, 512])
        hid_ps = [psi(f"hid_ps{v}", [P, F1 // P, ROWS]) for v in range(2)]
        out_ps = psi("out_ps", [P, 2, D])
        w_loaded = [sems(f"s2_w_loaded{u}") for u in range(2)]
        r_loaded = [sems(f"s2_r_loaded{v}") for v in range(2)]
        r_turned = sems("s2_r_turned")
        rT_ready = sems("s2_rT_ready")
        hid_made = sems("s2_hid_made")
        hid_ready = sems("s2_hid_ready")
        out_made = sems("s2_out_made")
        out_ready = sems("s2_out_ready")
        stored = [sems(f"s2_stored{v}") for v in range(2)]
        GPE = CAP // ROWS
        groups = E1 * GPE
        src = slots.rearrange("(g t p) d -> g p t d", p=P, t=2)
        dst = done.rearrange("(g t p) d -> g p t d", p=P, t=2)
        PER = 2 * GPE

        with nc.Block() as block:

            def pairs(eng, body):
                for j in range(PER):
                    body(j, j % 2, j // GPE, j < 2, 0, j)
                with eng.Fori(1, E1 // 2) as i:
                    for j in range(PER):
                        body(i * PER + j, j % 2, j // GPE, False, i, j)

            @block.sync
            def _(sp):
                def load_w(e, u):
                    sp.dma_start(w1[u][:, :], dram["L0_ffn_W1"][bass.ds(e, 1)].squeeze(0)).then_inc(w_loaded[u], 16)
                    sp.dma_start(w2[u][:, :, :], dram["L0_ffn_W2"].rearrange("e (f p) d -> e p f d", p=P)[bass.ds(e, 1)]
                                 .squeeze(0)).then_inc(w_loaded[u], 16)

                def body(g, v, u, first, i, j):
                    if j % GPE == 0:
                        if not (isinstance(i, int)):
                            sp.wait_ge(out_made, g - GPE)
                        load_w(i * 2 + u, u)
                    if not first:
                        sp.wait_ge(r_turned, g - 1)
                    sp.dma_start(rows[v][:, :, :], src[bass.ds(g, 1)].squeeze(0)).then_inc(r_loaded[v], 16)

                pairs(sp, body)

            @block.tensor
            def _(pe):
                def turn(g, v, first, loads):
                    pe.wait_ge(r_loaded[v], loads * 16)
                    if not first:
                        pe.wait_ge(rT_ready, g)
                    for t in range(2):
                        last = pe.transpose(turn_out[:, t * P:(t + 1) * P], rows[v][:, t, :], c["ident"][:, :])
                    last.then_inc(r_turned, 1)

                def down(g, v, u, first):
                    pe.wait_ge(hid_ready, g + 1)
                    if not first:
                        pe.wait_ge(out_ready, g)
                    for t in range(2):
                        for f in range(F1 // P):
                            last = pe.matmul(out_ps[:, t, :], hid[v][:, f, t * P:(t + 1) * P], w2[u][:, f, :],
                                             start=(f == 0), stop=(f == F1 // P - 1), skip_group_check=True)
                    last.then_inc(out_made, 1)

                def up(g, v, u, first, loads):
                    pe.wait_ge(w_loaded[u], loads * 32)
                    pe.wait_ge(rT_ready, g + 1)
                    if not first:
                        pe.wait_ge(hid_ready, g - 1)
                    for f in range(F1 // P):
                        last = pe.matmul(hid_ps[v][:, f, :], w1[u][:, f * P:(f + 1) * P], rT[v][:, :],
                                         start=True, stop=True)
                    last.then_inc(hid_made, 1)

                def body(g, v, u, first, i, j):
                    begins = isinstance(i, int) and j == 0
                    turn(g, v, begins, i * GPE + j // 2 + 1)
                    up(g, v, u, first, i + 1)
                    if not begins:
                        down(g - 1, 1 - v, (u if j % GPE else 1 - u), isinstance(i, int) and j == 1)

                pairs(pe, body)
                down(groups - 1, 1, 1, False)

            @block.scalar
            def _(act):
                def body(g, v, u, first, i, j):
                    act.wait_ge(r_turned, g + 1)
                    if not first:
                        act.wait_ge(hid_made, g - 1)
                    act.activation(rT[v][:, :], turn_out[:, 0:ROWS], ACT.Copy).then_inc(rT_ready, 1)
                    act.wait_ge(hid_made, g + 1)
                    if not first:
                        act.wait_ge(out_made, g - 1)
                    act.activation(hid[v][:, :, :], hid_ps[v][:, :, :], ACT.Relu).then_inc(hid_ready, 1)

                pairs(act, body)

            @block.vector
            def _(dve):
                def body(g, v, u, first, i, j):
                    dve.wait_ge(out_made, g + 1)
                    if not first:
                        dve.wait_ge(stored[v], (i * GPE + j // 2) * 16)
                    dve.tensor_copy(res[v][:, :, :], out_ps[:, :, :]).then_inc(out_ready, 1)

                pairs(dve, body)

            @block.gpsimd
            def _(pool):
                def body(g, v, u, first, i, j):
                    pool.wait_ge(out_ready, g + 1)
                    pool.dma_start(dst[bass.ds(g, 1)].squeeze(0), res[v][:, :, :]).then_inc(stored[v], 16)

                pairs(pool, body)
                for v in range(2):
                    pool.wait_ge(stored[v], 16 * groups // 2)

    G = sb("G", [P, T, D])
    own = sems("s2_own")
    GATHERS = 4
    gathered = [sems(f"s2_gathered{i}") for i in range(GATHERS)]
    lnst = sb("lnst", [P, T, 6])
    ln = sems("s2_ln")
    with nc.Block() as block:

        @block.scalar
        def _(act):
            for i in range(GATHERS):
                part = slice(i * T // GATHERS, (i + 1) * T // GATHERS)
                act.activation(G[:, part, :], X[:, part, :], ACT.Copy).then_inc(own, 1)

        @block.gpsimd
        def _(pool):
            for i in range(GATHERS):
                pool.wait_ge(own, i + 1)
                for t in range(i * T // GATHERS, (i + 1) * T // GATHERS):
                    pool.indirect_dma_start(G[:, t, :], None, done, bass.IndirectOffsetOnAxis(ap=slot_u[:, t:t + 1], axis=0),
                                            bounds_check=E1 * CAP - 1, oob_is_err=False).then_inc(gathered[i], 16)

        @block.vector
        def _(dve):
            for i in range(GATHERS):
                dve.wait_ge(gathered[i], 16 * (T // GATHERS))
                for t in range(i * T // GATHERS, (i + 1) * T // GATHERS):
                    last = dve.scalar_tensor_tensor(X[:, t, :], G[:, t, :], factor[:, t:t + 1], X[:, t, :],
                                                    ALU.mult, ALU.add)
                last.then_inc(ln, 1)
                dve.wait_ge(ln, 2 * i + 1)
                for t in range(i * T // GATHERS, (i + 1) * T // GATHERS):
                    last = dve.bn_stats(lnst[:, t, :], X[:, t, :])
                last.then_inc(ln, 1)
                dve.wait_ge(ln, 2 * i + 2)
                for t in range(i * T // GATHERS, (i + 1) * T // GATHERS):
                    dve.bn_aggr(stats[:, t, :], lnst[:, t, :])



ATT_CHUNKS = [(0, 0, 8), (1, 0, 4), (1, 4, 4), (0, 8, 8), (1, 8, 4), (1, 12, 4)]
STEPS = len(ATT_CHUNKS)


def softmax_stage(nc, ctx, sems, name, X, kept, centre, scale, second_scale, stats, c, kind):
    def sb(n, shape, dt=F32):
        return ctx.enter_context(nc.sbuf_tensor(f"{name}_{n}", shape, dt))

    def ps(n, shape):
        return ctx.enter_context(nc.psum_tensor(f"{name}_{n}", shape, F32))

    rows = [sb(f"rows{u}", [P, 2, D]) for u in range(2)]
    lean_rows = [sb(f"lean_rows{u}", [P, 2, D]) for u in range(2)] if second_scale is not None else None
    TAKES = kind.takes
    TURN_FIRST = kind.slots > 2
    SLOTS, WORK, HEADS = kind.slots, kind.work_banks, kind.heads_banks
    scores = [ps(f"scores{s}", [P, 1024]) for s in range(SLOTS)]
    heads = [ps(f"heads{s}", [P, 512]) for s in range(HEADS)]
    work = [ps(f"work{s}", [P, 512]) for s in range(WORK)]
    att = [sb(f"att{s}", [P, 1024]) for s in range(SLOTS)]
    attT = [sb(f"attT{s}", [P, 1024]) for s in range(SLOTS)]
    peak = [sb(f"peak{s}", [P, 8]) for s in range(SLOTS)]
    if TAKES:
        total = [sb(f"total{s}", [P, 8]) for s in range(SLOTS)]
        rinv = [sb(f"rinv{s}", [P, 8]) for s in range(SLOTS)]
        rwide = [sb(f"rwide{s}", [P, 512]) for s in range(SLOTS)]
    total_rows = sb("total_rows", [P, 2, D])
    lnst = sb("lnst", [P, 2, 6])
    agg = sb("agg", [P, 2, 2])

    weights_loaded = sems(name + "_weights_loaded")
    rows_ready = sems(name + "_rows_ready")
    rows_kept = sems(name + "_rows_kept")
    job_made = sems(name + "_job_made")
    job_read = sems(name + "_job_read")
    scored = [sems(f"{name}_scored{s}") for s in range(SLOTS)]
    peak_ready = [sems(f"{name}_peak_ready{s}") for s in range(SLOTS)]
    att_ready = [sems(f"{name}_att_ready{s}") for s in range(SLOTS)]
    if TAKES:
        rinv_ready = [sems(f"{name}_rinv_ready{s}") for s in range(SLOTS)]
        rwide_ready = [sems(f"{name}_rwide_ready{s}") for s in range(SLOTS)]
    turned = [sems(f"{name}_turned{s}") for s in range(SLOTS)]
    attT_ready = [sems(f"{name}_attT_ready{s}") for s in range(SLOTS)]
    heads_read = [sems(f"{name}_heads_read{s}") for s in range(HEADS)]
    if not TAKES:
        heads_made = sems(name + "_heads_made")
    ln_step = sems(name + "_ln_step")

    k = kind(sb, sems, c, rows if second_scale is None else lean_rows)
    project_jobs, finish_jobs = k["project"], k["finish"]
    NP, NF = len(project_jobs), len(finish_jobs)
    PROJECT_STEPS, FINISH_STEPS = k["project_steps"], k["finish_steps"]
    PER_SLOT = STEPS // SLOTS
    PER_BANK = STEPS // HEADS if TAKES else 1
    ORDER = []
    for step in range(STEPS):
        if TAKES:
            ORDER += [(step, 0 if step >= SLOTS else -1, "take")]
        ORDER += [(step, 1, a) for a, at in enumerate(PROJECT_STEPS) if at == step]
        ORDER += [(step, -1, a) for a, at in enumerate(FINISH_STEPS) if at == step]

    def body_jobs(first=False, last=False):
        return [job for job in ORDER if not (first and job[1] < 0 or last and job[1] > 0)]

    MISSING = len(ORDER) - len(body_jobs(first=True))

    def jobs_before(n):
        return NP if isinstance(n, int) and n == 0 else n * len(ORDER) + NP - MISSING

    def bank_before(u, first):
        return NP if first else u * len(ORDER) + NP - MISSING

    def projected(n):
        if isinstance(n, int) and n == 0:
            return NP
        order = body_jobs(first=isinstance(n, int) and n == 1)
        return jobs_before(n - 1) + max(i for i, (_, to, _) in enumerate(order) if to == 1) + 1

    def run_step(n, u, step, first, last, run, kinds=("take", "other")):
        for i, (at, to, a) in enumerate(body_jobs(first, last)):
            if at == step and ("take" if a == "take" else "other") in kinds:
                run(n + to if to else n, u if to == 0 else 1 - u, jobs_before(n) + i,
                    (bank_before(u, first) + i) % WORK, to == 1, a, step)

    def run_tail(run):
        index = jobs_before(B - 1) + len(body_jobs(last=True))
        left = ([("take", step) for step in range(SLOTS)] if TAKES else []) + [(a, STEPS) for a in range(NF)]
        for i, (a, step) in enumerate(left):
            run(B - 1, (B - 1) % 2, index + i, (bank_before(1, False) + len(body_jobs(last=True)) + i) % WORK,
                False, a, step)

    def bodies(eng, body):
        body(0, 0, 0, first=True)
        body(1, 1, 0)
        with eng.Fori(1, B // 2 - 1) as i:
            body(i * 2, 0, i)
            body(i * 2 + 1, 1, i)
        body(B - 2, 0, B // 2 - 1)
        body(B - 1, 1, B // 2 - 1, last=True)

    def behind(n, u, j, lag):
        return (n, u, j - lag) if j >= lag else (n - 1, 1 - u, j - lag + STEPS)

    def exists(j, lag, first):
        return j >= lag or not first

    def used(n, j):
        return n * PER_SLOT + j // SLOTS

    with nc.Block() as block:

        @block.sync
        def _(sp):
            for dst, src in k["loads"]:
                sp.dma_start(dst, src).then_inc(weights_loaded, 16)
            if k["spread"]:
                k["spread"](sp, job_read, projected, bodies)

        @block.gpsimd
        def _(pool):
            for zeros in k["zeros"]:
                pool.memset(zeros, 0.0).then_inc(k["zeroed"], 1)

            def keep(n, u):
                pool.wait_ge(rows_ready, n + 1)
                pool.tensor_copy(kept[:, bass.ds(n * 2, 2), :], rows[u][:, :, :]).then_inc(rows_kept, 1)

            def widen(n, u, j):
                s = j % SLOTS
                half, h0, nh = ATT_CHUNKS[j]
                pool.wait_ge(rinv_ready[s], used(n, j) + 1)
                if not (isinstance(n, int) and n == 0 and j < SLOTS):
                    pool.wait_ge(att_ready[s], used(n, j) + 1)
                out = rwide[s][:, 0:nh * k["head_dim"]].rearrange("p (h d) -> p h d", h=nh)
                pool.tensor_tensor(out, broadcast_last(rinv[s][:, 0:nh], k["head_dim"]),
                                   broadcast_middle(c["ones"][:, 0:k["head_dim"]], nh), ALU.mult)\
                    .then_inc(rwide_ready[s], 1)

            def body(n, u, i, first=False, last=False):
                if first:
                    keep(0, 0)
                if not last:
                    keep(n + 1, 1 - u)
                if TAKES:
                    for j in range(STEPS):
                        widen(n, u, j)

            bodies(pool, body)

        @block.tensor
        def _(pe):
            pe.wait_ge(weights_loaded, 16 * len(k["loads"]))
            pe.wait_ge(c["const_step"], CONSTANTS)

            def job(n, u, index, b, is_p, a, step):
                if a == "take":
                    j = (step - SLOTS) % STEPS
                    s = j % SLOTS
                    pe.wait_ge(job_read, index + 1 - WORK)
                    pe.wait_ge(rwide_ready[s], used(n, j) + 1)
                    for b4 in range(ATT_CHUNKS[j][2] // 2):
                        last = pe.transpose(work[b][:, b4 * P:(b4 + 1) * P], rwide[s][:, b4 * P:(b4 + 1) * P],
                                            c["ident"][:, :])
                    last.then_inc(job_made, 1)
                    return
                work_of, _, waits_for_last = (project_jobs if is_p else finish_jobs)[a]
                if waits_for_last:
                    pe.wait_ge(job_read, index)
                elif not (isinstance(index, int) and index < WORK):
                    pe.wait_ge(job_read, index + 1 - WORK)
                if is_p and a == 0:
                    pe.wait_ge(rows_ready, n + 1)
                if not is_p and a == 0:
                    for h in range(HEADS):
                        pe.wait_ge(heads_read[h], (n + 1) * PER_BANK)
                work_of(pe, work[b], u).then_inc(job_made, 1)

            def weigh(n, u, j):
                s = j % SLOTS
                half, h0, nh = ATT_CHUNKS[j]
                pe.wait_ge(attT_ready[s], (used(n, j) + 1) * 2)
                b = j % HEADS
                if TAKES:
                    if not (isinstance(n, int) and n == 0 and j < HEADS):
                        pe.wait_ge(heads_read[b], n * PER_BANK + j // HEADS)
                elif j == 0 and not (isinstance(n, int) and n == 0):
                    pe.wait_ge(heads_read[0], n)
                last = k["weigh"](pe, u, j, half, h0, nh, attT[s], heads[b])
                if not TAKES and j == STEPS - 1:
                    last.then_inc(heads_made, 1)

            def score(n, u, i, j):
                s = j % SLOTS
                half, h0, nh = ATT_CHUNKS[j]
                keys = (half + 1) * P
                if j == 0:
                    pe.wait_ge(job_read, projected(n))
                    if k["spread"]:
                        pe.wait_ge(k["spread_done"][u], (i + 1) * k["spread_count"])
                k["score"](pe, u, half, h0, nh, keys, scores[s])
                for b in range(2):
                    out = scores[s][:, b * 512:(b + 1) * 512].rearrange("p (h k) -> p h k", k=keys)
                    last = pe.matmul(out[:, :, keys - P:keys], c["minus_ident_bf"][:, :],
                                     broadcast_middle(c["far_mask"][:, :], 512 // keys),
                                     start=False, stop=True, skip_group_check=True)
                last.then_inc(scored[s], 1)

            def turn(n, u, j):
                s = j % SLOTS
                pe.wait_ge(att_ready[s], used(n, j) + 1)
                for bank in range(2):
                    for b in range(bank * 4, bank * 4 + 4):
                        last = pe.transpose(scores[s][:, b * P:(b + 1) * P], att[s][:, b * P:(b + 1) * P],
                                            c["ident"][:, :])
                    last.then_inc(turned[s], 1)

            def body(n, u, i, first=False, last=False):
                for j in range(STEPS):
                    if TURN_FIRST and exists(j, SLOTS - 1, first):
                        turn(*behind(n, u, j, SLOTS - 1))
                    if exists(j, SLOTS, first):
                        weigh(*behind(n, u, j, SLOTS))
                    score(n, u, i, j)
                    run_step(n, u, j, first, last, job, ["take"])
                    if not TURN_FIRST and exists(j, SLOTS - 1, first):
                        turn(*behind(n, u, j, SLOTS - 1))
                    run_step(n, u, j, first, last, job, ["other"])
                if last:
                    for j in range(STEPS, STEPS + SLOTS):
                        if TURN_FIRST and j < STEPS + SLOTS - 1:
                            turn(n, u, j - SLOTS + 1)
                        weigh(n, u, j - SLOTS)
                        if not TURN_FIRST and j < STEPS + SLOTS - 1:
                            turn(n, u, j - SLOTS + 1)
                    run_tail(job)

            pe.wait_ge(k["zeroed"], len(k["zeros"]))
            for a in range(NP):
                job(0, 0, a, a % WORK, True, a, 0)
            bodies(pe, body)

        @block.scalar
        def _(act):
            def exponentials(n, j):
                s = j % SLOTS
                half, h0, nh = ATT_CHUNKS[j]
                keys = (half + 1) * P
                act.wait_ge(peak_ready[s], used(n, j) + 1)
                for a in range(nh):
                    last = act.activation(att[s][:, a * keys:(a + 1) * keys], scores[s][:, a * keys:(a + 1) * keys],
                                          ACT.Exp, bias=peak[s][:, a:a + 1],
                                          accum_out=total[s][:, a:a + 1] if TAKES else None)
                last.then_inc(att_ready[s], 1)

            def copy(n, u, j):
                s = j % SLOTS
                for bank in range(2):
                    part = slice(bank * 512, (bank + 1) * 512)
                    act.wait_ge(turned[s], used(n, j) * 2 + bank + 1)
                    act.activation(attT[s][:, part], scores[s][:, part], ACT.Copy).then_inc(attT_ready[s], 1)

            def body(n, u, i, first=False, last=False):
                for j in range(STEPS):
                    if exists(j, SLOTS - 1, first):
                        copy(*behind(n, u, j, SLOTS - 1))
                    exponentials(n, j)
                if last:
                    for j in range(STEPS - SLOTS + 1, STEPS):
                        copy(n, u, j)

            bodies(act, body)

        @block.vector
        def _(dve):
            dve.wait_ge(weights_loaded, 16 * len(k["loads"]))
            dve.wait_ge(c["const_step"], CONSTANTS)
            dve.wait_ge(k["zeroed"], len(k["zeros"]))

            def normalise_rows(n, u):
                for t in range(2):
                    tile = n * 2 + t
                    last = dve.tensor_scalar(rows[u][:, t, :], X[:, bass.ds(tile, 1), :].squeeze(1),
                                             centre[:, bass.ds(tile, 1), 0], scale[:, bass.ds(tile, 1)],
                                             ALU.subtract, ALU.mult)
                    if second_scale is not None:
                        last = dve.tensor_scalar(lean_rows[u][:, t, :], X[:, bass.ds(tile, 1), :].squeeze(1),
                                                 centre[:, bass.ds(tile, 1), 0], second_scale[:, bass.ds(tile, 1)],
                                                 ALU.subtract, ALU.mult)
                last.then_inc(rows_ready, 1)

            def job(n, u, index, b, is_p, a, step):
                if a == "take":
                    j = (step - SLOTS) % STEPS
                    half, h0, nh = ATT_CHUNKS[j]
                    dve.wait_ge(job_made, index + 1)
                    h = j % HEADS
                    if not (isinstance(n, int) and n == 0 and j < HEADS):
                        dve.wait_ge(heads_read[h], n * PER_BANK + j // HEADS)
                    k["copy_sums"](dve, h, nh, work[b]).then_inc(job_read, 1)
                    dve.wait_ge(job_read, index + 1)
                    k["take_heads"](dve, u, h, half, h0, nh, heads[h]).then_inc(heads_read[h], 1)
                    return
                if not is_p and a == NF - 1:
                    residual(n, u, index, b)
                    return
                dve.wait_ge(job_made, index + 1)
                (project_jobs if is_p else finish_jobs)[a][1](dve, work[b], u).then_inc(job_read, 1)

            def residual(n, u, index, b):
                dve.wait_ge(job_made, index + 1)
                dve.wait_ge(rows_kept, n + 1)
                pair = bass.ds(n * 2, 2)
                attended = work[b][:, 0:2 * D].rearrange("p (t d) -> p t d", t=2)
                dve.tensor_tensor(total_rows[:, :, :], attended, kept[:, pair, :], ALU.add).then_inc(ln_step, 1)
                dve.tensor_tensor(X[:, pair, :], attended, kept[:, pair, :], ALU.add).then_inc(job_read, 1)
                tile_statistics(dve, total_rows, lnst, agg, c["carrier"], stats, n, ln_step)

            def peaks(n, j):
                s = j % SLOTS
                half, h0, nh = ATT_CHUNKS[j]
                dve.wait_ge(scored[s], used(n, j) + 1)
                dve.tensor_reduce(peak[s][:, 0:nh], scores[s][:, :].rearrange("p (h k) -> p h k", h=nh), AX.X,
                                  ALU.max, negate=True).then_inc(peak_ready[s], 1)

            def sums(n, u, j):
                s = j % SLOTS
                nh = ATT_CHUNKS[j][2]
                dve.wait_ge(att_ready[s], used(n, j) + 1)
                dve.reciprocal(rinv[s][:, 0:nh], total[s][:, 0:nh]).then_inc(rinv_ready[s], 1)

            def take_heads(n, u):
                dve.wait_ge(heads_made, n + 1)
                k["take_heads"](dve, n, u, heads[0]).then_inc(heads_read[0], 1)

            def body(n, u, i, first=False, last=False):
                for j in range(STEPS):
                    if TAKES and exists(j, SLOTS - 1, first):
                        sums(*behind(n, u, j, SLOTS - 1))
                    if not TAKES and j == SLOTS - 1 and not first:
                        take_heads(n - 1, 1 - u)
                    peaks(n, j)
                    if j == 0 and not last:
                        if not first:
                            dve.wait_ge(rows_kept, n)
                        normalise_rows(n + 1, 1 - u)
                    run_step(n, u, j, first, last, job)
                if last:
                    if TAKES:
                        for j in range(STEPS, STEPS + SLOTS - 1):
                            sums(n, u, j - SLOTS + 1)
                    else:
                        take_heads(n, u)
                    run_tail(job)

            normalise_rows(0, 0)
            for a in range(NP):
                job(0, 0, a, a % WORK, True, a, 0)
            bodies(dve, body)


def gqa(dram):
    HQ, HKV, HD = 16, 4, 64
    PAIRS = HQ * HD // P

    def kind(sb, sems, c, rows):
        wq = sb("wq", [P, HQ * HD])
        wk = sb("wk", [P, HKV, 2, HD])
        wv = sb("wv", [P, HKV * HD])
        wo = sb("wo", [P, PAIRS, D])
        xT = sb("xT", [P, N])
        qT = [sb(f"qT{u}", [P, PAIRS, N]) for u in range(2)]
        kT = [sb(f"kT{u}", [P, HKV, 2, N]) for u in range(2)]
        v = [sb(f"v{u}", [P, 2, HKV * HD]) for u in range(2)]
        oT = [sb(f"oT{u}", [P, PAIRS, N]) for u in range(2)]
        rsumsT = [sb(f"rsumsT{b}", [P, 4 * P]) for b in range(2)]

        def halves(w):
            return w[:, :].rearrange("p (t n) -> p t n", t=2)

        def turn_rows(pe, w, u):
            for t in range(2):
                last = pe.transpose(w[:, t * P:(t + 1) * P], rows[u][:, t, :], c["ident"][:, :])
            return last

        def make_q(b):
            def pe_part(pe, w, u):
                for j in range(2):
                    last = pe.matmul(w[:, j * N:(j + 1) * N], wq[:, (2 * b + j) * P:(2 * b + j + 1) * P], xT[:, :],
                                     start=True, stop=True)
                return last
            return pe_part, lambda dve, w, u: dve.tensor_scalar(qT[u][:, 2 * b:2 * b + 2, :], halves(w),
                                                                float(HD) ** -0.5, None, ALU.mult), b == 0

        def make_k(b):
            def pe_part(pe, w, u):
                for j in range(2):
                    last = pe.matmul(w[:, j * N:(j + 1) * N], wk[:, 2 * b + j, :, :].rearrange("p t d -> p (t d)"),
                                     xT[:, :], start=True, stop=True)
                return last

            def dve_part(dve, w, u):
                for r in range(2):
                    rows_of = slice(r * HD, (r + 1) * HD)
                    last = dve.tensor_copy(kT[u][rows_of, 2 * b:2 * b + 2, r, :], halves(w)[rows_of, :, :])
                return last
            return pe_part, dve_part, False

        def make_v(pe, w, u):
            for t in range(2):
                last = pe.matmul(w[:, t * HKV * HD:(t + 1) * HKV * HD], xT[:, t * P:(t + 1) * P], wv[:, :],
                                 start=True, stop=True)
            return last

        def score(pe, u, half, h0, nh, keys, out):
            for a in range(0, nh, 2):
                b = (h0 + a) // 2
                pe.matmul(out[:, a * keys:(a + 2) * keys], qT[u][:, b, half * P:(half + 1) * P],
                          kT[u][:, (h0 + a) // 4, :, 0:keys], start=(a * keys % 512 == 0), stop=False,
                          skip_group_check=True)

        def weigh(pe, u, j, half, h0, nh, attT, out):
            blocks = half + 1
            turned = attT[:, :].rearrange("p (a r kb q) -> p r kb a q", r=2, kb=blocks, q=P)
            for g in range(nh // 4):
                for kb in range(blocks):
                    for r in range(2):
                        last = pe.matmul(out[r * HD:(r + 1) * HD, g * 2 * P:(g + 1) * 2 * P],
                                         v[u][:, kb, (h0 // 4 + g) * HD:(h0 // 4 + g + 1) * HD],
                                         turned[:, r, kb, 2 * g:2 * g + 2, :], start=(g == 0 and kb == 0),
                                         stop=(kb == half), tile_position=(0, r * HD), skip_group_check=True)
            return last

        def copy_sums(dve, b, nh, w):
            return dve.tensor_copy(rsumsT[b][:, 0:nh // 2 * P], w[:, 0:nh // 2 * P])

        def take_heads(dve, u, b, half, h0, nh, heads):
            def blocks(ap):
                return ap[:, 0:nh // 2 * P].rearrange("p (b q) -> p b q", q=P)
            return dve.tensor_tensor(oT[u][:, h0 // 2:(h0 + nh) // 2, half * P:(half + 1) * P], blocks(heads),
                                     blocks(rsumsT[b]), ALU.mult)

        def project_out(pe, w, u):
            for t in range(2):
                for b in range(PAIRS):
                    last = pe.matmul(w[:, t * D:(t + 1) * D], oT[u][:, b, t * P:(t + 1) * P], wo[:, b, :],
                                     start=(b == 0), stop=(b == PAIRS - 1), skip_group_check=True)
            return last

        return {
            "loads": [(wq[:, :], dram["Wq"]), (wk[:, :, 0, :], dram["Wk"].rearrange("p (h d) -> p h d", d=HD)),
                      (wk[:, :, 1, :], dram["Wk"].rearrange("p (h d) -> p h d", d=HD)), (wv[:, :], dram["Wv"]),
                      (wo[:, :, :], dram["Wo"].rearrange("(b p) d -> p b d", p=P))],
            "zeros": [kT[u][(1 - r) * HD:(2 - r) * HD, :, r, :] for u in range(2) for r in range(2)],
            "zeroed": sems("gqa_zeroed"),
            "spread": None,
            "score": score, "weigh": weigh, "take_heads": take_heads, "copy_sums": copy_sums, "head_dim": HD,
            "project": [(turn_rows, lambda dve, w, u: dve.tensor_copy(xT[:, :], w[:, 0:N]), False)]
            + [make_q(b) for b in range(4)] + [make_k(b) for b in range(2)]
            + [(make_v, lambda dve, w, u: dve.tensor_copy(v[u][:, :, :], halves(w)), False)],
            "project_steps": [0, 1, 2, 3, 3, 4, 4, 5],
            "finish": [(project_out, None, False)],
            "finish_steps": [2],
        }

    kind.slots, kind.work_banks, kind.heads_banks, kind.takes = 2, 2, 2, True
    return kind


def latent(dram):
    LATENT = 64

    def order(h):
        return h % 4 * 4 + h // 4

    def kind(sb, sems, c, rows):
        wq = sb("wq", [P, D])
        wdown = sb("wdown", [P, LATENT])
        wuk = sb("wuk", [LATENT, D])
        wuv = sb("wuv", [LATENT, D])
        wo = sb("wo", [P, D])
        gain = sb("gain", [P, 1])
        hT = sb("hT", [P, N])
        cT = sb("cT", [LATENT, N])
        qT = [sb(f"qT{u}", [P, N]) for u in range(2)]
        kT = [sb(f"kT{u}", [P, N]) for u in range(2)]
        kM = [sb(f"kM{u}", [P, H, N]) for u in range(2)]
        vM = [sb(f"vM{u}", [P, 2, 4, 4 * (4 * DH + DH)]) for u in range(2)]
        oT = [sb(f"oT{u}", [P, N]) for u in range(2)]
        rsums = sb("rsums", [P, N])
        inverted = sems("mla_inverted")
        spread_done = [sems(f"mla_spread{u}") for u in range(2)]

        def turn(source):
            def pe_part(pe, w, u):
                for t in range(2):
                    last = pe.transpose(w[:, t * P:(t + 1) * P], source(u, t), c["ident"][:, :])
                return last
            return pe_part

        def make_q_latent(pe, w, u):
            pe.matmul(w[:, 0:N], wq[:, :], hT[:, :], start=True, stop=True)
            return pe.matmul(w[0:LATENT, N:2 * N], wdown[:, :], hT[:, :], start=True, stop=True)

        def take_q_latent(dve, w, u):
            dve.tensor_scalar(qT[u][:, :], w[:, 0:N], float(DH) ** -0.5, None, ALU.mult)
            return dve.tensor_copy(cT[:, :], w[0:LATENT, N:2 * N])

        def make_kv(pe, w, u):
            pe.matmul(w[:, 0:N], wuk[:, :], cT[:, :], start=True, stop=True)
            for t in range(2):
                last = pe.matmul(w[:, N + t * D:N + (t + 1) * D], cT[:, t * P:(t + 1) * P], wuv[:, :],
                                 start=True, stop=True)
            return last

        def take_kv(dve, w, u):
            for t in range(2):
                strips = vM[u][:, t, :, :].rearrange("p g (m c) -> p g m c", m=4)
                dve.tensor_copy(strips[:, :, :, 0:DH],
                                w[:, N + t * D:N + (t + 1) * D].rearrange("p (g m d) -> p g m d", g=4, m=4))
            return dve.tensor_copy(kT[u][:, :], w[:, 0:N])

        def spread(sp, job_read, projected, bodies):
            sp.wait_ge(zeroed, 4)

            def body(n, u, i, first=False, last=False):
                sp.wait_ge(job_read, projected(n))
                for h in range(H):
                    rows_of = slice(h * DH, (h + 1) * DH)
                    sp.dma_start(kM[u][rows_of, order(h), :], kT[u][rows_of, :]).then_inc(spread_done[u], 16)
            bodies(sp, body)

        def score(pe, u, half, h0, nh, keys, out):
            per = 512 // keys
            for b in range(2):
                pe.matmul(out[:, b * 512:(b + 1) * 512], qT[u][:, half * P:(half + 1) * P],
                          kM[u][:, h0 + b * per:h0 + (b + 1) * per, 0:keys], start=True, stop=False,
                          skip_group_check=True)

        def weigh(pe, u, j, half, h0, nh, attT, out):
            for kb in range(half + 1):
                for a in range(nh):
                    m, g = divmod(h0 + a, 4)
                    col = (a * (half + 1) + kb) * P
                    for which, values in enumerate((vM[u][:, kb, g, 32 * m:32 * m + 32], c["head_ones"][:, m, :])):
                        at = which * N + half * P
                        last = pe.matmul(out[32 * g:32 * g + 32, at:at + P], values, attT[:, col:col + P],
                                         start=(j == 0 and a < 4 and which == 0), stop=False,
                                         tile_position=(0, 32 * g), skip_group_check=True)
            return last

        def take_heads(dve, n, u, heads):
            dve.reciprocal(rsums[:, :], heads[:, N:2 * N]).then_inc(inverted, 1)
            dve.wait_ge(inverted, n + 1)
            return dve.tensor_tensor(oT[u][:, :], heads[:, 0:N], rsums[:, :], ALU.mult)

        def project_out(pe, w, u):
            for t in range(2):
                last = pe.matmul(w[:, t * D:(t + 1) * D], oT[u][:, t * P:(t + 1) * P], wo[:, :], start=True, stop=True)
            return last

        zeroed = sems("mla_zeroed")
        return {
            "loads": [(wq[:, :], dram["Wq"]), (wdown[:, :], dram["Wdkv"]), (wuk[:, :], dram["Wuk"]),
                      (wuv[:, :], dram["Wuv"]), (wo[:, :], dram["Wo"]), (gain[:, :], dram["g1"])],
            "zeros": [kM[u][:, :, :] for u in range(2)] + [vM[u][:, :, :, :] for u in range(2)],
            "zeroed": zeroed,
            "spread": spread, "spread_done": spread_done, "spread_count": 16 * H,
            "score": score, "weigh": weigh, "take_heads": take_heads,
            "project": [(turn(lambda u, t: rows[u][:, t, :]),
                         lambda dve, w, u: dve.tensor_scalar(hT[:, :], w[:, 0:N], gain[:, 0:1], None, ALU.mult), False),
                        (make_q_latent, take_q_latent, True), (make_kv, take_kv, True)],
            "project_steps": [0, 1, 2],
            "finish": [(project_out, None, True)],
            "finish_steps": [4],
        }

    kind.slots, kind.work_banks, kind.heads_banks, kind.takes = 3, 1, 1, False
    return kind



E2 = 8
F2 = 256
SPAN = 512
SPAN_TILES = SPAN // P


def choose_two(nc, ctx, sems, logits, share):
    T = TILES

    def sb(name, shape):
        return ctx.enter_context(nc.sbuf_tensor("c2_" + name, shape, F32))

    first = sb("first", [P, T])
    second = sb("second", [P, T])
    rank = sb("rank", [P, T])
    eq = sb("eq", [P, T, E2])
    rest = sb("rest", [P, T, E2])
    hot1 = sb("hot1", [P, T, E2])
    hot2 = sb("hot2", [P, T, E2])
    early = sb("early", [P, E2])
    gap = sb("gap", [P, T])
    ratio = sb("ratio", [P, T])
    one = sb("one", [P, T])
    g1 = sb("g1", [P, T])
    early_ready = sems("c2_early_ready")
    gap_ready = sems("c2_gap_ready")
    ratio_ready = sems("c2_ratio_ready")
    step = sems("c2_step")

    with nc.Block() as block:

        @block.gpsimd
        def _(pool):
            pool.iota(early[:, :], pattern=[[-1, E2]], base=E2, channel_multiplier=0,
                      allow_small_or_imprecise_dtypes=True).then_inc(early_ready, 1)

        @block.scalar
        def _(act):
            act.wait_ge(gap_ready, 1)
            act.activation(ratio[:, :], gap[:, :], ACT.Exp).then_inc(ratio_ready, 1)

        @block.vector
        def _(dve):
            n = [0]

            def settle(ins):
                n[0] += 1
                ins.then_inc(step, 1)
                dve.wait_ge(step, n[0])

            by_tile = lambda t: broadcast_last(t[:, :], E2)

            def largest(values, top, hot):
                settle(dve.tensor_reduce(top[:, :], values[:, :, :], AX.X, ALU.max))
                settle(dve.tensor_tensor(eq[:, :, :], values[:, :, :], by_tile(top), ALU.is_equal))
                settle(dve.tensor_tensor(eq[:, :, :], eq[:, :, :], broadcast_middle(early[:, :], T), ALU.mult))
                settle(dve.tensor_reduce(rank[:, :], eq[:, :, :], AX.X, ALU.max))
                settle(dve.tensor_tensor(hot[:, :, :], eq[:, :, :], by_tile(rank), ALU.is_equal))

            dve.wait_ge(early_ready, 1)
            largest(logits, first, hot1)
            settle(dve.tensor_scalar(rest[:, :, :], hot1[:, :, :], -3e38, None, ALU.mult))
            settle(dve.tensor_tensor(rest[:, :, :], rest[:, :, :], logits[:, :, :], ALU.add))
            largest(rest, second, hot2)
            dve.tensor_tensor(gap[:, :], second[:, :], first[:, :], ALU.subtract).then_inc(gap_ready, 1)
            dve.wait_ge(ratio_ready, 1)
            settle(dve.tensor_scalar(one[:, :], ratio[:, :], 1.0, None, ALU.add))
            settle(dve.reciprocal(g1[:, :], one[:, :]))
            settle(dve.tensor_tensor(ratio[:, :], ratio[:, :], g1[:, :], ALU.mult))
            settle(dve.tensor_tensor(hot1[:, :, :], hot1[:, :, :], by_tile(g1), ALU.mult))
            settle(dve.tensor_tensor(hot2[:, :, :], hot2[:, :, :], by_tile(ratio), ALU.mult))
            dve.tensor_tensor(share[:, :, :], hot1[:, :, :], hot2[:, :, :], ALU.add)


def stage5(nc, ctx, sems, dram, X, rows3, hT_all, share, stats, c):
    def sb(name, shape, dt=F32):
        return ctx.enter_context(nc.sbuf_tensor("s5_" + name, shape, dt))

    def ps(name, shape):
        return ctx.enter_context(nc.psum_tensor("s5_" + name, shape, F32))

    FB = F2 // P
    SPANS = B * N // SPAN
    w1 = sb("w1", [P, E2, F2])
    w2 = sb("w2", [P, E2, FB, D])
    hid = [sb(f"hid{v}", [P, FB, SPAN]) for v in range(2)]
    acc = [sb(f"acc{v}", [P, SPAN_TILES, D]) for v in range(2)]
    part = sb("part", [P, SPAN_TILES, E2])
    lnst = sb("lnst", [P, SPAN_TILES, 6])
    agg = sb("agg", [P, SPAN_TILES, 2])
    summed = sems("s5_summed")
    hid_ps = [ps(f"hid_ps{v}", [P, FB, SPAN]) for v in range(2)]
    out_ps = [ps(f"out_ps{v}", [P, SPAN_TILES, D]) for v in range(2)]
    loaded = sems("s5_loaded")
    hid_made = sems("s5_hid_made")
    hid_ready = sems("s5_hid_ready")
    out_made = sems("s5_out_made")
    out_read = sems("s5_out_read")
    step = sems("s5_step")

    def spans(eng, body):
        body(0)
        with eng.Fori(1, SPANS) as i:
            body(i)

    with nc.Block() as block:

        @block.sync
        def _(sp):
            sp.dma_start(w1[:, :, :], dram["w1"].rearrange("e d f -> d e f")).then_inc(loaded, 16)
            sp.dma_start(w2[:, :, :, :], dram["w2"].rearrange("e (b p) d -> p e b d", p=P)).then_inc(loaded, 16)

        @block.tensor
        def _(pe):
            pe.wait_ge(loaded, 32)

            def up(i, e, start):
                v = e % 2
                k = i * E2 + e
                if not start:
                    pe.wait_ge(hid_ready, k - 1)
                for b in range(FB):
                    last = pe.matmul(hid_ps[v][:, b, :], w1[:, e, b * P:(b + 1) * P], hT_all[:, bass.ds(i * SPAN, SPAN)],
                                     start=True, stop=True)
                last.then_inc(hid_made, 1)

            def down(i, e, start):
                v = e % 2
                k = i * E2 + e
                pe.wait_ge(hid_ready, k + 1)
                if not start:
                    pe.wait_ge(out_read, k - 1)
                for t in range(SPAN_TILES):
                    for b in range(FB):
                        last = pe.matmul(out_ps[v][:, t, :], hid[v][:, b, t * P:(t + 1) * P], w2[:, e, b, :],
                                         start=(b == 0), stop=(b == FB - 1), skip_group_check=True)
                last.then_inc(out_made, 1)

            def body(i):
                start = isinstance(i, int)
                for e in range(E2):
                    up(i, e, start and e < 2)
                    if e:
                        down(i, e - 1, start and e < 3)
                    elif not start:
                        down(i - 1, E2 - 1, False)

            spans(pe, body)
            down(SPANS - 1, E2 - 1, False)

        @block.scalar
        def _(act):
            def body(i):
                for e in range(E2):
                    k = i * E2 + e
                    act.wait_ge(hid_made, k + 1)
                    if not (isinstance(i, int) and e < 2):
                        act.wait_ge(out_made, k - 1)
                    act.activation(hid[e % 2][:, :, :], hid_ps[e % 2][:, :, :], ACT.Silu).then_inc(hid_ready, 1)

            spans(act, body)

        @block.vector
        def _(dve):
            def body(i):
                X4 = X[:, bass.ds(i * SPAN_TILES, SPAN_TILES), :]
                dve.tensor_copy(part[:, :, :], share[:, bass.ds(i * SPAN_TILES, SPAN_TILES), :])
                dve.tensor_tensor(acc[1][:, :, :], X4, rows3[:, bass.ds(i * SPAN_TILES, SPAN_TILES), :], ALU.add)\
                    .then_inc(summed, 1)
                dve.wait_ge(summed, i + 1)
                for e in range(E2):
                    k = i * E2 + e
                    dve.wait_ge(out_made, k + 1)
                    for t in range(SPAN_TILES):
                        last = dve.scalar_tensor_tensor(acc[e % 2][:, t, :], out_ps[e % 2][:, t, :], part[:, t, e:e + 1],
                                                        acc[1 - e % 2][:, t, :], ALU.mult, ALU.add)
                    last.then_inc(out_read, 1)
                    dve.wait_ge(out_read, k + 1)
                dve.tensor_scalar(X4, acc[1][:, :, :], 1.0, None, ALU.mult).then_inc(step, 1)
                tile_statistics(dve, acc[1], lnst, agg, c["carrier"], stats, i, step)

            spans(dve, body)


def last_norm(nc, ctx, sems, X, stats, rstd, out):
    CHUNK = 8
    made = sems("ln_made")
    stored = sems("stored")
    view = out.rearrange("b (t p) d -> p (b t) d", p=P)
    with nc.Block() as block:

        @block.vector
        def _(dve):
            for t in range(TILES):
                last = dve.tensor_scalar(X[:, t, :], X[:, t, :], stats[:, t, 0:1], rstd[:, t:t + 1],
                                         ALU.subtract, ALU.mult)
                if t % CHUNK == CHUNK - 1:
                    last.then_inc(made, 1)

        @block.sync
        def _(sp):
            for k in range(TILES // CHUNK):
                sp.wait_ge(made, k + 1)
                sp.dma_start(view[:, k * CHUNK:(k + 1) * CHUNK, :], X[:, k * CHUNK:(k + 1) * CHUNK, :])\
                    .then_inc(stored, 16)
            sp.wait_ge(stored, 16 * (TILES // CHUNK))



def build(nc, dram):
    with ExitStack() as ctx:
        def sems(name):
            return ctx.enter_context(nc.semaphore(name))

        def sb(name, shape):
            return ctx.enter_context(nc.sbuf_tensor(name, shape, F32))

        c = constants(nc, ctx, sems)
        c["const_step"] = sems("const_step")
        routed = [sems("routed_" + of) for of in ("rows_ready", "rows_kept", "turned", "rT_ready", "lg_made",
                                                  "lg_read")]
        counted = [sems("mean_square_made"), sems("mean_square_rooted"), 0, 0]
        X = sb("X", [P, TILES, D])
        stats = sb("stats", [P, TILES, 2])
        rstd = sb("rstd", [P, TILES])
        rms = sb("rms", [P, TILES])
        both = sb("both", [P, TILES])
        logits = sb("logits", [P, TILES, E1])
        share = sb("share", [P, TILES, E2])
        rows3 = sb("rows3", [P, TILES, D])
        if "slots" not in dram:
            for name in ("slots", "done"):
                dram[name] = nc.dram_tensor(name, (E1 * CAP, D), F32, kind="Internal").ap()

        def variance(dve, out):
            yield dve.tensor_copy(out[:, :], stats[:, :, 1])

        def square_of_rows(dve, out):
            yield dve.tensor_tensor(out[:, :], rstd[:, :], rstd[:, :], ALU.mult)
            yield dve.tensor_tensor(out[:, :], out[:, :], stats[:, :, 1], ALU.mult)

        def mean_square(dve, out):
            yield dve.tensor_tensor(out[:, :], stats[:, :, 0], stats[:, :, 0], ALU.mult)
            yield dve.tensor_tensor(out[:, :], out[:, :], stats[:, :, 1], ALU.add)

        norm = (variance, rstd, LN_EPS)
        with ExitStack() as inner:
            stage1(nc, inner, sems, dram, X, stats, c)
        with ExitStack() as inner:
            inverse_roots(nc, inner, counted, "norm1", [norm])
        with ExitStack() as inner:
            router(nc, inner, sems, routed, 0, "route1", X, stats, rstd, None, True, None, dram["L0_ffn_Wr"], logits, c)
        with ExitStack() as inner:
            stage2(nc, inner, sems, dram, X, stats, logits, c)
        with ExitStack() as inner:
            inverse_roots(nc, inner, counted, "norm2", [norm])
        with ExitStack() as inner:
            softmax_stage(nc, inner, sems, "gqa", X, X, stats, rstd, None, stats, c, gqa(dram["gqa"]))
        with ExitStack() as inner:
            inverse_roots(nc, inner, counted, "norm3", [norm, (square_of_rows, rms, RMS_EPS)])
        with nc.Block() as block:

            @block.vector
            def _(dve):
                dve.tensor_tensor(both[:, :], rstd[:, :], rms[:, :], ALU.mult)

        with ExitStack() as inner:
            softmax_stage(nc, inner, sems, "mla", X, rows3, stats, rstd, both, stats, c, latent(dram["mla"]))
        with ExitStack() as outer:
            hT_all = outer.enter_context(nc.sbuf_tensor("hT_all", [P, B * N], F32))
            with ExitStack() as inner:
                inverse_roots(nc, inner, counted, "norm4", [(mean_square, rms, RMS_EPS)])
            with ExitStack() as inner:
                router(nc, inner, sems, routed, B, "route2", X, None, rms, dram["g2"], False,
                       hT_all, dram["gate_w"], logits, c)
            with ExitStack() as inner:
                choose_two(nc, inner, sems, logits, share)
            with ExitStack() as inner:
                stage5(nc, inner, sems, dram, X, rows3, hT_all, share, stats, c)
        with ExitStack() as inner:
            inverse_roots(nc, inner, counted, "norm5", [norm])
        with ExitStack() as inner:
            last_norm(nc, inner, sems, X, stats, rstd, dram["out"])


def named(given):
    return given | {
        "WqkvT": given["L0_attn_Wqkv"], "WoT": given["L0_attn_Wo"], "g2": given["L1_ffn_g2"],
        "gate_w": given["L1_ffn_gate_w"], "w1": given["L1_ffn_w1"], "w2": given["L1_ffn_w2"],
        "gqa": {n: given["L1_attn_" + n] for n in ("Wq", "Wk", "Wv", "Wo")},
        "mla": {n: given["L1_ffn_" + n] for n in ("Wq", "Wdkv", "Wuk", "Wuv", "Wo", "g1")},
    }


_NAMES = ["L0_attn_x", "L0_attn_Wqkv", "L0_attn_Wo", "L0_ffn_Wr", "L0_ffn_W1", "L0_ffn_W2", "L1_attn_Wq", "L1_attn_Wk",
          "L1_attn_Wv", "L1_attn_Wo", "L1_ffn_g1", "L1_ffn_Wq", "L1_ffn_Wdkv", "L1_ffn_Wuk", "L1_ffn_Wuv", "L1_ffn_Wo",
          "L1_ffn_g2", "L1_ffn_gate_w", "L1_ffn_w1", "L1_ffn_w2"]


def kernel(**inputs):
    import concourse.bacc as _bacc
    from concourse.bass_utils import run_bass_kernel_spmd as _run

    nc = _bacc.Bacc("TRN2", target_bir_lowering=False, num_devices=1)
    arrays, given = {}, {}
    for name in _NAMES:
        a = np.asarray(inputs[name])
        if name in ("L0_attn_Wqkv", "L0_attn_Wo"):
            a = a.T
        if name in ("L1_ffn_g1", "L1_ffn_g2"):
            a = a.reshape(D, 1)
        a = np.ascontiguousarray(a)
        arrays[f"in_{name}"] = a
        given[name] = nc.dram_tensor(f"in_{name}", a.shape, mybir.dt.from_np(a.dtype), kind="ExternalInput").ap()
    given["out"] = nc.dram_tensor("out_0", (B, N, D), F32, kind="ExternalOutput").ap()
    build(nc, named(given))
    r = _run(nc, [arrays], core_ids=[0])
    return r.results[0]["out_0"]
```
